# Optimizing a Trainium2 kernel written in Bass

```python
import numpy as np
import jax
import jax.numpy as jnp

def _softmax(x, axis=-1):
    return jax.nn.softmax(x, axis=axis)

def _gelu(x):
    return jax.nn.gelu(x, approximate=True)

def _silu(x):
    return jax.nn.silu(x)

def _sigmoid(x):
    return jax.nn.sigmoid(x)

def _layernorm(x, axis=-1, eps=1e-05):
    m = jnp.mean(x, axis=axis, keepdims=True)
    v = jnp.var(x, axis=axis, keepdims=True)
    return (x - m) / jnp.sqrt(v + eps)

def _scatter_add(tgt, idx, src, axis=0):
    return tgt.at[idx].add(src)

def _segment_sum(src, seg, n):
    return jax.ops.segment_sum(src, seg, n)
kernel_name = 'mk_prb_d1_jaxref_r4_c1c510'

def setup_inputs(seed: int=0):
    np.random.seed(seed)
    _w = jnp.asarray

    def _L0_attn_setup():
        import jax, jax.numpy as jnp
        import numpy as np
        EPS = 1e-12

        def _ln(x, g, b):
            m = x.mean(-1, keepdims=True)
            v = x.var(-1, keepdims=True)
            return (x - m) / jnp.sqrt(v + EPS) * g + b

        def _shift(x):
            return jnp.pad(x[:, :-1], ((0, 0), (1, 0), (0, 0)))
        key = jax.random.key(seed)
        ks = jax.random.split(key, 20)
        B, T, H = (4, 512, 512)
        I = 4 * H
        f32 = jnp.float32

        def gamma(k):
            return 1.0 + 0.1 * jax.random.normal(k, (H,), f32)

        def beta(k):
            return 0.1 * jax.random.normal(k, (H,), f32)

        def w(k, i, o):
            return 0.02 * jax.random.normal(k, (i, o), f32)
        return {'x': jax.random.normal(ks[0], (B, T, H), f32), 'ln1_g': gamma(ks[1]), 'ln1_b': beta(ks[2]), 'ln2_g': gamma(ks[3]), 'ln2_b': beta(ks[4]), 'tm_g': gamma(ks[5]), 'tm_b': beta(ks[6]), 'time_decay': -(0.2 + jax.random.uniform(ks[7], (H,), f32)), 'time_first': jax.random.uniform(ks[8], (H,), f32), 'Wk': w(ks[9], H, H), 'Wv': w(ks[10], H, H), 'Wr': w(ks[11], H, H), 'Wo': w(ks[12], H, H), 'bo': jnp.zeros((H,), f32), 'cm_g': gamma(ks[13]), 'cm_b': beta(ks[14]), 'Wck': w(ks[15], H, I), 'Wcv': w(ks[16], I, H), 'Wcr': w(ks[17], H, H)}
    _L0_attn_in = _L0_attn_setup()

    def _L0_ffn_setup():
        import jax, jax.numpy as jnp
        import numpy as np
        B, S, HID = (2, 512, 512)
        NUM_HEADS = 16
        HEAD_DIM = HID // NUM_HEADS
        NUM_EXPERTS = 8
        TOP_K = 2
        INTER = 1024
        EPS = 1e-05

        def _rmsnorm(x, w, eps=EPS):
            return x * jax.lax.rsqrt(jnp.mean(x * x, axis=-1, keepdims=True) + eps) * w

        def _moe(x_flat, Wr, Wg, Wu, Wd):
            T = x_flat.shape[0]
            logits = x_flat @ Wr.T
            top_logits, top_idx = jax.lax.top_k(logits, TOP_K)
            probs = jax.nn.softmax(top_logits, axis=-1)
            cw = jnp.zeros((T, NUM_EXPERTS), x_flat.dtype)
            cw = cw.at[jnp.arange(T)[:, None], top_idx].add(probs)
            hg = jnp.einsum('eih,th->eti', Wg, x_flat)
            hu = jnp.einsum('eih,th->eti', Wu, x_flat)
            y = jnp.einsum('ehi,eti->eth', Wd, jax.nn.silu(hg) * hu)
            return jnp.einsum('eth,te->th', y, cw)
        key = jax.random.key(seed)
        ks = jax.random.split(key, 12)
        sd_h = 1.0 / np.sqrt(HID)
        sd_i = 1.0 / np.sqrt(INTER)
        return {'x': jax.random.normal(ks[0], (B, S, HID), jnp.float32), 'Wq': jax.random.normal(ks[1], (HID, HID), jnp.float32) * sd_h, 'Wk': jax.random.normal(ks[2], (HID, HID), jnp.float32) * sd_h, 'Wv': jax.random.normal(ks[3], (HID, HID), jnp.float32) * sd_h, 'Wo': jax.random.normal(ks[4], (HID, HID), jnp.float32) * sd_h, 'w_ln1': jnp.ones((HID,), jnp.float32), 'w_ln2': jnp.ones((HID,), jnp.float32), 'Wr': jax.random.normal(ks[5], (NUM_EXPERTS, HID), jnp.float32) * sd_h, 'Wg': jax.random.normal(ks[6], (NUM_EXPERTS, INTER, HID), jnp.float32) * sd_h, 'Wu': jax.random.normal(ks[7], (NUM_EXPERTS, INTER, HID), jnp.float32) * sd_h, 'Wd': jax.random.normal(ks[8], (NUM_EXPERTS, HID, INTER), jnp.float32) * sd_i}
    _L0_ffn_in = _L0_ffn_setup()
    _d = {'L0_attn_x': _L0_attn_in['x'], 'L0_attn_ln1_g': _L0_attn_in['ln1_g'], 'L0_attn_ln1_b': _L0_attn_in['ln1_b'], 'L0_attn_ln2_g': _L0_attn_in['ln2_g'], 'L0_attn_ln2_b': _L0_attn_in['ln2_b'], 'L0_attn_tm_g': _L0_attn_in['tm_g'], 'L0_attn_tm_b': _L0_attn_in['tm_b'], 'L0_attn_time_decay': _L0_attn_in['time_decay'], 'L0_attn_time_first': _L0_attn_in['time_first'], 'L0_attn_Wk': _L0_attn_in['Wk'], 'L0_attn_Wv': _L0_attn_in['Wv'], 'L0_attn_Wr': _L0_attn_in['Wr'], 'L0_attn_Wo': _L0_attn_in['Wo'], 'L0_attn_bo': _L0_attn_in['bo'], 'L0_attn_cm_g': _L0_attn_in['cm_g'], 'L0_attn_cm_b': _L0_attn_in['cm_b'], 'L0_attn_Wck': _L0_attn_in['Wck'], 'L0_attn_Wcv': _L0_attn_in['Wcv'], 'L0_attn_Wcr': _L0_attn_in['Wcr'], 'L0_ffn_Wq': _L0_ffn_in['Wq'], 'L0_ffn_Wk': _L0_ffn_in['Wk'], 'L0_ffn_Wv': _L0_ffn_in['Wv'], 'L0_ffn_Wo': _L0_ffn_in['Wo'], 'L0_ffn_w_ln1': _L0_ffn_in['w_ln1'], 'L0_ffn_w_ln2': _L0_ffn_in['w_ln2'], 'L0_ffn_Wr': _L0_ffn_in['Wr'], 'L0_ffn_Wg': _L0_ffn_in['Wg'], 'L0_ffn_Wu': _L0_ffn_in['Wu'], 'L0_ffn_Wd': _L0_ffn_in['Wd']}
    _x0 = _d['L0_attn_x']
    _d['L0_attn_x'] = jax.random.normal(jax.random.fold_in(jax.random.key(seed), 1), (4, 512, 512), dtype=_x0.dtype)
    del _x0
    return _d

def reference(L0_attn_x, L0_attn_ln1_g, L0_attn_ln1_b, L0_attn_ln2_g, L0_attn_ln2_b, L0_attn_tm_g, L0_attn_tm_b, L0_attn_time_decay, L0_attn_time_first, L0_attn_Wk, L0_attn_Wv, L0_attn_Wr, L0_attn_Wo, L0_attn_bo, L0_attn_cm_g, L0_attn_cm_b, L0_attn_Wck, L0_attn_Wcv, L0_attn_Wcr, L0_ffn_Wq, L0_ffn_Wk, L0_ffn_Wv, L0_ffn_Wo, L0_ffn_w_ln1, L0_ffn_w_ln2, L0_ffn_Wr, L0_ffn_Wg, L0_ffn_Wu, L0_ffn_Wd):

    def _L0_attn_ref(x, ln1_g, ln1_b, ln2_g, ln2_b, tm_g, tm_b, time_decay, time_first, Wk, Wv, Wr, Wo, bo, cm_g, cm_b, Wck, Wcv, Wcr):
        import jax, jax.numpy as jnp
        import numpy as np
        EPS = 1e-12

        def _ln(x, g, b):
            m = x.mean(-1, keepdims=True)
            v = x.var(-1, keepdims=True)
            return (x - m) / jnp.sqrt(v + EPS) * g + b

        def _shift(x):
            return jnp.pad(x[:, :-1], ((0, 0), (1, 0), (0, 0)))
        B, T, H = x.shape
        x1 = _ln(x, ln1_g, ln1_b)
        xln = _ln(x1, tm_g, tm_b)
        xs = _shift(xln)
        mix = xln * time_first + xs * (1.0 - time_first)
        v = xln @ Wv
        r = jax.nn.sigmoid(mix @ Wr)
        dec = jnp.exp(time_decay[None, :] * (T - 1 - jnp.arange(T))[:, None])
        vmix = jnp.einsum('bth,th->bh', v, dec)[:, None, :]
        time_out = r * (vmix @ Wo + bo)
        x2 = x + time_out
        xc = _ln(_ln(x2, ln2_g, ln2_b), cm_g, cm_b)
        xcs = _shift(xc)
        kc = jnp.square(jax.nn.relu(xcs @ Wck))
        vc = kc @ Wcv
        rc = jax.nn.sigmoid(xc @ Wcr)
        return x2 + rc * vc

    def _L0_ffn_ref(x, Wq, Wk, Wv, Wo, w_ln1, w_ln2, Wr, Wg, Wu, Wd):
        import jax, jax.numpy as jnp
        import numpy as np
        B, S, HID = (2, 512, 512)
        NUM_HEADS = 16
        HEAD_DIM = HID // NUM_HEADS
        NUM_EXPERTS = 8
        TOP_K = 2
        INTER = 1024
        EPS = 1e-05

        def _rmsnorm(x, w, eps=EPS):
            return x * jax.lax.rsqrt(jnp.mean(x * x, axis=-1, keepdims=True) + eps) * w

        def _moe(x_flat, Wr, Wg, Wu, Wd):
            T = x_flat.shape[0]
            logits = x_flat @ Wr.T
            top_logits, top_idx = jax.lax.top_k(logits, TOP_K)
            probs = jax.nn.softmax(top_logits, axis=-1)
            cw = jnp.zeros((T, NUM_EXPERTS), x_flat.dtype)
            cw = cw.at[jnp.arange(T)[:, None], top_idx].add(probs)
            hg = jnp.einsum('eih,th->eti', Wg, x_flat)
            hu = jnp.einsum('eih,th->eti', Wu, x_flat)
            y = jnp.einsum('ehi,eti->eth', Wd, jax.nn.silu(hg) * hu)
            return jnp.einsum('eth,te->th', y, cw)
        b, s, hid = x.shape
        residual = x
        xn = _rmsnorm(x, w_ln1)
        q = (xn @ Wq.T).reshape(b, s, NUM_HEADS, HEAD_DIM)
        k = (xn @ Wk.T).reshape(b, s, NUM_HEADS, HEAD_DIM)
        v = (xn @ Wv.T).reshape(b, s, NUM_HEADS, HEAD_DIM)
        scale = 1.0 / np.sqrt(HEAD_DIM)
        attn = jnp.einsum('bqhd,bkhd->bhqk', q, k) * scale
        causal = jnp.tril(jnp.ones((s, s), bool))
        attn = jnp.where(causal[None, None], attn, -jnp.inf)
        attn = jax.nn.softmax(attn, axis=-1)
        h = jnp.einsum('bhqk,bkhd->bqhd', attn, v).reshape(b, s, hid)
        x = residual + h @ Wo.T
        residual = x
        xn = _rmsnorm(x, w_ln2)
        moe_out = _moe(xn.reshape(-1, hid), Wr, Wg, Wu, Wd).reshape(b, s, hid)
        return residual + moe_out
    x = L0_attn_x
    xn = _layernorm(x, axis=-1)
    x = x + _L0_attn_ref(xn, L0_attn_ln1_g, L0_attn_ln1_b, L0_attn_ln2_g, L0_attn_ln2_b, L0_attn_tm_g, L0_attn_tm_b, L0_attn_time_decay, L0_attn_time_first, L0_attn_Wk, L0_attn_Wv, L0_attn_Wr, L0_attn_Wo, L0_attn_bo, L0_attn_cm_g, L0_attn_cm_b, L0_attn_Wck, L0_attn_Wcv, L0_attn_Wcr) + _L0_ffn_ref(xn, L0_ffn_Wq, L0_ffn_Wk, L0_ffn_Wv, L0_ffn_Wo, L0_ffn_w_ln1, L0_ffn_w_ln2, L0_ffn_Wr, L0_ffn_Wg, L0_ffn_Wu, L0_ffn_Wd)
    return x

_drawn_inputs = setup_inputs


def setup_inputs(seed=0):
    import zlib

    import numpy as np

    out = dict(_drawn_inputs(seed))
    spreads = {'L0_attn_bo': (0.0, 0.494), 'L0_ffn_w_ln1': (1.0, 0.6), 'L0_ffn_w_ln2': (1.0, 0.6)}
    factors = {'L0_attn_ln1_g': 8.0,
     'L0_attn_ln1_b': 6.775,
     'L0_attn_ln2_g': 8.0,
     'L0_attn_ln2_b': 8.0,
     'L0_attn_tm_g': 8.0,
     'L0_attn_tm_b': 5.715,
     'L0_attn_time_decay': 4.97,
     'L0_attn_time_first': 8.0,
     'L0_attn_Wr': 6.826,
     'L0_attn_cm_g': 8.0,
     'L0_attn_cm_b': 8.0,
     'L0_attn_Wcr': 6.846}
    for name, (base, spread) in spreads.items():
        noise = np.random.default_rng([zlib.crc32(name.encode()), seed]).standard_normal(out[name].shape)
        drawn = base * np.exp(spread * noise) if base else spread * noise
        out[name] = jnp.asarray(drawn.astype(out[name].dtype))
    for name, factor in factors.items():
        out[name] = (out[name] * factor).astype(out[name].dtype)
    return out
```

```python
from contextlib import ExitStack

import concourse.bass as bass
from concourse import mybir

F32 = mybir.dt.float32
F32R = mybir.dt.float32r
BF16 = mybir.dt.bfloat16
ALU = mybir.AluOpType
ACT = mybir.ActivationFunctionType
AX = mybir.AxisListType

P = 128
B, S, H = 4, 512, 512
TT = S // P
HC = H // P
HEADS, HD = 16, 32
E = 8
I_CM = 2048
I_MOE = 1024
CH = 256
CK = CH // P
CHUNKS_CM = I_CM // CH
CHUNKS_MOE = E * I_MOE // CH
NEG = -1.0e30
LN_EPS = 1e-5
LN12_EPS = 1e-12
RMS_EPS = 1e-5
QK_SCALE = HD ** -0.5

V_TMG, V_TMB, V_TF, V_TD, V_CMG, V_CMB, V_W1, V_W2 = range(8)
R_G1, R_B1, R_G2, R_B2 = range(4)


def mm3(pe, out, w_hi, w_lo, x_hi, x_lo, first, last):
    pe.matmul(out, lhsT=w_hi, rhs=x_hi, start=first, stop=False)
    pe.matmul(out, lhsT=w_hi, rhs=x_lo, start=False, stop=False)
    return pe.matmul(out, lhsT=w_lo, rhs=x_hi, start=False, stop=last)


def time_mix_phase(nc, psum, ident, d):
    with ExitStack() as ctx:
        def sb(name, shape, dt=F32):
            return ctx.enter_context(nc.sbuf_tensor("tm_" + name, shape, dt))

        def sem(name):
            return ctx.enter_context(nc.semaphore("tm_" + name))

        w_stage = sb("w_stage", [P, 3, HC * H])
        w_hi = sb("w_hi", [P, 3, HC, H], F32R)
        w_lo = sb("w_lo", [P, 3, HC, H], F32R)
        wo = sb("wo", [P, HC, H])
        bo_row = sb("bo_row", [1, H])
        ones_row = sb("ones_row", [1, P])
        vecs = sb("vecs", [P, 8, HC])
        rows = sb("rows", [P, 4, H])
        one_minus_tf = sb("one_minus_tf", [P, HC])
        steps_left = sb("steps_left", [P, S])
        decay = sb("decay", [P, HC, S])
        x_in = sb("x_in", [P, TT, H])
        xn = sb("xn", [P, TT, H])
        t1 = sb("t1", [P, TT, H])
        t2 = sb("t2", [P, TT, H])
        xT = sb("xT", [P, HC, S + 2])
        x_hi = sb("x_hi", [P, HC, S], F32R)
        x_lo = sb("x_lo", [P, HC, S], F32R)
        mix = sb("mix", [P, HC, S])
        m_hi = sb("m_hi", [P, HC, S], F32R)
        m_lo = sb("m_lo", [P, HC, S], F32R)
        junk = sb("junk", [P, S])
        vmix = sb("vmix", [P, HC])
        vmix_wide = sb("vmix_wide", [P, HC, P])
        stats = sb("stats", [P, TT, 6])
        mv = sb("mv", [P, TT, 2])
        rstd = sb("rstd", [P, TT])
        nmr = sb("nmr", [P, TT])
        var_eps = sb("var_eps", [P, TT])
        spare = sb("spare", [P, 8])
        minus_half = sb("minus_half", [P, TT])

        const_in = sem("const_in")
        w_in = sem("w_in")
        w_hi_ready = sem("w_hi_ready")
        w_lo_ready = sem("w_lo_ready")
        consts_ready = sem("consts_ready")
        steps_ready = sem("steps_ready")
        decay_ready = sem("decay_ready")
        x_loaded = sem("x_loaded")
        stat = sem("stat")
        half_ready = sem("half_ready")
        rstd_ready = sem("rstd_ready")
        xn_ready = sem("xn_ready")
        x1_step = sem("x1_step")
        norm_ready = sem("norm_ready")
        turned = sem("turned")
        xT_ready = sem("xT_ready")
        x_hi_ready = sem("x_hi_ready")
        x_lo_ready = sem("x_lo_ready")
        mix_step = sem("mix_step")
        m_hi_ready = sem("m_hi_ready")
        m_lo_ready = sem("m_lo_ready")
        v_done = sem("v_done")
        vmix_step = sem("vmix_step")
        row_done = sem("row_done")
        r_done = sem("r_done")
        r_ready = sem("r_ready")
        x2_step = sem("x2_step")
        base_ready = sem("base_ready")
        x2n_step = sem("x2n_step")
        rc_done = sem("rc_done")
        rc_ready = sem("rc_ready")
        xn_out = sem("xn_out")
        base_out = sem("base_out")
        xc_out = sem("xc_out")
        rc_out = sem("rc_out")

        tokens = "(j p) h -> p j h"
        block = ctx.enter_context(nc.Block())

        @block.sync
        def _(sp):
            sp.dma_start(vecs[:, :, :], d["vecs"]).then_inc(const_in, 16)
            for n in range(4):
                sp.dma_start(rows[:, n, :], d["rows"][n:n + 1, :].partition_broadcast(P)).then_inc(const_in, 16)
            for n in range(3):
                sp.dma_start(w_stage[:, n, :], d["w_tm"][n]).then_inc(w_in, 16)
            sp.dma_start(wo[:, :, :], d["w_tm"][3].rearrange("p (k n) -> p k n", k=HC)).then_inc(const_in, 16)
            sp.dma_start(bo_row[:, :], d["rows"][4:5, :]).then_inc(const_in, 16)
            with sp.Fori(0, B) as b:
                sp.wait_ge(base_out, b * 16 + 16)
                sp.dma_start(x_in[:, :, :], d["x"][b].rearrange(tokens, p=P)).then_inc(x_loaded, 16)
                sp.wait_ge(xn_ready, b * TT + TT)
                sp.dma_start(d["xn"][b].rearrange(tokens, p=P), xn[:, :, :]).then_inc(xn_out, 16)
                sp.wait_ge(base_ready, b + 1)
                sp.dma_start(d["base"][b].rearrange(tokens, p=P), x_in[:, :, :]).then_inc(base_out, 16)
                sp.wait_ge(m_hi_ready, b * 2 * HC + 2 * HC)
                sp.dma_start(d["xc_hi"][b], m_hi[:, :, :].bitcast(F32)).then_inc(xc_out, 16)
                sp.wait_ge(m_lo_ready, b * 2 * HC + 2 * HC)
                sp.dma_start(d["xc_lo"][b], m_lo[:, :, :].bitcast(F32)).then_inc(xc_out, 16)
            sp.wait_ge(xn_out, 16 * (B + 1))
            sp.wait_ge(base_out, 16 * (B + 1))
            sp.wait_ge(xc_out, 32 * (B + 1))
            sp.wait_ge(rc_out, 16 * (B + 1))

        @block.gpsimd
        def _(pool):
            pool.iota(steps_left[:, :], [[-1, S]], base=S - 1, channel_multiplier=0,
                      allow_small_or_imprecise_dtypes=True).then_inc(steps_ready, 1)
            for n in range(3):
                pool.wait_ge(w_hi_ready, n + 1)
                pool.tensor_tensor(w_lo[:, n, :, :].rearrange("p k n -> p (k n)"), w_stage[:, n, :],
                                   w_hi[:, n, :, :].rearrange("p k n -> p (k n)").bitcast(F32),
                                   ALU.subtract).then_inc(w_lo_ready, 1)
            pool.memset(minus_half[:, :], -0.5).then_inc(half_ready, 1)
            pool.wait_ge(half_ready, 1)

            def inverse_root(turn):
                pool.wait_ge(stat, turn * 10 + 2 * TT + 1)
                pool.tensor_tensor(rstd[:, :], var_eps[:, :], minus_half[:, :], ALU.pow).then_inc(rstd_ready, 1)

            with pool.Fori(0, B) as b:
                for n in range(3):
                    inverse_root(b * 5 + n)
                for c in range(HC):
                    pool.wait_ge(x_hi_ready, b * HC + c + 1)
                    pool.tensor_tensor(x_lo[:, c, :], xT[:, c, 1:S + 1], x_hi[:, c, :].bitcast(F32),
                                       ALU.subtract).then_inc(x_lo_ready, 1)
                for c in range(HC):
                    pool.wait_ge(m_hi_ready, b * 2 * HC + c + 1)
                    pool.tensor_tensor(m_lo[:, c, :], mix[:, c, :], m_hi[:, c, :].bitcast(F32),
                                       ALU.subtract).then_inc(m_lo_ready, 1)
                inverse_root(b * 5 + 3)
                inverse_root(b * 5 + 4)
                pool.wait_ge(x2_step, b * 2 * TT + 2 * TT)
                pool.tensor_tensor(x_in[:, :, :], x_in[:, :, :], t1[:, :, :], ALU.add).then_inc(base_ready, 1)
                for c in range(HC):
                    pool.wait_ge(m_hi_ready, b * 2 * HC + HC + c + 1)
                    pool.tensor_tensor(m_lo[:, c, :], xT[:, c, 1:S + 1], m_hi[:, c, :].bitcast(F32),
                                       ALU.subtract).then_inc(m_lo_ready, 1)

        @block.scalar
        def _(act):
            act.wait_ge(const_in, 16 * 7)
            act.wait_ge(steps_ready, 1)
            for c in range(HC):
                act.activation(decay[:, c, :], steps_left[:, :], ACT.Exp,
                               scale=vecs[:, V_TD, c:c + 1]).then_inc(decay_ready, 1)
            for n in range(3):
                act.wait_ge(w_in, 16 * (n + 1))
                act.activation(w_hi[:, n, :, :].rearrange("p k n -> p (k n)"), w_stage[:, n, :],
                               ACT.Copy).then_inc(w_hi_ready, 1)
            with act.Fori(0, B) as b:
                act.wait_ge(stat, b * 50 + 10)
                for j in range(TT):
                    act.activation(xn[:, j, :], x_in[:, j, :], ACT.Identity, bias=nmr[:, j:j + 1],
                                   scale=rstd[:, j:j + 1]).then_inc(xn_ready, 1)
                act.wait_ge(stat, b * 50 + 30)
                for j in range(TT):
                    act.activation(t2[:, j, :], t1[:, j, :], ACT.Identity, bias=nmr[:, j:j + 1],
                                   scale=rstd[:, j:j + 1]).then_inc(norm_ready, 1)
                for c in range(HC):
                    act.wait_ge(turned, b * 2 * HC + c + 1)
                    act.activation(xT[:, c, 1:S + 1], psum[c][:, :], ACT.Identity,
                                   bias=vecs[:, V_TMB, c:c + 1], scale=vecs[:, V_TMG, c:c + 1]).then_inc(xT_ready, 1)
                    act.activation(x_hi[:, c, :], psum[c][:, :], ACT.Identity,
                                   bias=vecs[:, V_TMB, c:c + 1],
                                   scale=vecs[:, V_TMG, c:c + 1]).then_inc(x_hi_ready, 1)
                for c in range(HC):
                    act.wait_ge(mix_step, b * 2 * HC + 2 * c + 2)
                    act.activation(m_hi[:, c, :], mix[:, c, :], ACT.Copy).then_inc(m_hi_ready, 1)
                for j in range(TT):
                    act.wait_ge(r_done, b * TT + j + 1)
                    act.activation(t1[:, j, :], psum[j][:, :], ACT.Sigmoid).then_inc(r_ready, 1)
                act.wait_ge(stat, b * 50 + 50)
                for j in range(TT):
                    act.activation(t2[:, j, :], t2[:, j, :], ACT.Identity, bias=nmr[:, j:j + 1],
                                   scale=rstd[:, j:j + 1]).then_inc(norm_ready, 1)
                for c in range(HC):
                    act.wait_ge(turned, b * 2 * HC + HC + c + 1)
                    act.activation(xT[:, c, 1:S + 1], psum[HC + c][:, :], ACT.Identity,
                                   bias=vecs[:, V_CMB, c:c + 1], scale=vecs[:, V_CMG, c:c + 1]).then_inc(xT_ready, 1)
                    act.activation(m_hi[:, c, :], psum[HC + c][:, :], ACT.Identity,
                                   bias=vecs[:, V_CMB, c:c + 1],
                                   scale=vecs[:, V_CMG, c:c + 1]).then_inc(m_hi_ready, 1)
                for j in range(TT):
                    act.wait_ge(rc_done, b * TT + j + 1)
                    act.activation(t2[:, j, :], psum[j][:, :], ACT.Sigmoid).then_inc(rc_ready, 1)
                act.wait_ge(rc_ready, b * TT + TT)
                act.dma_start(d["rc"][b].rearrange(tokens, p=P), t2[:, :, :]).then_inc(rc_out, 16)

        @block.vector
        def _(dve):
            dve.memset(ones_row[:, :], 1.0).then_inc(consts_ready, 1)
            for c in range(HC):
                dve.memset(xT[:, c, 0:1], 0.0).then_inc(consts_ready, 1)
            dve.wait_ge(const_in, 16 * 7)
            dve.tensor_scalar(one_minus_tf[:, :], vecs[:, V_TF, :], -1.0, 1.0, ALU.mult,
                              ALU.add).then_inc(consts_ready, 1)
            for i, (out_sem, n) in enumerate(((xn_out, 16), (base_out, 16), (xc_out, 32), (rc_out, 16))):
                dve.memset(spare[:, i:i + 1], 0.0).then_inc(out_sem, n)
            dve.wait_ge(consts_ready, HC + 2)

            def moments(src, turn, eps):
                base = turn * 10
                for j in range(TT):
                    dve.bn_stats(stats[:, j, :], src[:, j, :]).then_inc(stat, 1)
                dve.wait_ge(stat, base + TT)
                dve.memset(spare[:, 4:5], 0.0)
                for j in range(TT):
                    dve.bn_aggr(mv[:, j, :], stats[:, j, :]).then_inc(stat, 1)
                dve.wait_ge(stat, base + 2 * TT)
                dve.tensor_scalar(var_eps[:, :], mv[:, :, 1], eps, None, ALU.add).then_inc(stat, 1)
                dve.wait_ge(rstd_ready, turn + 1)
                dve.scalar_tensor_tensor(nmr[:, :], mv[:, :, 0], -1.0, rstd[:, :], ALU.mult,
                                         ALU.mult).then_inc(stat, 1)
                dve.wait_ge(stat, base + 2 * TT + 2)

            def affine_norm(dst, src, row_g, row_b, step, base):
                for j in range(TT):
                    dve.scalar_tensor_tensor(dst[:, j, :], src[:, j, :], mv[:, j, 0:1], rows[:, row_g, :],
                                             ALU.subtract, ALU.mult).then_inc(step, 1)
                for j in range(TT):
                    dve.wait_ge(step, base + j + 1)
                    dve.scalar_tensor_tensor(dst[:, j, :], dst[:, j, :], rstd[:, j:j + 1], rows[:, row_b, :],
                                             ALU.mult, ALU.add).then_inc(step, 1)
                dve.wait_ge(step, base + 2 * TT)

            with dve.Fori(0, B) as b:
                dve.wait_ge(x_loaded, b * 16 + 16)
                dve.wait_ge(xn_out, b * 16 + 16)
                dve.wait_ge(rc_out, b * 16 + 16)
                dve.wait_ge(xc_out, b * 32 + 32)
                moments(x_in, b * 5, LN_EPS)
                dve.wait_ge(xn_ready, b * TT + TT)
                moments(xn, b * 5 + 1, LN12_EPS)
                affine_norm(t1, xn, R_G1, R_B1, x1_step, b * 2 * TT)
                moments(t1, b * 5 + 2, LN12_EPS)
                for c in range(HC):
                    dve.wait_ge(xT_ready, b * 2 * HC + c + 1)
                    dve.tensor_scalar(mix[:, c, :], xT[:, c, 1:S + 1], vecs[:, V_TF, c:c + 1], None,
                                      ALU.mult).then_inc(mix_step, 1)
                    dve.wait_ge(mix_step, b * 2 * HC + 2 * c + 1)
                    dve.scalar_tensor_tensor(mix[:, c, :], xT[:, c, 0:S], one_minus_tf[:, c:c + 1], mix[:, c, :],
                                             ALU.mult, ALU.add).then_inc(mix_step, 1)
                dve.wait_ge(decay_ready, HC)
                for m in range(HC):
                    dve.wait_ge(v_done, b * HC + m + 1)
                    if m:
                        dve.wait_ge(vmix_step, b * (HC + 1) + m)
                    dve.tensor_tensor_reduce(junk[:, :], psum[HC + m][:, :], decay[:, m, :], 1.0, 0.0, ALU.mult,
                                             ALU.add, vmix[:, m:m + 1]).then_inc(vmix_step, 1)
                dve.wait_ge(vmix_step, b * (HC + 1) + HC)
                dve.tensor_copy(vmix_wide[:, :, :],
                                vmix[:, :].unsqueeze(2).to_broadcast([P, HC, P])).then_inc(vmix_step, 1)
                dve.wait_ge(row_done, b + 1)
                for j in range(TT):
                    dve.wait_ge(r_ready, b * TT + j + 1)
                    dve.tensor_tensor(t1[:, j, :], t1[:, j, :], psum[HC][:, :], ALU.mult).then_inc(x2_step, 1)
                for j in range(TT):
                    dve.wait_ge(x2_step, b * 2 * TT + j + 1)
                    dve.tensor_tensor(t1[:, j, :], t1[:, j, :], xn[:, j, :], ALU.add).then_inc(x2_step, 1)
                dve.wait_ge(x2_step, b * 2 * TT + 2 * TT)
                moments(t1, b * 5 + 3, LN12_EPS)
                affine_norm(t2, t1, R_G2, R_B2, x2n_step, b * 2 * TT)
                moments(t2, b * 5 + 4, LN12_EPS)
                dve.wait_ge(norm_ready, b * 2 * TT + 2 * TT)
                dve.wait_ge(base_ready, b + 1)

        @block.tensor
        def _(pe):
            def turn(bank, base):
                for c in range(HC):
                    for j in range(TT):
                        t = pe.transpose(psum[bank + c][:, j * P:(j + 1) * P], t2[:, j, c * P:(c + 1) * P], ident)
                    t.then_inc(turned, 1)

            pe.wait_ge(w_hi_ready, 3)
            pe.wait_ge(w_lo_ready, 3)
            pe.wait_ge(const_in, 16 * 7)
            pe.wait_ge(consts_ready, 1)
            with pe.Fori(0, B) as b:
                pe.wait_ge(rc_out, b * 16 + 16)
                pe.wait_ge(norm_ready, b * 2 * TT + TT)
                turn(0, b)
                pe.wait_ge(xc_out, b * 32 + 32)
                for m in range(HC):
                    for k in range(HC):
                        if m == 0:
                            pe.wait_ge(x_hi_ready, b * HC + k + 1)
                            pe.wait_ge(x_lo_ready, b * HC + k + 1)
                        cols = slice(m * P, (m + 1) * P)
                        last = mm3(pe, psum[HC + m][:, :], w_hi[:, 0, k, cols], w_lo[:, 0, k, cols],
                                   x_hi[:, k, :], x_lo[:, k, :], k == 0, k == HC - 1)
                    last.then_inc(v_done, 1)
                for j in range(TT):
                    for k in range(HC):
                        if j == 0:
                            pe.wait_ge(m_lo_ready, b * 2 * HC + k + 1)
                        cols = slice(j * P, (j + 1) * P)
                        last = mm3(pe, psum[j][:, :], m_hi[:, k, cols], m_lo[:, k, cols],
                                   w_hi[:, 1, k, :], w_lo[:, 1, k, :], k == 0, k == HC - 1)
                    last.then_inc(r_done, 1)
                pe.wait_ge(vmix_step, b * (HC + 1) + HC + 1)
                for m in range(HC):
                    pe.matmul(psum[HC][:, :], lhsT=vmix_wide[:, m, :], rhs=wo[:, m, :], start=(m == 0), stop=False)
                pe.matmul(psum[HC][:, :], lhsT=ones_row[:, :], rhs=bo_row[:, :], start=False,
                          stop=True).then_inc(row_done, 1)
                pe.wait_ge(x2_step, b * 2 * TT + TT)
                pe.wait_ge(norm_ready, b * 2 * TT + 2 * TT)
                turn(HC, b)
                pe.wait_ge(r_ready, b * TT + TT)
                for j in range(TT):
                    for k in range(HC):
                        if j == 0:
                            pe.wait_ge(m_lo_ready, b * 2 * HC + HC + k + 1)
                        cols = slice(j * P, (j + 1) * P)
                        last = mm3(pe, psum[j][:, :], m_hi[:, k, cols], m_lo[:, k, cols],
                                   w_hi[:, 2, k, :], w_lo[:, 2, k, :], k == 0, k == HC - 1)
                    last.then_inc(rc_done, 1)


def mlp_phase(nc, psum, d, gated):
    n_chunks = CHUNKS_MOE if gated else CHUNKS_CM
    name = "moe_" if gated else "cm_"
    n_up = 2 if gated else 1
    WG, WU = 0, HC * CH
    WD = n_up * HC * CH
    WW = WD + CK * H
    STEPS = 2 * B
    TURNS = n_chunks // 2
    w_src = d["w_moe"] if gated else d["w_cm"]
    src_hi, src_lo = (d["x2_hi"], d["x2_lo"]) if gated else (d["xc_hi"], d["xc_lo"])
    dst = d["out"] if gated else d["vc"]
    SHIFT = 0 if gated else 1
    tokens = "(j p) h -> p j h"

    with ExitStack() as ctx:
        def sb(nm, shape, dt=F32):
            return ctx.enter_context(nc.sbuf_tensor(name + nm, shape, dt))

        def sem(nm):
            return ctx.enter_context(nc.semaphore(name + nm))

        x_hi = sb("x_hi", [P, HC, B, S + 2], F32R)
        x_lo = sb("x_lo", [P, HC, B, S + 2], F32R)
        acc = sb("acc", [P, B * TT, H])
        stage = sb("stage", [P, 2, WW])
        w_hi = sb("w_hi", [P, 2, WW], F32R)
        w_lo = sb("w_lo", [P, 2, WW], F32R)
        gate = sb("gate", [P, CK, S])
        spare = sb("spare", [P, 8])
        a = sb("a", [P, CK, S])
        a_hi = sb("a_hi", [P, 2, CK, S], F32R)
        a_lo = sb("a_lo", [P, 2, CK, S], F32R)
        if gated:
            cw_in = sb("cw_in", [P, B, TT * E])
            cw_all = sb("cw_all", [P, E, 2, B * TT])
            cw = sb("cw", [P, B * TT])

        x_loaded = [sem(f"x_loaded{b}") for b in range(B)]
        stage_in = [sem(f"stage_in{u}") for u in range(2)]
        w_hi_ready = [sem(f"w_hi_ready{u}") for u in range(2)]
        w_lo_ready = [sem(f"w_lo_ready{u}") for u in range(2)]
        acc_in = sem("acc_in")
        cw_loaded = sem("cw_loaded")
        cw_ready = sem("cw_ready")
        zeroed = sem("zeroed")
        gu_done = sem("gu_done")
        gate_free = sem("gate_free")
        a_full = sem("a_full")
        a_hi_ready = sem("a_hi_ready")
        a_lo_ready = sem("a_lo_ready")
        y_done = sem("y_done")
        y_free = sem("y_free")
        out_done = sem("out_done")
        g_bank = psum[0:CK]
        u_bank = psum[CK:2 * CK]
        y_bank = psum[2 * CK:2 * CK + TT]

        block = ctx.enter_context(nc.Block())

        @block.sync
        def _(sp):
            def load(u, n):
                sp.dma_start(stage[:, u, :], w_src[n]).then_inc(stage_in[u], 16)

            load(0, 0)
            for b in range(B):
                sp.dma_start(x_hi[:, :, b, 2:S + 2].bitcast(F32), src_hi[b]).then_inc(x_loaded[b], 16)
                sp.dma_start(x_lo[:, :, b, 2:S + 2].bitcast(F32), src_lo[b]).then_inc(x_loaded[b], 16)
                if b == 0:
                    load(1, 1)
            if gated:
                sp.dma_start(cw_in[:, :, :], d["cw"].rearrange("b p t -> p b t")).then_inc(cw_loaded, 16)
                for b in range(B):
                    sp.dma_start(acc[:, b * TT:(b + 1) * TT, :],
                                 d["pre"][b].rearrange(tokens, p=P)).then_inc(acc_in, 16)
            with sp.Fori(0, TURNS - 1) as it:
                for u in range(2):
                    sp.wait_ge(w_lo_ready[u], it + 1)
                    load(u, it * 2 + u + 2)
            for b in range(B):
                sp.wait_ge(y_free, 4 * TT + TURNS * STEPS * TT - (B - 1 - b) * TT)
                sp.dma_start(dst[b].rearrange(tokens, p=P), acc[:, b * TT:(b + 1) * TT, :]).then_inc(out_done, 16)
            sp.wait_ge(out_done, 16 * B)

        @block.gpsimd
        def _(pool):
            def split(u, n):
                pool.wait_ge(w_hi_ready[u], n + 1)
                pool.tensor_tensor(w_lo[:, u, :], stage[:, u, :], w_hi[:, u, :].bitcast(F32),
                                   ALU.subtract).then_inc(w_lo_ready[u], 1)

            def low(g, s):
                for m in range(CK):
                    pool.wait_ge(a_hi_ready, g * CK + m + 1)
                    pool.tensor_tensor(a_lo[:, s % 2, m, :], a[:, m, :], a_hi[:, s % 2, m, :].bitcast(F32),
                                       ALU.subtract).then_inc(a_lo_ready, 1)

            def turn(it, last):
                for s in range(STEPS):
                    if s == 0:
                        split(1, it)
                    if s == B and not last:
                        split(0, it + 1)
                    if not (last and s == STEPS - 1):
                        low(it * STEPS + s + 1, s + 1)

            pool.memset(spare[:, 4:5], 0.0).then_inc(a_lo_ready, CK)
            split(0, 0)
            low(0, 0)
            with pool.Fori(0, TURNS - 1) as it:
                turn(it, False)
            turn(TURNS - 1, True)

        @block.scalar
        def _(act):
            def split(u, n, g):
                act.wait_ge(stage_in[u], n * 16 + 16)
                if g is not None:
                    act.wait_ge(y_done, g * TT + 2 * TT)
                act.activation(w_hi[:, u, :], stage[:, u, :], ACT.Copy).then_inc(w_hi_ready[u], 1)

            def up(g, s):
                for m in range(CK):
                    act.wait_ge(gu_done, g * CK + m + 1)
                    act.wait_ge(a_full, g * CK + m + 1)
                    act.activation(gate[:, m, :], g_bank[m][:, :],
                                   ACT.Silu if gated else ACT.Relu).then_inc(gate_free, 1)
                for m in range(CK):
                    act.wait_ge(a_full, g * CK + CK + m + 1)
                    if m == 0:
                        act.wait_ge(y_done, g * TT + TT)
                    act.activation(a_hi[:, s % 2, m, :], a[:, m, :], ACT.Copy).then_inc(a_hi_ready, 1)

            def turn(it, last):
                for s in range(STEPS):
                    if s == 0:
                        split(1, it, it * STEPS)
                    if s == B and not last:
                        split(0, it + 1, it * STEPS + B)
                    if not (last and s == STEPS - 1):
                        up(it * STEPS + s + 1, s + 1)

            split(0, 0, None)
            up(0, 0)
            with act.Fori(0, TURNS - 1) as it:
                turn(it, False)
            turn(TURNS - 1, True)

        @block.vector
        def _(dve):
            if not gated:
                dve.memset(x_hi[:, :, :, 0:2].bitcast(F32), 0.0).then_inc(zeroed, 1)
                dve.memset(x_lo[:, :, :, 0:2].bitcast(F32), 0.0).then_inc(zeroed, 1)
                dve.memset(acc[:, :, :], 0.0).then_inc(zeroed, 1)
                dve.wait_ge(zeroed, 3)
            dve.memset(spare[:, 0:1], 0.0).then_inc(gate_free, CK)
            dve.memset(spare[:, 1:2], 0.0).then_inc(a_full, CK)
            dve.memset(spare[:, 2:3], 0.0).then_inc(y_done, 2 * TT)
            dve.memset(spare[:, 3:4], 0.0).then_inc(y_free, 4 * TT)
            if gated:
                dve.wait_ge(cw_loaded, 16)
                for n in range(2):
                    for b in range(B):
                        dve.tensor_copy(cw_all[:, :, n, b * TT:(b + 1) * TT],
                                        cw_in[:, b, :].rearrange("p (j e) -> p e j", e=E)).then_inc(cw_ready, 1)
                dve.wait_ge(acc_in, 16 * B)

            def product(g):
                for m in range(CK):
                    dve.wait_ge(gate_free, g * CK + m + CK + 1)
                    dve.wait_ge(a_lo_ready, g * CK + m + 1)
                    if gated:
                        i = dve.tensor_tensor(a[:, m, :], gate[:, m, :], u_bank[m][:, :], ALU.mult)
                    else:
                        i = dve.scalar_tensor_tensor(a[:, m, :], g_bank[m][:, :], 0.0, gate[:, m, :],
                                                     ALU.max, ALU.mult)
                    i.then_inc(a_full, 1)

            def accumulate(g, s):
                for j in range(TT):
                    t = (s % B) * TT + j
                    dve.wait_ge(y_done, g * TT + 2 * TT + j + 1)
                    dve.wait_ge(y_free, g * TT + j + 1)
                    if gated:
                        i = dve.scalar_tensor_tensor(acc[:, t, :], y_bank[j][:, :], cw[:, t:t + 1], acc[:, t, :],
                                                     ALU.mult, ALU.add)
                    else:
                        i = dve.tensor_tensor(acc[:, t, :], y_bank[j][:, :], acc[:, t, :], ALU.add)
                    i.then_inc(y_free, 1)

            def turn(it, last):
                if gated:
                    dve.wait_ge(cw_ready, it + 2 * B)
                    dve.wait_ge(y_free, it * STEPS * TT + 4 * TT)
                    dve.tensor_copy(cw[:, :], cw_by_turn[:, it, :]).then_inc(cw_ready, 1)
                    dve.wait_ge(cw_ready, it + 2 * B + 1)
                for s in range(STEPS):
                    if not (last and s == STEPS - 1):
                        product(it * STEPS + s + 1)
                    accumulate(it * STEPS + s, s)

            if gated:
                cw_by_turn = cw_all[:, :, :, :].rearrange("p e n t -> p (e n) t")
            product(0)
            with dve.Fori(0, TURNS - 1) as it:
                turn(it, False)
            turn(TURNS - 1, True)

        @block.tensor
        def _(pe):
            def up(g, s, n):
                u, b = (s // B) % 2, s % B
                if b == 0:
                    pe.wait_ge(w_lo_ready[u], n + 1)
                pe.wait_ge(x_loaded[b], 32)
                lo = 2 - SHIFT
                for m in range(CK):
                    if gated:
                        pe.wait_ge(gate_free, g * CK + m + 1)
                    pe.wait_ge(a_full, g * CK + m + 1)
                    for w0, bank in ((WG, g_bank), (WU, u_bank))[:n_up]:
                        for k in range(HC):
                            cols = slice(w0 + k * CH + m * P, w0 + k * CH + (m + 1) * P)
                            last = mm3(pe, bank[m][:, :], w_hi[:, u, cols], w_lo[:, u, cols],
                                       x_hi[:, k, b, lo:lo + S], x_lo[:, k, b, lo:lo + S], k == 0, k == HC - 1)
                    last.then_inc(gu_done, 1)

            def down(g, s):
                u = s // B
                pe.wait_ge(a_lo_ready, g * CK + 2 * CK)
                for j in range(TT):
                    pe.wait_ge(y_free, g * TT + 3 * TT + j + 1)
                    for m in range(CK):
                        cols = slice(j * P, (j + 1) * P)
                        rows = slice(WD + m * H, WD + (m + 1) * H)
                        last = mm3(pe, y_bank[j][:, :], a_hi[:, s % 2, m, cols], a_lo[:, s % 2, m, cols],
                                   w_hi[:, u, rows], w_lo[:, u, rows], m == 0, m == CK - 1)
                    last.then_inc(y_done, 1)

            def turn(it, last):
                for s in range(STEPS):
                    if not (last and s == STEPS - 1):
                        up(it * STEPS + s + 1, s + 1, it + (s + 1) // STEPS)
                    down(it * STEPS + s, s)

            if not gated:
                pe.wait_ge(zeroed, 3)
            up(0, 0, 0)
            with pe.Fori(0, TURNS - 1) as it:
                turn(it, False)
            turn(TURNS - 1, True)


def attention_phase(nc, psum, ident, ident_bf, causal, d):
    N_W = 4
    S_AT = {3: (0, 0), 2: (1, 0), 0: (1, 3 * P), 1: (2, 0)}
    PT_AT = {0: (0, 0), 1: (1, 0), 3: (1, 3 * P), 2: (2, 0)}
    PT_COLS = 512 + 512 + 256

    with ExitStack() as ctx:
        def sb(name, shape, dt=F32):
            return ctx.enter_context(nc.sbuf_tensor("at_" + name, shape, dt))

        def sem(name):
            return ctx.enter_context(nc.semaphore("at_" + name))

        w_stage = sb("w_stage", [P, 2, HC * H])
        w_hi = sb("w_hi", [P, N_W, HC, H], F32R)
        w_lo = sb("w_lo", [P, N_W, HC, H], F32R)
        wr = sb("wr", [P, HC, E])
        vecs = sb("vecs", [P, 8, HC])
        prefer = sb("prefer", [P, E])
        xn = sb("xn", [P, TT, H])
        t = sb("t", [P, TT, H])
        xT = sb("xT", [P, HC, S])
        x_hi = sb("x_hi", [P, HC, S], F32R)
        x_lo = sb("x_lo", [P, HC, S], F32R)
        qT = sb("qT", [P, HC, S])
        kT = sb("kT", [P, HC, S])
        v = sb("v", [P, TT, H])
        probs = sb("probs", [P, 2, TT, S])
        pT = sb("pT", [P, 2, PT_COLS])
        xp = sb("xp", [P, TT, H])
        base = sb("base", [P, TT, H])
        rc = sb("rc", [P, TT, H])
        vc = sb("vc", [P, TT, H])
        sq = sb("sq", [P, TT])
        mean_sq = sb("mean_sq", [P, TT])
        spare = sb("spare", [P, 8])
        minus_half = sb("minus_half", [P, TT])
        rstd = sb("rstd", [P, TT])
        row_max = sb("row_max", [P, HEADS, TT])
        bias = sb("bias", [P, HEADS, TT])
        row_sum = sb("row_sum", [P, HEADS, TT])
        row_rec = sb("row_rec", [P, HEADS, TT])
        logits = sb("logits", [P, TT, E])
        left = sb("left", [P, TT, E])
        hit = sb("hit", [P, TT, E])
        first = sb("first", [P, TT, E])
        second = sb("second", [P, TT, E])
        top = sb("top", [P, 2, TT])
        pick = sb("pick", [P, TT])
        gap = sb("gap", [P, TT])
        odds = sb("odds", [P, TT])
        p1 = sb("p1", [P, TT])
        p2 = sb("p2", [P, TT])
        cw = sb("cw", [P, TT, E])

        const_in = sem("const_in")
        w_in = [sem(f"w_in{n}") for n in range(N_W)]
        w_hi_ready = sem("w_hi_ready")
        w_lo_ready = sem("w_lo_ready")
        prefer_ready = sem("prefer_ready")
        xn_loaded = sem("xn_loaded")
        res_loaded = sem("res_loaded")
        sq_ready = sem("sq_ready")
        mean_sq_ready = sem("mean_sq_ready")
        half_ready = sem("half_ready")
        rstd_ready = sem("rstd_ready")
        norm_ready = sem("norm_ready")
        turned = sem("turned")
        xT_ready = sem("xT_ready")
        x_hi_ready = sem("x_hi_ready")
        x_lo_ready = sem("x_lo_ready")
        q_done = sem("q_done")
        k_done = sem("k_done")
        v_done = sem("v_done")
        q_ready = sem("q_ready")
        k_ready = sem("k_ready")
        v_ready = sem("v_ready")
        scores_done = sem("scores_done")
        max_step = sem("max_step")
        bias_ready = sem("bias_ready")
        exp_ready = sem("exp_ready")
        probs_turned = sem("probs_turned")
        pT_by_act = sem("pT_by_act")
        pT_by_dve = sem("pT_by_dve")
        heads_done = sem("heads_done")
        rec_ready = sem("rec_ready")
        o_ready = sem("o_ready")
        proj_done = sem("proj_done")
        xp_ready = sem("xp_ready")
        logits_done = sem("logits_done")
        route = sem("route")
        route2 = sem("route2")
        gap_ready = sem("gap_ready")
        odds_ready = sem("odds_ready")
        cw_ready = sem("cw_ready")
        pre_step = sem("pre_step")
        x2_out = sem("x2_out")
        cw_out = sem("cw_out")
        pre_out = sem("pre_out")

        tokens = "(j p) h -> p j h"
        block = ctx.enter_context(nc.Block())

        @block.sync
        def _(sp):
            sp.dma_start(vecs[:, :, :], d["vecs"]).then_inc(const_in, 16)
            sp.dma_start(wr[:, :, :], d["w_r"]).then_inc(const_in, 16)
            for n in range(N_W):
                if n >= 2:
                    sp.wait_ge(w_lo_ready, n - 1)
                sp.dma_start(w_stage[:, n % 2, :], d["w_at"][n]).then_inc(w_in[n], 16)
            with sp.Fori(0, B) as b:
                sp.dma_start(xn[:, :, :], d["xn"][b].rearrange(tokens, p=P)).then_inc(xn_loaded, 16)
                sp.wait_ge(pre_out, b * 16 + 16)
                for dst, src in ((base, "base"), (rc, "rc"), (vc, "vc")):
                    sp.dma_start(dst[:, :, :], d[src][b].rearrange(tokens, p=P)).then_inc(res_loaded, 16)
                sp.wait_ge(x_hi_ready, b * 3 * HC + 3 * HC)
                sp.dma_start(d["x2_hi"][b], x_hi[:, :, :].bitcast(F32)).then_inc(x2_out, 16)
                sp.wait_ge(x_lo_ready, b * 3 * HC + 3 * HC)
                sp.dma_start(d["x2_lo"][b], x_lo[:, :, :].bitcast(F32)).then_inc(x2_out, 16)
                sp.wait_ge(pre_step, b * 3 + 3)
                sp.dma_start(d["pre"][b].rearrange(tokens, p=P), rc[:, :, :]).then_inc(pre_out, 16)
                sp.wait_ge(cw_ready, b * 2 + 2)
                sp.dma_start(d["cw"][b], cw[:, :, :].rearrange("p j e -> p (j e)")).then_inc(cw_out, 16)
            sp.wait_ge(x2_out, 32 * (B + 1))
            sp.wait_ge(pre_out, 16 * (B + 1))
            sp.wait_ge(cw_out, 16 * (B + 1))

        @block.gpsimd
        def _(pool):
            pool.iota(prefer[:, :], [[-1, E]], base=E, channel_multiplier=0,
                      allow_small_or_imprecise_dtypes=True).then_inc(prefer_ready, 1)
            pool.memset(spare[:, 0:1], 0.0).then_inc(x2_out, 32)
            pool.memset(spare[:, 1:2], 0.0).then_inc(pre_out, 16)
            pool.memset(spare[:, 2:3], 0.0).then_inc(cw_out, 16)
            for n in range(N_W):
                pool.wait_ge(w_hi_ready, n + 1)
                pool.tensor_tensor(w_lo[:, n, :, :].rearrange("p k n -> p (k n)"), w_stage[:, n % 2, :],
                                   w_hi[:, n, :, :].rearrange("p k n -> p (k n)").bitcast(F32),
                                   ALU.subtract).then_inc(w_lo_ready, 1)

            def low(b, turn):
                for c in range(HC):
                    pool.wait_ge(x_hi_ready, b * 3 * HC + turn * HC + c + 1)
                    pool.tensor_tensor(x_lo[:, c, :], xT[:, c, :], x_hi[:, c, :].bitcast(F32),
                                       ALU.subtract).then_inc(x_lo_ready, 1)

            pool.memset(minus_half[:, :], -0.5).then_inc(half_ready, 1)
            pool.wait_ge(half_ready, 1)

            def inverse_root(turn):
                pool.wait_ge(mean_sq_ready, turn + 1)
                pool.tensor_tensor(rstd[:, :], mean_sq[:, :], minus_half[:, :], ALU.pow).then_inc(rstd_ready, 1)

            with pool.Fori(0, B) as b:
                inverse_root(b * 2)
                low(b, 0)
                pool.wait_ge(res_loaded, b * 48 + 48)
                pool.tensor_tensor(rc[:, :, :], rc[:, :, :], vc[:, :, :], ALU.mult).then_inc(pre_step, 1)
                pool.wait_ge(pre_step, b * 3 + 1)
                pool.tensor_tensor(rc[:, :, :], rc[:, :, :], base[:, :, :], ALU.add).then_inc(pre_step, 1)
                low(b, 1)
                inverse_root(b * 2 + 1)
                low(b, 2)
                pool.wait_ge(xp_ready, b * TT + TT)
                pool.wait_ge(pre_step, b * 3 + 2)
                pool.tensor_tensor(rc[:, :, :], rc[:, :, :], xp[:, :, :], ALU.add).then_inc(pre_step, 1)

        @block.scalar
        def _(act):
            for n in range(N_W):
                act.wait_ge(w_in[n], 16)
                act.activation(w_hi[:, n, :, :].rearrange("p k n -> p (k n)"), w_stage[:, n % 2, :],
                               ACT.Copy).then_inc(w_hi_ready, 1)
            act.wait_ge(const_in, 32)

            def squares(src, b, turn):
                for j in range(TT):
                    if turn:
                        act.wait_ge(xp_ready, b * TT + j + 1)
                    act.activation(t[:, j, :], src[:, j, :], ACT.Square,
                                   accum_out=sq[:, j:j + 1]).then_inc(sq_ready, 1)

            def scaled(src, b, turn):
                act.wait_ge(rstd_ready, b * 2 + turn + 1)
                for j in range(TT):
                    act.activation(t[:, j, :], src[:, j, :], ACT.Copy,
                                   scale=rstd[:, j:j + 1]).then_inc(norm_ready, 1)

            def split_turned(b, turn, gain):
                for c in range(HC):
                    act.wait_ge(turned, b * 3 * HC + turn * HC + c + 1)
                    scale = 1.0 if gain is None else vecs[:, gain, c:c + 1]
                    act.activation(xT[:, c, :], psum[c][:, :], ACT.Copy, scale=scale).then_inc(xT_ready, 1)
                    act.activation(x_hi[:, c, :], psum[c][:, :], ACT.Copy, scale=scale).then_inc(x_hi_ready, 1)

            def exps(b, h):
                act.wait_ge(bias_ready, b * HEADS + h + 1)
                if h >= 2:
                    act.wait_ge(probs_turned, b * HEADS + h - 1)
                for j in range(TT):
                    bank, col = S_AT[j]
                    n = (j + 1) * P
                    act.activation(probs[:, h % 2, j, 0:n], psum[3 * (h % 2) + bank][:, col:col + n], ACT.Exp,
                                   bias=bias[:, h, j:j + 1], scale=QK_SCALE,
                                   accum_out=row_sum[:, h, j:j + 1]).then_inc(exp_ready, 1)

            with act.Fori(0, B) as b:
                act.wait_ge(xn_loaded, b * 16 + 16)
                act.wait_ge(x2_out, b * 32 + 32)
                squares(xn, b, 0)
                scaled(xn, b, 0)
                split_turned(b, 0, V_W1)
                for m in range(HC):
                    act.wait_ge(k_done, b * HC + m + 1)
                    act.activation(kT[:, m, :], psum[m][:, :], ACT.Copy).then_inc(k_ready, 1)
                exps(b, 0)
                for h in range(HEADS):
                    act.wait_ge(probs_turned, b * HEADS + h + 1)
                    if h >= 2:
                        act.wait_ge(heads_done, b * HEADS + h - 1)
                    act.activation(pT[:, h % 2, 0:S], psum[3 * (h % 2)][:, :], ACT.Copy).then_inc(pT_by_act, 1)
                    if h + 1 < HEADS:
                        exps(b, h + 1)
                split_turned(b, 1, None)
                squares(xp, b, 1)
                scaled(xp, b, 1)
                split_turned(b, 2, V_W2)
                act.wait_ge(gap_ready, b + 1)
                act.activation(odds[:, :], gap[:, :], ACT.Exp).then_inc(odds_ready, 1)

        @block.vector
        def _(dve):
            dve.wait_ge(prefer_ready, 1)

            def inverse_rms(b, turn):
                dve.wait_ge(sq_ready, b * 2 * TT + turn * TT + TT)
                dve.tensor_scalar(mean_sq[:, :], sq[:, :], 1.0 / H, RMS_EPS, ALU.mult, ALU.add).then_inc(mean_sq_ready, 1)

            def maxima(b, h):
                dve.wait_ge(scores_done, b * HEADS + h + 1)
                for j in range(TT):
                    bank, col = S_AT[j]
                    dve.tensor_reduce(row_max[:, h, j:j + 1], psum[3 * (h % 2) + bank][:, col:col + (j + 1) * P],
                                      AX.X, ALU.max).then_inc(max_step, 1)
                dve.wait_ge(max_step, b * HEADS * TT + h * TT + TT)
                dve.tensor_scalar(bias[:, h, :], row_max[:, h, :], -QK_SCALE, None, ALU.mult).then_inc(bias_ready, 1)

            def outputs(b, h):
                dve.wait_ge(exp_ready, b * HEADS * TT + h * TT + TT)
                dve.reciprocal(row_rec[:, h, :], row_sum[:, h, :]).then_inc(rec_ready, 1)
                dve.wait_ge(rec_ready, b * HEADS + h + 1)
                dve.wait_ge(heads_done, b * HEADS + h + 1)
                dve.tensor_tensor(t[:, :, h * HD:(h + 1) * HD],
                                  psum[6 + h % 2][:, 0:TT * HD].rearrange("p (j n) -> p j n", j=TT),
                                  row_rec[:, h, :].unsqueeze(2).to_broadcast([P, TT, HD]),
                                  ALU.mult).then_inc(o_ready, 1)

            def per_tile(x):
                return x.unsqueeze(2).to_broadcast([P, TT, E])

            def routing(b):
                steps = [0]

                def step(i):
                    i.then_inc(route, 1)
                    steps[0] += 1
                    dve.wait_ge(route, b * 15 + steps[0])

                def one_hot(dst, src, n):
                    step(dve.tensor_reduce(top[:, n, :], src[:, :, :], AX.X, ALU.max))
                    step(dve.tensor_tensor(hit[:, :, :], src[:, :, :], per_tile(top[:, n, :]), ALU.is_equal))
                    step(dve.tensor_tensor(hit[:, :, :], hit[:, :, :],
                                           prefer[:, :].unsqueeze(1).to_broadcast([P, TT, E]), ALU.mult))
                    step(dve.tensor_reduce(pick[:, :], hit[:, :, :], AX.X, ALU.max))
                    step(dve.tensor_tensor(dst[:, :, :], hit[:, :, :], per_tile(pick[:, :]), ALU.is_equal))

                dve.wait_ge(logits_done, b + 1)
                step(dve.tensor_copy(logits[:, :, :], psum[4][:, 0:TT * E].rearrange("p (j e) -> p j e", e=E)))
                one_hot(first, logits, 0)
                step(dve.scalar_tensor_tensor(left[:, :, :], first[:, :, :], NEG, logits[:, :, :], ALU.mult, ALU.add))
                one_hot(second, left, 1)
                dve.tensor_tensor(gap[:, :], top[:, 1, :], top[:, 0, :], ALU.subtract).then_inc(gap_ready, 1)
                dve.wait_ge(odds_ready, b + 1)
                step(dve.tensor_scalar(p2[:, :], odds[:, :], 1.0, None, ALU.add))
                step(dve.reciprocal(p1[:, :], p2[:, :]))
                step(dve.tensor_tensor(p2[:, :], odds[:, :], p1[:, :], ALU.mult))
                assert steps[0] == 15
                dve.wait_ge(cw_out, b * 16 + 16)
                dve.tensor_tensor(cw[:, :, :], second[:, :, :], per_tile(p2[:, :]), ALU.mult).then_inc(cw_ready, 1)
                dve.tensor_tensor(first[:, :, :], first[:, :, :], per_tile(p1[:, :]), ALU.mult).then_inc(route2, 1)
                dve.wait_ge(cw_ready, b * 2 + 1)
                dve.wait_ge(route2, b + 1)
                dve.tensor_tensor(cw[:, :, :], cw[:, :, :], first[:, :, :], ALU.add).then_inc(cw_ready, 1)

            with dve.Fori(0, B) as b:
                inverse_rms(b, 0)
                for m in range(HC):
                    dve.wait_ge(q_done, b * HC + m + 1)
                    dve.tensor_copy(qT[:, m, :], psum[4 + m][:, :]).then_inc(q_ready, 1)
                for j in range(TT):
                    dve.wait_ge(v_done, b * TT + j + 1)
                    dve.tensor_copy(v[:, j, :], psum[4 + j][:, :]).then_inc(v_ready, 1)
                maxima(b, 0)
                for h in range(HEADS):
                    if h + 1 < HEADS:
                        maxima(b, h + 1)
                    dve.wait_ge(probs_turned, b * HEADS + h + 1)
                    if h >= 2:
                        dve.wait_ge(heads_done, b * HEADS + h - 1)
                    dve.tensor_copy(pT[:, h % 2, S:2 * S], psum[3 * (h % 2) + 1][:, :]).then_inc(pT_by_dve, 1)
                    dve.tensor_copy(pT[:, h % 2, 2 * S:PT_COLS],
                                    psum[3 * (h % 2) + 2][:, 0:2 * P]).then_inc(pT_by_dve, 1)
                    if h >= 2:
                        outputs(b, h - 2)
                outputs(b, HEADS - 2)
                outputs(b, HEADS - 1)
                for j in range(TT):
                    dve.wait_ge(proj_done, b * TT + j + 1)
                    dve.tensor_tensor(xp[:, j, :], psum[4 + j][:, :], xn[:, j, :], ALU.add).then_inc(xp_ready, 1)
                inverse_rms(b, 1)
                routing(b)
                dve.wait_ge(pre_step, b * 3 + 3)

        @block.tensor
        def _(pe):
            def turn():
                for c in range(HC):
                    for j in range(TT):
                        i = pe.transpose(psum[c][:, j * P:(j + 1) * P], t[:, j, c * P:(c + 1) * P], ident)
                    i.then_inc(turned, 1)

            def by_feature(n, bank, done):
                for m in range(HC):
                    for k in range(HC):
                        cols = slice(m * P, (m + 1) * P)
                        last = mm3(pe, psum[bank + m][:, :], w_hi[:, n, k, cols], w_lo[:, n, k, cols],
                                   x_hi[:, k, :], x_lo[:, k, :], k == 0, k == HC - 1)
                    last.then_inc(done, 1)

            def by_token(n, bank, done):
                for j in range(TT):
                    for k in range(HC):
                        cols = slice(j * P, (j + 1) * P)
                        last = mm3(pe, psum[bank + j][:, :], x_hi[:, k, cols], x_lo[:, k, cols],
                                   w_hi[:, n, k, :], w_lo[:, n, k, :], k == 0, k == HC - 1)
                    last.then_inc(done, 1)

            def scores(h):
                c, rows = h // 4, slice(h % 4 * HD, h % 4 * HD + HD)
                for j in (3, 2, 0, 1):
                    bank, col = S_AT[j]
                    out = psum[3 * (h % 2) + bank]
                    pe.matmul(out[:, col:col + (j + 1) * P], lhsT=qT[rows, c, j * P:(j + 1) * P],
                              rhs=kT[rows, c, 0:(j + 1) * P], start=True, stop=False)
                    i = pe.matmul(out[:, col + j * P:col + (j + 1) * P], lhsT=ident_bf, rhs=causal,
                                  start=False, stop=True)
                i.then_inc(scores_done, 1)

            def turn_probs(h):
                for kt in range(TT):
                    bank, col = PT_AT[kt]
                    for j in range(kt, TT):
                        at = col + (j - kt) * P
                        i = pe.transpose(psum[3 * (h % 2) + bank][:, at:at + P],
                                         probs[:, h % 2, j, kt * P:(kt + 1) * P], ident)
                i.then_inc(probs_turned, 1)

            def head_output(b, h):
                pe.wait_ge(pT_by_act, b * HEADS + h + 1)
                pe.wait_ge(pT_by_dve, b * 2 * HEADS + 2 * h + 2)
                if h >= 2:
                    pe.wait_ge(o_ready, b * HEADS + h - 1)
                for j in range(TT):
                    for kt in range(j + 1):
                        bank, col = PT_AT[kt]
                        at = bank * S + col + (j - kt) * P
                        i = pe.matmul(psum[6 + h % 2][:, j * HD:(j + 1) * HD], lhsT=pT[:, h % 2, at:at + P],
                                      rhs=v[:, kt, h * HD:(h + 1) * HD], start=(kt == 0), stop=(kt == j))
                i.then_inc(heads_done, 1)

            pe.wait_ge(w_lo_ready, N_W)
            pe.wait_ge(const_in, 32)
            with pe.Fori(0, B) as b:
                pe.wait_ge(norm_ready, b * 2 * TT + TT)
                turn()
                pe.wait_ge(x_lo_ready, b * 3 * HC + HC)
                pe.wait_ge(cw_out, b * 16 + 16)
                by_feature(0, 4, q_done)
                by_feature(1, 0, k_done)
                pe.wait_ge(q_ready, b * HC + HC)
                by_token(2, 4, v_done)
                pe.wait_ge(k_ready, b * HC + HC)
                scores(0)
                pe.wait_ge(v_ready, b * TT + TT)
                for h in range(HEADS):
                    if h >= 2:
                        head_output(b, h - 2)
                    if h + 1 < HEADS:
                        if h >= 1:
                            pe.wait_ge(pT_by_act, b * HEADS + h)
                            pe.wait_ge(pT_by_dve, b * 2 * HEADS + 2 * h)
                        scores(h + 1)
                    pe.wait_ge(exp_ready, b * HEADS * TT + h * TT + TT)
                    turn_probs(h)
                head_output(b, HEADS - 2)
                head_output(b, HEADS - 1)
                pe.wait_ge(o_ready, b * HEADS + HEADS)
                turn()
                pe.wait_ge(x_lo_ready, b * 3 * HC + 2 * HC)
                by_token(3, 4, proj_done)
                pe.wait_ge(norm_ready, b * 2 * TT + 2 * TT)
                turn()
                pe.wait_ge(xT_ready, b * 3 * HC + 3 * HC)
                for j in range(TT):
                    for k in range(HC):
                        i = pe.matmul(psum[4][:, j * E:(j + 1) * E], lhsT=xT[:, k, j * P:(j + 1) * P],
                                      rhs=wr[:, k, :], start=(k == 0), stop=(k == HC - 1))
                i.then_inc(logits_done, 1)


def constants(nc, ident, ident_bf, causal):
    with ExitStack() as ctx:
        filled = ctx.enter_context(nc.semaphore("c_filled"))
        block = ctx.enter_context(nc.Block())

        @block.gpsimd
        def _(pool):
            pool.memset(ident[:, :], 0.0).then_inc(filled, 1)
            pool.memset(ident_bf[:, :], 0.0).then_inc(filled, 1)
            pool.memset(causal[:, :], 0.0).then_inc(filled, 1)
            pool.wait_ge(filled, 3)
            for m in (ident, ident_bf):
                pool.affine_select(out=m[:, :], in_=m[:, :], compare_op=ALU.not_equal, fill=1.0, base=0,
                                   pattern=[[-1, P]], channel_multiplier=1).then_inc(filled, 1)
            pool.affine_select(out=causal[:, :], in_=causal[:, :], compare_op=ALU.is_ge, fill=NEG, base=0,
                               pattern=[[-1, P]], channel_multiplier=1).then_inc(filled, 1)
            pool.wait_ge(filled, 6)


def build(nc, d):
    for name, shape in (("xn", [B, S, H]), ("base", [B, S, H]), ("rc", [B, S, H]), ("vc", [B, S, H]),
                        ("pre", [B, S, H]), ("cw", [B, P, TT * E]), ("xc_hi", [B, P, HC, S]),
                        ("xc_lo", [B, P, HC, S]), ("x2_hi", [B, P, HC, S]), ("x2_lo", [B, P, HC, S])):
        d[name] = nc.dram_tensor("scratch_" + name, shape, F32, kind="Internal").ap()
    with ExitStack() as ctx:
        psum = [ctx.enter_context(nc.psum_tensor(f"bank{n}", [P, 512], F32)) for n in range(8)]
        ident = ctx.enter_context(nc.sbuf_tensor("ident", [P, P], F32))
        ident_bf = ctx.enter_context(nc.sbuf_tensor("ident_bf", [P, P], BF16))
        causal = ctx.enter_context(nc.sbuf_tensor("causal", [P, P], BF16))
        constants(nc, ident, ident_bf, causal)
        time_mix_phase(nc, psum, ident[:, :], d)
        mlp_phase(nc, psum, d, gated=False)
        attention_phase(nc, psum, ident[:, :], ident_bf[:, :], causal[:, :], d)
        mlp_phase(nc, psum, d, gated=True)


def kernel(**inputs):
    import numpy as np
    import concourse.bacc as bacc
    from concourse.bass_utils import run_bass_kernel_spmd

    g = {n.replace("L0_", ""): np.asarray(a) for n, a in inputs.items()}

    def in_tiles(w):
        k = w.shape[0] // P
        return w.reshape(k, P, -1).transpose(1, 0, 2).reshape(P, -1)

    def up_chunks(w):
        return w.reshape(HC, P, -1, CH).transpose(2, 1, 0, 3).reshape(-1, P, HC * CH)

    def down_chunks(w):
        return w.reshape(-1, CK, P, H).transpose(0, 2, 1, 3).reshape(-1, P, CK * H)

    def per_feature(v):
        return v.reshape(HC, P).T

    def experts_up(w):
        return np.concatenate([up_chunks(w[e].T) for e in range(E)])

    arrays = {
        "x": g["attn_x"],
        "w_tm": np.stack([in_tiles(g["attn_" + n]) for n in ("Wv", "Wr", "Wcr", "Wo")]),
        "w_at": np.stack([in_tiles(g["ffn_" + n].T) for n in ("Wq", "Wk", "Wv", "Wo")]),
        "w_r": g["ffn_Wr"].T.reshape(HC, P, E).transpose(1, 0, 2),
        "w_cm": np.concatenate([up_chunks(g["attn_Wck"]), down_chunks(g["attn_Wcv"])], axis=2),
        "w_moe": np.concatenate([experts_up(g["ffn_Wg"]), experts_up(g["ffn_Wu"]),
                                 np.concatenate([down_chunks(g["ffn_Wd"][e].T) for e in range(E)])], axis=2),
        "vecs": np.stack([per_feature(g[n]) for n in (
            "attn_tm_g", "attn_tm_b", "attn_time_first", "attn_time_decay", "attn_cm_g", "attn_cm_b",
            "ffn_w_ln1", "ffn_w_ln2")], axis=1),
        "rows": np.stack([g["attn_" + n] for n in ("ln1_g", "ln1_b", "ln2_g", "ln2_b", "bo")]),
    }
    arrays = {"in_" + n: np.ascontiguousarray(a) for n, a in arrays.items()}
    nc = bacc.Bacc("TRN2", target_bir_lowering=False, num_devices=1)
    d = {n[3:]: nc.dram_tensor(n, a.shape, F32, kind="ExternalInput").ap() for n, a in arrays.items()}
    d["out"] = nc.dram_tensor("out", [B, S, H], F32, kind="ExternalOutput").ap()
    build(nc, d)
    r = run_bass_kernel_spmd(nc, [arrays], core_ids=[0])
    return r.results[0]["out"]
```

```python
from contextlib import ExitStack

import concourse.bass as bass
from concourse import mybir

F32 = mybir.dt.float32
F32R = mybir.dt.float32r
BF16 = mybir.dt.bfloat16
ALU = mybir.AluOpType
ACT = mybir.ActivationFunctionType
AX = mybir.AxisListType

P = 128
B, S, H = 4, 512, 512
TT = S // P
HC = H // P
HEADS, HD = 16, 32
E = 8
I_CM = 2048
I_MOE = 1024
CH = 256
CK = CH // P
CHUNKS_CM = I_CM // CH
CHUNKS_E = I_MOE // CH
T_ALL = B * TT
TILE = 256
TP = TILE // P
TILES = (2 * B * S - E) // TILE + E
MAX_TILES = B * S // TILE
ROUTE = 2 * TT * E + 2 * TT
NEG = -1.0e30
LN_EPS = 1e-5
LN12_EPS = 1e-12
RMS_EPS = 1e-5
QK_SCALE = HD ** -0.5

V_TMG, V_TMB, V_TF, V_TD, V_CMG, V_CMB, V_W1, V_W2 = range(8)
R_G1, R_B1, R_G2, R_B2 = range(4)


def mm3(pe, out, w_hi, w_lo, x_hi, x_lo, first, last):
    pe.matmul(out, lhsT=w_hi, rhs=x_hi, start=first, stop=False)
    pe.matmul(out, lhsT=w_hi, rhs=x_lo, start=False, stop=False)
    return pe.matmul(out, lhsT=w_lo, rhs=x_hi, start=False, stop=last)


def time_mix_phase(nc, psum, ident, d):
    with ExitStack() as ctx:
        def sb(name, shape, dt=F32):
            return ctx.enter_context(nc.sbuf_tensor("tm_" + name, shape, dt))

        def sem(name):
            return ctx.enter_context(nc.semaphore("tm_" + name))

        w_stage = sb("w_stage", [P, 3, HC * H])
        w_hi = sb("w_hi", [P, 3, HC, H], F32R)
        w_lo = sb("w_lo", [P, 3, HC, H], F32R)
        wo = sb("wo", [P, HC, H])
        bo_row = sb("bo_row", [1, H])
        ones_row = sb("ones_row", [1, P])
        vecs = sb("vecs", [P, 8, HC])
        rows = sb("rows", [P, 4, H])
        one_minus_tf = sb("one_minus_tf", [P, HC])
        steps_left = sb("steps_left", [P, S])
        decay = sb("decay", [P, HC, S])
        x_in = sb("x_in", [P, TT, H])
        xn = sb("xn", [P, TT, H])
        t1 = sb("t1", [P, TT, H])
        t2 = sb("t2", [P, TT, H])
        xT = sb("xT", [P, HC, S + 2])
        x_hi = sb("x_hi", [P, HC, S], F32R)
        x_lo = sb("x_lo", [P, HC, S], F32R)
        mix = sb("mix", [P, HC, S])
        m_hi = sb("m_hi", [P, HC, S], F32R)
        m_lo = sb("m_lo", [P, HC, S], F32R)
        junk = sb("junk", [P, S])
        vmix = sb("vmix", [P, HC])
        vmix_wide = sb("vmix_wide", [P, HC, P])
        stats = sb("stats", [P, TT, 6])
        mv = sb("mv", [P, TT, 2])
        rstd = sb("rstd", [P, TT])
        nmr = sb("nmr", [P, TT])
        var_eps = sb("var_eps", [P, TT])
        spare = sb("spare", [P, 8])
        minus_half = sb("minus_half", [P, TT])

        const_in = sem("const_in")
        w_in = sem("w_in")
        w_hi_ready = sem("w_hi_ready")
        w_lo_ready = sem("w_lo_ready")
        consts_ready = sem("consts_ready")
        steps_ready = sem("steps_ready")
        decay_ready = sem("decay_ready")
        x_loaded = sem("x_loaded")
        stat = sem("stat")
        half_ready = sem("half_ready")
        rstd_ready = sem("rstd_ready")
        xn_ready = sem("xn_ready")
        x1_step = sem("x1_step")
        norm_ready = sem("norm_ready")
        turned = sem("turned")
        xT_ready = sem("xT_ready")
        x_hi_ready = sem("x_hi_ready")
        x_lo_ready = sem("x_lo_ready")
        mix_step = sem("mix_step")
        m_hi_ready = sem("m_hi_ready")
        m_lo_ready = sem("m_lo_ready")
        v_done = sem("v_done")
        vmix_step = sem("vmix_step")
        row_done = sem("row_done")
        r_done = sem("r_done")
        r_ready = sem("r_ready")
        x2_step = sem("x2_step")
        base_ready = sem("base_ready")
        x2n_step = sem("x2n_step")
        rc_done = sem("rc_done")
        rc_ready = sem("rc_ready")
        xn_out = sem("xn_out")
        base_out = sem("base_out")
        xc_out = sem("xc_out")
        rc_out = sem("rc_out")

        tokens = "(j p) h -> p j h"
        block = ctx.enter_context(nc.Block())

        @block.sync
        def _(sp):
            sp.dma_start(vecs[:, :, :], d["vecs"]).then_inc(const_in, 16)
            for n in range(4):
                sp.dma_start(rows[:, n, :], d["rows"][n:n + 1, :].partition_broadcast(P)).then_inc(const_in, 16)
            for n in range(3):
                sp.dma_start(w_stage[:, n, :], d["w_tm"][n]).then_inc(w_in, 16)
            sp.dma_start(wo[:, :, :], d["w_tm"][3].rearrange("p (k n) -> p k n", k=HC)).then_inc(const_in, 16)
            sp.dma_start(bo_row[:, :], d["rows"][4:5, :]).then_inc(const_in, 16)
            with sp.Fori(0, B) as b:
                sp.wait_ge(base_out, b * 16 + 16)
                sp.dma_start(x_in[:, :, :], d["x"][b].rearrange(tokens, p=P)).then_inc(x_loaded, 16)
                sp.wait_ge(xn_ready, b * TT + TT)
                sp.dma_start(d["xn"][b].rearrange(tokens, p=P), xn[:, :, :]).then_inc(xn_out, 16)
                sp.wait_ge(base_ready, b + 1)
                sp.dma_start(d["base"][b].rearrange(tokens, p=P), x_in[:, :, :]).then_inc(base_out, 16)
                sp.wait_ge(m_hi_ready, b * 2 * HC + 2 * HC)
                sp.dma_start(d["xc_hi"][b], m_hi[:, :, :].bitcast(F32)).then_inc(xc_out, 16)
                sp.wait_ge(m_lo_ready, b * 2 * HC + 2 * HC)
                sp.dma_start(d["xc_lo"][b], m_lo[:, :, :].bitcast(F32)).then_inc(xc_out, 16)
            sp.wait_ge(xn_out, 16 * (B + 1))
            sp.wait_ge(base_out, 16 * (B + 1))
            sp.wait_ge(xc_out, 32 * (B + 1))
            sp.wait_ge(rc_out, 16 * (B + 1))

        @block.gpsimd
        def _(pool):
            pool.iota(steps_left[:, :], [[-1, S]], base=S - 1, channel_multiplier=0,
                      allow_small_or_imprecise_dtypes=True).then_inc(steps_ready, 1)
            for n in range(3):
                pool.wait_ge(w_hi_ready, n + 1)
                pool.tensor_tensor(w_lo[:, n, :, :].rearrange("p k n -> p (k n)"), w_stage[:, n, :],
                                   w_hi[:, n, :, :].rearrange("p k n -> p (k n)").bitcast(F32),
                                   ALU.subtract).then_inc(w_lo_ready, 1)
            pool.memset(minus_half[:, :], -0.5).then_inc(half_ready, 1)
            pool.wait_ge(half_ready, 1)

            def inverse_root(turn):
                pool.wait_ge(stat, turn * 10 + 2 * TT + 1)
                pool.tensor_tensor(rstd[:, :], var_eps[:, :], minus_half[:, :], ALU.pow).then_inc(rstd_ready, 1)

            with pool.Fori(0, B) as b:
                for n in range(3):
                    inverse_root(b * 5 + n)
                for c in range(HC):
                    pool.wait_ge(x_hi_ready, b * HC + c + 1)
                    pool.tensor_tensor(x_lo[:, c, :], xT[:, c, 1:S + 1], x_hi[:, c, :].bitcast(F32),
                                       ALU.subtract).then_inc(x_lo_ready, 1)
                for c in range(HC):
                    pool.wait_ge(m_hi_ready, b * 2 * HC + c + 1)
                    pool.tensor_tensor(m_lo[:, c, :], mix[:, c, :], m_hi[:, c, :].bitcast(F32),
                                       ALU.subtract).then_inc(m_lo_ready, 1)
                inverse_root(b * 5 + 3)
                inverse_root(b * 5 + 4)
                pool.wait_ge(x2_step, b * 2 * TT + 2 * TT)
                pool.tensor_tensor(x_in[:, :, :], x_in[:, :, :], t1[:, :, :], ALU.add).then_inc(base_ready, 1)
                for c in range(HC):
                    pool.wait_ge(m_hi_ready, b * 2 * HC + HC + c + 1)
                    pool.tensor_tensor(m_lo[:, c, :], xT[:, c, 1:S + 1], m_hi[:, c, :].bitcast(F32),
                                       ALU.subtract).then_inc(m_lo_ready, 1)

        @block.scalar
        def _(act):
            act.wait_ge(const_in, 16 * 7)
            act.wait_ge(steps_ready, 1)
            for c in range(HC):
                act.activation(decay[:, c, :], steps_left[:, :], ACT.Exp,
                               scale=vecs[:, V_TD, c:c + 1]).then_inc(decay_ready, 1)
            for n in range(3):
                act.wait_ge(w_in, 16 * (n + 1))
                act.activation(w_hi[:, n, :, :].rearrange("p k n -> p (k n)"), w_stage[:, n, :],
                               ACT.Copy).then_inc(w_hi_ready, 1)
            with act.Fori(0, B) as b:
                act.wait_ge(stat, b * 50 + 10)
                for j in range(TT):
                    act.activation(xn[:, j, :], x_in[:, j, :], ACT.Identity, bias=nmr[:, j:j + 1],
                                   scale=rstd[:, j:j + 1]).then_inc(xn_ready, 1)
                act.wait_ge(stat, b * 50 + 30)
                for j in range(TT):
                    act.activation(t2[:, j, :], t1[:, j, :], ACT.Identity, bias=nmr[:, j:j + 1],
                                   scale=rstd[:, j:j + 1]).then_inc(norm_ready, 1)
                for c in range(HC):
                    act.wait_ge(turned, b * 2 * HC + c + 1)
                    act.activation(xT[:, c, 1:S + 1], psum[c][:, :], ACT.Identity,
                                   bias=vecs[:, V_TMB, c:c + 1], scale=vecs[:, V_TMG, c:c + 1]).then_inc(xT_ready, 1)
                    act.activation(x_hi[:, c, :], psum[c][:, :], ACT.Identity,
                                   bias=vecs[:, V_TMB, c:c + 1],
                                   scale=vecs[:, V_TMG, c:c + 1]).then_inc(x_hi_ready, 1)
                for c in range(HC):
                    act.wait_ge(mix_step, b * 2 * HC + 2 * c + 2)
                    act.activation(m_hi[:, c, :], mix[:, c, :], ACT.Copy).then_inc(m_hi_ready, 1)
                for j in range(TT):
                    act.wait_ge(r_done, b * TT + j + 1)
                    act.activation(t1[:, j, :], psum[j][:, :], ACT.Sigmoid).then_inc(r_ready, 1)
                act.wait_ge(stat, b * 50 + 50)
                for j in range(TT):
                    act.activation(t2[:, j, :], t2[:, j, :], ACT.Identity, bias=nmr[:, j:j + 1],
                                   scale=rstd[:, j:j + 1]).then_inc(norm_ready, 1)
                for c in range(HC):
                    act.wait_ge(turned, b * 2 * HC + HC + c + 1)
                    act.activation(xT[:, c, 1:S + 1], psum[HC + c][:, :], ACT.Identity,
                                   bias=vecs[:, V_CMB, c:c + 1], scale=vecs[:, V_CMG, c:c + 1]).then_inc(xT_ready, 1)
                    act.activation(m_hi[:, c, :], psum[HC + c][:, :], ACT.Identity,
                                   bias=vecs[:, V_CMB, c:c + 1],
                                   scale=vecs[:, V_CMG, c:c + 1]).then_inc(m_hi_ready, 1)
                for j in range(TT):
                    act.wait_ge(rc_done, b * TT + j + 1)
                    act.activation(t2[:, j, :], psum[j][:, :], ACT.Sigmoid).then_inc(rc_ready, 1)
                act.wait_ge(rc_ready, b * TT + TT)
                act.dma_start(d["rc"][b].rearrange(tokens, p=P), t2[:, :, :]).then_inc(rc_out, 16)

        @block.vector
        def _(dve):
            dve.memset(ones_row[:, :], 1.0).then_inc(consts_ready, 1)
            for c in range(HC):
                dve.memset(xT[:, c, 0:1], 0.0).then_inc(consts_ready, 1)
            dve.wait_ge(const_in, 16 * 7)
            dve.tensor_scalar(one_minus_tf[:, :], vecs[:, V_TF, :], -1.0, 1.0, ALU.mult,
                              ALU.add).then_inc(consts_ready, 1)
            for i, (out_sem, n) in enumerate(((xn_out, 16), (base_out, 16), (xc_out, 32), (rc_out, 16))):
                dve.memset(spare[:, i:i + 1], 0.0).then_inc(out_sem, n)
            dve.wait_ge(consts_ready, HC + 2)

            def moments(src, turn, eps):
                base = turn * 10
                for j in range(TT):
                    dve.bn_stats(stats[:, j, :], src[:, j, :]).then_inc(stat, 1)
                dve.wait_ge(stat, base + TT)
                dve.memset(spare[:, 4:5], 0.0)
                for j in range(TT):
                    dve.bn_aggr(mv[:, j, :], stats[:, j, :]).then_inc(stat, 1)
                dve.wait_ge(stat, base + 2 * TT)
                dve.tensor_scalar(var_eps[:, :], mv[:, :, 1], eps, None, ALU.add).then_inc(stat, 1)
                dve.wait_ge(rstd_ready, turn + 1)
                dve.scalar_tensor_tensor(nmr[:, :], mv[:, :, 0], -1.0, rstd[:, :], ALU.mult,
                                         ALU.mult).then_inc(stat, 1)
                dve.wait_ge(stat, base + 2 * TT + 2)

            def affine_norm(dst, src, row_g, row_b, step, base):
                for j in range(TT):
                    dve.scalar_tensor_tensor(dst[:, j, :], src[:, j, :], mv[:, j, 0:1], rows[:, row_g, :],
                                             ALU.subtract, ALU.mult).then_inc(step, 1)
                for j in range(TT):
                    dve.wait_ge(step, base + j + 1)
                    dve.scalar_tensor_tensor(dst[:, j, :], dst[:, j, :], rstd[:, j:j + 1], rows[:, row_b, :],
                                             ALU.mult, ALU.add).then_inc(step, 1)
                dve.wait_ge(step, base + 2 * TT)

            with dve.Fori(0, B) as b:
                dve.wait_ge(x_loaded, b * 16 + 16)
                dve.wait_ge(xn_out, b * 16 + 16)
                dve.wait_ge(rc_out, b * 16 + 16)
                dve.wait_ge(xc_out, b * 32 + 32)
                moments(x_in, b * 5, LN_EPS)
                dve.wait_ge(xn_ready, b * TT + TT)
                moments(xn, b * 5 + 1, LN12_EPS)
                affine_norm(t1, xn, R_G1, R_B1, x1_step, b * 2 * TT)
                moments(t1, b * 5 + 2, LN12_EPS)
                for c in range(HC):
                    dve.wait_ge(xT_ready, b * 2 * HC + c + 1)
                    dve.tensor_scalar(mix[:, c, :], xT[:, c, 1:S + 1], vecs[:, V_TF, c:c + 1], None,
                                      ALU.mult).then_inc(mix_step, 1)
                    dve.wait_ge(mix_step, b * 2 * HC + 2 * c + 1)
                    dve.scalar_tensor_tensor(mix[:, c, :], xT[:, c, 0:S], one_minus_tf[:, c:c + 1], mix[:, c, :],
                                             ALU.mult, ALU.add).then_inc(mix_step, 1)
                dve.wait_ge(decay_ready, HC)
                for m in range(HC):
                    dve.wait_ge(v_done, b * HC + m + 1)
                    if m:
                        dve.wait_ge(vmix_step, b * (HC + 1) + m)
                    dve.tensor_tensor_reduce(junk[:, :], psum[HC + m][:, :], decay[:, m, :], 1.0, 0.0, ALU.mult,
                                             ALU.add, vmix[:, m:m + 1]).then_inc(vmix_step, 1)
                dve.wait_ge(vmix_step, b * (HC + 1) + HC)
                dve.tensor_copy(vmix_wide[:, :, :],
                                vmix[:, :].unsqueeze(2).to_broadcast([P, HC, P])).then_inc(vmix_step, 1)
                dve.wait_ge(row_done, b + 1)
                for j in range(TT):
                    dve.wait_ge(r_ready, b * TT + j + 1)
                    dve.tensor_tensor(t1[:, j, :], t1[:, j, :], psum[HC][:, :], ALU.mult).then_inc(x2_step, 1)
                for j in range(TT):
                    dve.wait_ge(x2_step, b * 2 * TT + j + 1)
                    dve.tensor_tensor(t1[:, j, :], t1[:, j, :], xn[:, j, :], ALU.add).then_inc(x2_step, 1)
                dve.wait_ge(x2_step, b * 2 * TT + 2 * TT)
                moments(t1, b * 5 + 3, LN12_EPS)
                affine_norm(t2, t1, R_G2, R_B2, x2n_step, b * 2 * TT)
                moments(t2, b * 5 + 4, LN12_EPS)
                dve.wait_ge(norm_ready, b * 2 * TT + 2 * TT)
                dve.wait_ge(base_ready, b + 1)

        @block.tensor
        def _(pe):
            def turn(bank, base):
                for c in range(HC):
                    for j in range(TT):
                        t = pe.transpose(psum[bank + c][:, j * P:(j + 1) * P], t2[:, j, c * P:(c + 1) * P], ident)
                    t.then_inc(turned, 1)

            pe.wait_ge(w_hi_ready, 3)
            pe.wait_ge(w_lo_ready, 3)
            pe.wait_ge(const_in, 16 * 7)
            pe.wait_ge(consts_ready, 1)
            with pe.Fori(0, B) as b:
                pe.wait_ge(rc_out, b * 16 + 16)
                pe.wait_ge(norm_ready, b * 2 * TT + TT)
                turn(0, b)
                pe.wait_ge(xc_out, b * 32 + 32)
                for m in range(HC):
                    for k in range(HC):
                        if m == 0:
                            pe.wait_ge(x_hi_ready, b * HC + k + 1)
                            pe.wait_ge(x_lo_ready, b * HC + k + 1)
                        cols = slice(m * P, (m + 1) * P)
                        last = mm3(pe, psum[HC + m][:, :], w_hi[:, 0, k, cols], w_lo[:, 0, k, cols],
                                   x_hi[:, k, :], x_lo[:, k, :], k == 0, k == HC - 1)
                    last.then_inc(v_done, 1)
                for j in range(TT):
                    for k in range(HC):
                        if j == 0:
                            pe.wait_ge(m_lo_ready, b * 2 * HC + k + 1)
                        cols = slice(j * P, (j + 1) * P)
                        last = mm3(pe, psum[j][:, :], m_hi[:, k, cols], m_lo[:, k, cols],
                                   w_hi[:, 1, k, :], w_lo[:, 1, k, :], k == 0, k == HC - 1)
                    last.then_inc(r_done, 1)
                pe.wait_ge(vmix_step, b * (HC + 1) + HC + 1)
                for m in range(HC):
                    pe.matmul(psum[HC][:, :], lhsT=vmix_wide[:, m, :], rhs=wo[:, m, :], start=(m == 0), stop=False)
                pe.matmul(psum[HC][:, :], lhsT=ones_row[:, :], rhs=bo_row[:, :], start=False,
                          stop=True).then_inc(row_done, 1)
                pe.wait_ge(x2_step, b * 2 * TT + TT)
                pe.wait_ge(norm_ready, b * 2 * TT + 2 * TT)
                turn(HC, b)
                pe.wait_ge(r_ready, b * TT + TT)
                for j in range(TT):
                    for k in range(HC):
                        if j == 0:
                            pe.wait_ge(m_lo_ready, b * 2 * HC + HC + k + 1)
                        cols = slice(j * P, (j + 1) * P)
                        last = mm3(pe, psum[j][:, :], m_hi[:, k, cols], m_lo[:, k, cols],
                                   w_hi[:, 2, k, :], w_lo[:, 2, k, :], k == 0, k == HC - 1)
                    last.then_inc(rc_done, 1)


def channel_mix_phase(nc, psum, d, routing):
    WD = HC * CH
    WW = WD + CK * H
    STEPS = 2 * B
    TURNS = CHUNKS_CM // 2
    tokens = "(j p) h -> p j h"

    with ExitStack() as ctx:
        def sb(nm, shape, dt=F32):
            return ctx.enter_context(nc.sbuf_tensor("cm_" + nm, shape, dt))

        def sem(nm):
            return ctx.enter_context(nc.semaphore("cm_" + nm))

        x_hi = sb("x_hi", [P, HC, B, S + 2], F32R)
        x_lo = sb("x_lo", [P, HC, B, S + 2], F32R)
        acc = sb("acc", [P, T_ALL, H])
        stage = sb("stage", [P, 2, WW])
        w_hi = sb("w_hi", [P, 2, WW], F32R)
        w_lo = sb("w_lo", [P, 2, WW], F32R)
        relu = sb("relu", [P, CK, S])
        a = sb("a", [P, CK, S])
        a_hi = sb("a_hi", [P, 2, CK, S], F32R)
        a_lo = sb("a_lo", [P, 2, CK, S], F32R)
        rc = sb("rc", [P, TT, H])
        pre = sb("pre", [P, TT, H])
        rows = sb("rows", [P, TT, H])
        spare = sb("spare", [P, 8])

        x_loaded = [sem(f"x_loaded{b}") for b in range(B)]
        stage_in = [sem(f"stage_in{u}") for u in range(2)]
        w_hi_ready = [sem(f"w_hi_ready{u}") for u in range(2)]
        w_lo_ready = [sem(f"w_lo_ready{u}") for u in range(2)]
        zeroed = sem("zeroed")
        up_done = sem("up_done")
        relu_ready = sem("relu_ready")
        a_full = sem("a_full")
        a_hi_ready = sem("a_hi_ready")
        a_lo_ready = sem("a_lo_ready")
        y_done = sem("y_done")
        y_free = sem("y_free")
        res_loaded = sem("res_loaded")
        gated = sem("gated")
        pre_out = sem("pre_out")
        rows_loaded = sem("rows_loaded")
        sent = sem("sent")
        up_bank = psum[0:CK]
        y_bank = psum[2 * CK:2 * CK + TT]
        route = Router(nc, ctx, psum[2], psum[3], routing)

        block = ctx.enter_context(nc.Block())

        @block.sync
        def _(sp):
            def load(u, n):
                sp.dma_start(stage[:, u, :], d["w_cm"][n]).then_inc(stage_in[u], 16)

            load(0, 0)
            for b in range(B):
                sp.dma_start(x_hi[:, :, b, 2:S + 2].bitcast(F32), d["xc_hi"][b]).then_inc(x_loaded[b], 16)
                sp.dma_start(x_lo[:, :, b, 2:S + 2].bitcast(F32), d["xc_lo"][b]).then_inc(x_loaded[b], 16)
                if b == 0:
                    sp.dma_start(route.rows_in, d["route"].rearrange("b p t -> p b t")).then_inc(route.loaded, 16)
                    load(1, 1)
            with sp.Fori(0, TURNS - 1) as it:
                for u in range(2):
                    sp.wait_ge(w_lo_ready[u], it + 1)
                    load(u, it * 2 + u + 2)
            with sp.Fori(0, B) as b:
                sp.wait_ge(pre_out, b * 16 + 16)
                sp.dma_start(rc[:, :, :], d["rc"][b].rearrange(tokens, p=P)).then_inc(res_loaded, 16)
                sp.dma_start(pre[:, :, :], d["pre"][b].rearrange(tokens, p=P)).then_inc(res_loaded, 16)
                sp.wait_ge(gated, b * 2 * TT + 2 * TT)
                sp.dma_start(d["pre2"][b].rearrange(tokens, p=P), pre[:, :, :]).then_inc(pre_out, 16)
            sp.wait_ge(pre_out, 16 * (B + 1))

        @block.gpsimd
        def _(pool):
            pool.memset(spare[:, 5:6], 0.0)
            route.masks_on_pool(pool)
            pool.wait_ge(route.slots_ready, 2)
            with pool.Fori(0, B) as b:
                pool.dma_start(rows[:, :, :], d["x2"][b].rearrange(tokens, p=P)).then_inc(rows_loaded, 16)
                for n in range(2):
                    pool.tensor_copy(route.now[:, n, :], route.slots[:, n, b, :]).then_inc(route.now_ready, 1)
                pool.wait_ge(route.now_ready, b * 2 + 2)
                pool.wait_ge(rows_loaded, b * 16 + 16)
                pool.tensor_tensor(spare[:, 6:7], spare[:, 5:6], spare[:, 5:6], ALU.add)
                for j in range(TT):
                    for n in range(2):
                        pool.indirect_dma_start(
                            out=d["tiles_in"], out_offset=bass.IndirectOffsetOnAxis(ap=route.now[:, n, j:j + 1], axis=0),
                            in_=rows[:, j, :], in_offset=None).then_inc(sent, 16)
                pool.wait_ge(sent, b * 32 * TT + 32 * TT)

        @block.scalar
        def _(act):
            def split(u, n, g):
                act.wait_ge(stage_in[u], n * 16 + 16)
                if g is not None:
                    act.wait_ge(y_done, g * TT + 2 * TT)
                act.activation(w_hi[:, u, :], stage[:, u, :], ACT.Copy).then_inc(w_hi_ready[u], 1)

            def up(g, s):
                for m in range(CK):
                    act.wait_ge(up_done, g * CK + m + 1)
                    act.wait_ge(a_full, g * CK + m + 1)
                    act.activation(relu[:, m, :], up_bank[m][:, :], ACT.Relu).then_inc(relu_ready, 1)
                for m in range(CK):
                    act.wait_ge(a_full, g * CK + CK + m + 1)
                    if m == 0:
                        act.wait_ge(y_done, g * TT + TT)
                    act.activation(a_hi[:, s % 2, m, :], a[:, m, :], ACT.Copy).then_inc(a_hi_ready, 1)

            def turn(it, last):
                for s in range(STEPS):
                    if s == 0:
                        split(1, it, it * STEPS)
                    if s == B and not last:
                        split(0, it + 1, it * STEPS + B)
                    if not (last and s == STEPS - 1):
                        up(it * STEPS + s + 1, s + 1)

            split(0, 0, None)
            up(0, 0)
            with act.Fori(0, TURNS - 1) as it:
                turn(it, False)
            turn(TURNS - 1, True)

        @block.vector
        def _(dve):
            dve.memset(x_hi[:, :, :, 0:2].bitcast(F32), 0.0).then_inc(zeroed, 1)
            dve.memset(x_lo[:, :, :, 0:2].bitcast(F32), 0.0).then_inc(zeroed, 1)
            dve.memset(acc[:, :, :], 0.0).then_inc(zeroed, 1)
            dve.memset(spare[:, 0:1], 0.0).then_inc(pre_out, 16)
            dve.memset(spare[:, 1:2], 0.0).then_inc(a_full, CK)
            dve.memset(spare[:, 2:3], 0.0).then_inc(y_done, 2 * TT)
            dve.memset(spare[:, 3:4], 0.0).then_inc(y_free, 4 * TT)
            dve.memset(spare[:, 4:5], 0.0).then_inc(a_lo_ready, CK)
            dve.wait_ge(zeroed, 3)
            route.on_dve(dve)

            def split(u, n):
                dve.wait_ge(w_hi_ready[u], n + 1)
                dve.tensor_tensor(w_lo[:, u, :], stage[:, u, :], w_hi[:, u, :].bitcast(F32),
                                  ALU.subtract).then_inc(w_lo_ready[u], 1)

            def product(g, s):
                for m in range(CK):
                    dve.wait_ge(relu_ready, g * CK + m + 1)
                    dve.wait_ge(a_lo_ready, g * CK + m + 1)
                    dve.scalar_tensor_tensor(a[:, m, :], up_bank[m][:, :], 0.0, relu[:, m, :],
                                             ALU.max, ALU.mult).then_inc(a_full, 1)
                for m in range(CK):
                    dve.wait_ge(a_hi_ready, g * CK + m + 1)
                    dve.tensor_tensor(a_lo[:, s % 2, m, :], a[:, m, :], a_hi[:, s % 2, m, :].bitcast(F32),
                                      ALU.subtract).then_inc(a_lo_ready, 1)

            def accumulate(g, s):
                for j in range(TT):
                    t = (s % B) * TT + j
                    dve.wait_ge(y_done, g * TT + 2 * TT + j + 1)
                    dve.wait_ge(y_free, g * TT + j + 1)
                    dve.tensor_tensor(acc[:, t, :], y_bank[j][:, :], acc[:, t, :], ALU.add).then_inc(y_free, 1)

            def gate(b):
                dve.wait_ge(res_loaded, b * 32 + 32)
                dve.wait_ge(y_free, 4 * TT + TURNS * STEPS * TT - (B - 1 - b) * TT)
                for j in range(TT):
                    dve.tensor_tensor(rc[:, j, :], rc[:, j, :], acc[:, b * TT + j, :], ALU.mult).then_inc(gated, 1)
                for j in range(TT):
                    dve.wait_ge(gated, b * 2 * TT + j + 1)
                    dve.tensor_tensor(pre[:, j, :], pre[:, j, :], rc[:, j, :], ALU.add).then_inc(gated, 1)

            def turn(it, last):
                for s in range(STEPS):
                    if s == 0:
                        split(1, it)
                    if s == B and not last:
                        split(0, it + 1)
                    if not (last and s == STEPS - 1):
                        product(it * STEPS + s + 1, s + 1)
                    accumulate(it * STEPS + s, s)
                    if last and s > B:
                        gate(s - B - 1)

            split(0, 0)
            product(0, 0)
            with dve.Fori(0, TURNS - 1) as it:
                turn(it, False)
            turn(TURNS - 1, True)
            gate(B - 1)

        @block.tensor
        def _(pe):
            def up(g, s, n):
                u, b = (s // B) % 2, s % B
                if b == 0:
                    pe.wait_ge(w_lo_ready[u], n + 1)
                pe.wait_ge(x_loaded[b], 32)
                for m in range(CK):
                    pe.wait_ge(a_full, g * CK + m + 1)
                    for k in range(HC):
                        cols = slice(k * CH + m * P, k * CH + (m + 1) * P)
                        last = mm3(pe, up_bank[m][:, :], w_hi[:, u, cols], w_lo[:, u, cols],
                                   x_hi[:, k, b, 1:S + 1], x_lo[:, k, b, 1:S + 1], k == 0, k == HC - 1)
                    last.then_inc(up_done, 1)

            def down(g, s):
                u = s // B
                pe.wait_ge(a_lo_ready, g * CK + 2 * CK)
                for j in range(TT):
                    pe.wait_ge(y_free, g * TT + 3 * TT + j + 1)
                    for m in range(CK):
                        cols = slice(j * P, (j + 1) * P)
                        rws = slice(WD + m * H, WD + (m + 1) * H)
                        last = mm3(pe, y_bank[j][:, :], a_hi[:, s % 2, m, cols], a_lo[:, s % 2, m, cols],
                                   w_hi[:, u, rws], w_lo[:, u, rws], m == 0, m == CK - 1)
                    last.then_inc(y_done, 1)

            def turn(it, last):
                for s in range(STEPS):
                    if not (last and s == STEPS - 1):
                        up(it * STEPS + s + 1, s + 1, it + (s + 1) // STEPS)
                    down(it * STEPS + s, s)

            route.on_pe(pe)
            pe.wait_ge(zeroed, 3)
            up(0, 0, 0)
            with pe.Fori(0, TURNS - 1) as it:
                turn(it, False)
            turn(TURNS - 1, True)


class Router:

    def __init__(self, nc, ctx, rank_bank, total_bank, routing):
        def sb(nm, shape, dt=F32):
            return ctx.enter_context(nc.sbuf_tensor("rt_" + nm, shape, dt))

        def sem(nm):
            return ctx.enter_context(nc.semaphore("rt_" + nm))

        self.slots, self.experts, self.weights = routing
        self.rank_bank, self.total_bank = rank_bank, total_bank
        self.raw = sb("raw", [P, B, ROUTE])
        self.rows_in = self.raw[:, :, :]
        self.now = sb("now", [P, 2, TT], mybir.dt.int32)
        self.before = sb("before", [P, P], BF16)
        self.ones = sb("ones", [P, P], BF16)
        self.member = sb("member", [P, T_ALL, E], BF16)
        self.total = sb("total", [P, T_ALL, E])
        self.upto = sb("upto", [P, T_ALL, E])
        self.slot = sb("slot", [P, T_ALL, E])
        self.one = sb("one", [P, TILES])
        self.limits = sb("limits", [P, MAX_TILES])
        self.numbers = sb("numbers", [P, TILES])
        self.over = sb("over", [P, E, MAX_TILES])
        self.n_tiles = sb("n_tiles", [P, E])
        self.tile_end = sb("tile_end", [P, E])
        self.first_slot = sb("first_slot", [P, E])
        self.picked = sb("picked", [P, 2, T_ALL, E])
        self.slot_f = sb("slot_f", [P, 2, T_ALL])
        self.past = sb("past", [P, TILES, E])
        self.expert_f = sb("expert_f", [P, TILES])
        self.loaded = sem("loaded")
        self.consts = sem("consts")
        self.step = sem("step")
        self.member_ready = sem("member_ready")
        self.counted = sem("counted")
        self.slots_ready = sem("slots_ready")
        self.now_ready = sem("now_ready")

    def masks_on_pool(self, pool):
        pool.memset(self.ones[:, :], 1.0).then_inc(self.consts, 1)
        pool.memset(self.one[:, :], 1.0).then_inc(self.consts, 1)
        pool.iota(self.limits[:, :], [[TILE, MAX_TILES]], base=0, channel_multiplier=0,
                  allow_small_or_imprecise_dtypes=True).then_inc(self.consts, 1)
        pool.iota(self.numbers[:, :], [[1, TILES]], base=0, channel_multiplier=0,
                  allow_small_or_imprecise_dtypes=True).then_inc(self.consts, 1)
        pool.wait_ge(self.consts, 4)
        pool.affine_select(out=self.before[:, :], in_=self.ones[:, :], compare_op=ALU.is_gt, fill=0.0, base=0,
                           pattern=[[1, P]], channel_multiplier=-1).then_inc(self.consts, 1)

    def on_pe(self, pe):
        pe.wait_ge(self.consts, 5)
        pe.wait_ge(self.member_ready, 1)
        member = self.member[:, :, :].rearrange("p t e -> p (t e)")
        pe.matmul(self.rank_bank[:, 0:T_ALL * E], lhsT=self.before[:, :], rhs=member, start=True,
                  stop=True).then_inc(self.counted, 1)
        pe.matmul(self.total_bank[:, 0:T_ALL * E], lhsT=self.ones[:, :], rhs=member, start=True,
                  stop=True).then_inc(self.counted, 1)

    def on_dve(self, dve):
        steps = [0]

        def step(i):
            i.then_inc(self.step, 1)
            steps[0] += 1
            dve.wait_ge(self.step, steps[0])

        dve.wait_ge(self.loaded, 16)
        dve.wait_ge(self.consts, 5)
        onehots = [self.raw[:, :, n * TT * E:(n + 1) * TT * E].rearrange("p b (j e) -> p b j e", e=E) for n in range(2)]

        def by_seq(x):
            return x.rearrange("p (b j) e -> p b j e", b=B)

        dve.tensor_tensor(by_seq(self.member[:, :, :]), onehots[0], onehots[1], ALU.add).then_inc(self.member_ready, 1)
        for n in range(2):
            step(dve.tensor_copy(self.weights[:, n, :, :], self.raw[:, :, 2 * TT * E + n * TT:2 * TT * E + (n + 1) * TT]))
        dve.wait_ge(self.counted, 2)
        step(dve.tensor_copy(self.total[:, :, :], self.total_bank[:, 0:T_ALL * E].rearrange("p (t e) -> p t e", e=E)))
        for e in range(E):
            step(dve.tensor_tensor_scan(self.upto[:, :, e], self.one[:, 0:T_ALL], self.total[:, :, e], 0.0,
                                        ALU.mult, ALU.add))
        count = self.upto[:, T_ALL - 1, :]
        step(dve.tensor_tensor(self.over[:, :, :], count.unsqueeze(2).to_broadcast([P, E, MAX_TILES]),
                               self.limits[:, :].unsqueeze(1).to_broadcast([P, E, MAX_TILES]), ALU.is_gt))
        step(dve.tensor_reduce(self.n_tiles[:, :], self.over[:, :, :], AX.X, ALU.add))
        step(dve.tensor_tensor_scan(self.tile_end[:, :], self.one[:, 0:E], self.n_tiles[:, :], 0.0, ALU.mult, ALU.add))
        step(dve.tensor_tensor(self.first_slot[:, :], self.tile_end[:, :], self.n_tiles[:, :], ALU.subtract))
        step(dve.tensor_scalar(self.first_slot[:, :], self.first_slot[:, :], float(TILE), None, ALU.mult))
        step(dve.tensor_tensor(self.upto[:, :, :], self.upto[:, :, :], self.total[:, :, :], ALU.subtract))
        step(dve.tensor_tensor(self.slot[:, :, :], self.upto[:, :, :],
                               self.first_slot[:, :].unsqueeze(1).to_broadcast([P, T_ALL, E]), ALU.add))
        step(dve.tensor_tensor(self.slot[:, :, :], self.slot[:, :, :],
                               self.rank_bank[:, 0:T_ALL * E].rearrange("p (t e) -> p t e", e=E), ALU.add))
        for n in range(2):
            step(dve.tensor_tensor(by_seq(self.picked[:, n, :, :]), by_seq(self.slot[:, :, :]), onehots[n], ALU.mult))
            step(dve.tensor_reduce(self.slot_f[:, n, :], self.picked[:, n, :, :], AX.X, ALU.add))
        for n in range(2):
            dve.tensor_copy(self.slots[:, n, :, :],
                            self.slot_f[:, n, :].rearrange("p (b j) -> p b j", b=B)).then_inc(self.slots_ready, 1)
        step(dve.tensor_tensor(self.past[:, :, :], self.numbers[:, :].unsqueeze(2).to_broadcast([P, TILES, E]),
                               self.tile_end[:, :].unsqueeze(1).to_broadcast([P, TILES, E]), ALU.is_ge))
        step(dve.tensor_reduce(self.expert_f[:, :], self.past[:, :, :], AX.X, ALU.add))
        step(dve.tensor_scalar(self.experts[:, :], self.expert_f[:, :], float(E - 1), None, ALU.min))


def experts_phase(nc, psum, ident, routing, d):
    C = CHUNKS_E
    WU, WD = HC * CH, 2 * HC * CH
    WW = WD + CK * H
    STAGES = C
    G = TILES * C
    TURNS = TILES // 2
    assert TILES % 2 == 1
    experts = routing[1]

    with ExitStack() as ctx:
        def sb(nm, shape, dt=F32):
            return ctx.enter_context(nc.sbuf_tensor("ex_" + nm, shape, dt))

        def sem(nm):
            return ctx.enter_context(nc.semaphore("ex_" + nm))

        gain = sb("gain", [P, 8, HC])
        x_in = sb("x_in", [P, 2, TP, H])
        x_hi = sb("x_hi", [P, 2, HC, TILE], F32R)
        x_lo = sb("x_lo", [P, 2, HC, TILE], F32R)
        stage = sb("stage", [P, STAGES, WW])
        w_hi = sb("w_hi", [P, 2, WW], F32R)
        w_lo = sb("w_lo", [P, 2, WW], F32R)
        gate = sb("gate", [P, CK, TILE])
        a = sb("a", [P, CK, TILE])
        a_hi = sb("a_hi", [P, 2, CK, TILE], F32R)
        a_lo = sb("a_lo", [P, 2, CK, TILE], F32R)
        y = sb("y", [P, 2, TP, H])
        spare = sb("spare", [P, 16])

        gain_in = sem("gain_in")
        stage_in = [sem(f"stage_in{c}") for c in range(STAGES)]
        x_loaded = [sem(f"x_loaded{p}") for p in range(2)]
        wu_hi_ready = sem("wu_hi_ready")
        wu_lo_ready = sem("wu_lo_ready")
        wd_hi_ready = sem("wd_hi_ready")
        wd_lo_ready = sem("wd_lo_ready")
        turned = sem("turned")
        x_hi_ready = sem("x_hi_ready")
        x_lo_ready = sem("x_lo_ready")
        up_done = sem("up_done")
        gate_ready = sem("gate_ready")
        a_full = sem("a_full")
        a_hi_ready = sem("a_hi_ready")
        a_lo_ready = sem("a_lo_ready")
        down_done = sem("down_done")
        y_by_act = sem("y_by_act")
        y_by_dve = sem("y_by_dve")
        y_out = [sem(f"y_out{p}") for p in range(2)]
        up_bank = psum[0:CK]
        turn_bank = psum[2:4]
        UP, DOWN = slice(0, WD), slice(WD, WW)

        def y_bank(p, j):
            return psum[4 + p * TP + j]

        rows = "(j p) h -> p j h"
        block = ctx.enter_context(nc.Block())

        def slots(it, last):
            for s in range(C if last else 2 * C):
                yield it * 2 * C + s, it * 2 + s // C, s // C, s % C

        @block.sync
        def _(sp):
            def tile(n, p):
                sp.wait_ge(turned, n + 1)
                sp.dma_start(x_in[:, p, :, :],
                             d["tiles_in"][bass.ds(n * TILE, TILE), :].rearrange(rows, p=P)).then_inc(x_loaded[p], 16)
                e = sp.value_load(experts[0:1, bass.ds(n, 1)], min_val=0, max_val=E - 1)
                for c in range(C):
                    sp.wait_ge(wd_lo_ready, n * C + c + 1)
                    sp.dma_start(stage[:, c, :], d["w_moe"][e * C + c]).then_inc(stage_in[c], 16)

            sp.dma_start(gain[:, :, :], d["vecs"]).then_inc(gain_in, 16)
            with sp.Fori(0, TURNS) as it:
                for p in range(2):
                    tile(it * 2 + p, p)
            tile(TILES - 1, 0)

        @block.gpsimd
        def _(pool):
            def low(g, s):
                for m in range(CK):
                    pool.wait_ge(a_hi_ready, g * CK + m + 1)
                    pool.tensor_tensor(a_lo[:, s % 2, m, :], a[:, m, :], a_hi[:, s % 2, m, :].bitcast(F32),
                                       ALU.subtract).then_inc(a_lo_ready, 1)

            def turn(it, last):
                for g, n, p, c in slots(it, last):
                    if not (last and c == C - 1):
                        low(g + 1, c + 1)

            low(0, 0)
            with pool.Fori(0, TURNS) as it:
                turn(it, False)
            turn(TURNS, True)

        @block.scalar
        def _(act):
            def split_up(g, n, c):
                act.wait_ge(stage_in[c], n * 16 + 16)
                act.activation(w_hi[:, c % 2, UP], stage[:, c, UP], ACT.Copy).then_inc(wu_hi_ready, 1)

            def split_down(g, c):
                act.activation(w_hi[:, c % 2, DOWN], stage[:, c, DOWN], ACT.Copy).then_inc(wd_hi_ready, 1)

            def split_x(n, p):
                act.wait_ge(turned, n + 3)
                for k in range(HC):
                    act.activation(x_hi[:, p, k, :], turn_bank[k // 2][:, k % 2 * TILE:(k % 2 + 1) * TILE], ACT.Copy,
                                   scale=gain[:, V_W2, k:k + 1]).then_inc(x_hi_ready, 1)

            def up(g, s, first):
                for m in range(CK):
                    act.wait_ge(up_done, g * CK + m + 1)
                    act.wait_ge(a_full, g * CK + m + 1)
                    act.activation(gate[:, m, :], up_bank[m][:, 0:TILE], ACT.Silu).then_inc(gate_ready, 1)
                for m in range(CK):
                    act.wait_ge(a_full, g * CK + CK + m + 1)
                    if m == 0 and not first:
                        act.wait_ge(down_done, g)
                    act.activation(a_hi[:, s % 2, m, :], a[:, m, :], ACT.Copy).then_inc(a_hi_ready, 1)

            def turn(it, last):
                for g, n, p, c in slots(it, last):
                    if not (last and c >= C - 2):
                        act.wait_ge(up_done, g * CK + CK)
                        split_up(g + 2, n + (c + 2) // C, (c + 2) % C)
                    if not (last and c == C - 1):
                        act.wait_ge(down_done, g + 1)
                        split_down(g + 1, (c + 1) % C)
                    if c == 1 and not last:
                        split_x(n + 1, 1 - p)
                    if not (last and c == C - 1):
                        up(g + 1, c + 1, False)
                    if c == C - 1:
                        act.wait_ge(down_done, g + 2)
                        act.wait_ge(y_out[p], it * 16 + 16)
                        act.activation(y[:, p, 0, :], y_bank(p, 0)[:, :], ACT.Copy).then_inc(y_by_act, 1)
                        act.wait_ge(y_by_act, n + 3)
                        act.wait_ge(y_by_dve, n + 3)
                        act.dma_start(d["tiles_out"][bass.ds(n * TILE, TILE), :].rearrange(rows, p=P),
                                      y[:, p, :, :]).then_inc(y_out[p], 16)

            act.wait_ge(gain_in, 16)
            split_x(0, 0)
            split_up(0, 0, 0)
            split_down(0, 0)
            split_up(1, 0, 1)
            up(0, 0, True)
            with act.Fori(0, TURNS) as it:
                turn(it, False)
            turn(TURNS, True)
            act.wait_ge(y_out[0], 16 * (TURNS + 2))
            act.wait_ge(y_out[1], 16 * (TURNS + 1))

        @block.vector
        def _(dve):
            def low(dst, src, hi):
                return dve.tensor_tensor(dst, src, hi.bitcast(F32), ALU.subtract)

            def split_up(g, c):
                dve.wait_ge(wu_hi_ready, g + 1)
                low(w_lo[:, c % 2, UP], stage[:, c, UP], w_hi[:, c % 2, UP]).then_inc(wu_lo_ready, 1)

            def split_down(g, c):
                dve.wait_ge(wd_hi_ready, g + 1)
                low(w_lo[:, c % 2, DOWN], stage[:, c, DOWN], w_hi[:, c % 2, DOWN]).then_inc(wd_lo_ready, 1)

            def split_x(n, p):
                for k in range(HC):
                    dve.wait_ge(x_hi_ready, n * HC + (k // 2) * 2 + 2)
                    dve.scalar_tensor_tensor(x_lo[:, p, k, :], turn_bank[k // 2][:, k % 2 * TILE:(k % 2 + 1) * TILE],
                                             gain[:, V_W2, k:k + 1], x_hi[:, p, k, :].bitcast(F32),
                                             ALU.mult, ALU.subtract).then_inc(x_lo_ready, 1)

            def product(g):
                for m in range(CK):
                    dve.wait_ge(gate_ready, g * CK + m + 1)
                    dve.wait_ge(a_lo_ready, g * CK + m + 1)
                    dve.tensor_tensor(a[:, m, :], gate[:, m, :], up_bank[m][:, TILE:2 * TILE],
                                      ALU.mult).then_inc(a_full, 1)

            def turn(it, last):
                for g, n, p, c in slots(it, last):
                    if not (last and c >= C - 2):
                        split_up(g + 2, (c + 2) % C)
                    if not (last and c == C - 1):
                        split_down(g + 1, (c + 1) % C)
                    if c == 1 and not last:
                        split_x(n + 1, 1 - p)
                    if not (last and c == C - 1):
                        product(g + 1)
                    if c == C - 1:
                        dve.wait_ge(down_done, g + 2)
                        dve.wait_ge(y_out[p], it * 16 + 16)
                        dve.tensor_copy(y[:, p, 1, :], y_bank(p, 1)[:, :]).then_inc(y_by_dve, 1)

            for i, (sm, n) in enumerate(((down_done, 1), (wd_lo_ready, STAGES), (a_full, CK), (a_lo_ready, CK),
                                         (turned, 2), (y_by_act, 2), (y_by_dve, 2), (y_out[0], 16),
                                         (y_out[1], 16))):
                dve.memset(spare[:, i:i + 1], 0.0).then_inc(sm, n)
            dve.wait_ge(gain_in, 16)
            split_x(0, 0)
            split_up(0, 0)
            split_down(0, 0)
            split_up(1, 1)
            product(0)
            with dve.Fori(0, TURNS) as it:
                turn(it, False)
            turn(TURNS, True)

        @block.tensor
        def _(pe):
            def turn_x(n, p, load, first):
                pe.wait_ge(x_loaded[p], load * 16 + 16)
                if not first:
                    pe.wait_ge(x_lo_ready, n * HC)
                for k in range(HC):
                    for j in range(TP):
                        at = k % 2 * TILE + j * P
                        i = pe.transpose(turn_bank[k // 2][:, at:at + P], x_in[:, p, j, k * P:(k + 1) * P], ident)
                i.then_inc(turned, 1)

            def up(g, n, p, c):
                pe.wait_ge(wu_lo_ready, g + 1)
                if c == 0:
                    pe.wait_ge(x_lo_ready, n * HC + HC)
                for m in range(CK):
                    pe.wait_ge(a_full, g * CK + m + 1)
                    for half, w0 in enumerate((0, WU)):
                        for k in range(HC):
                            cols = slice(w0 + k * CH + m * P, w0 + k * CH + (m + 1) * P)
                            last = mm3(pe, up_bank[m][:, half * TILE:(half + 1) * TILE], w_hi[:, c % 2, cols],
                                       w_lo[:, c % 2, cols], x_hi[:, p, k, :], x_lo[:, p, k, :], k == 0, k == HC - 1)
                    last.then_inc(up_done, 1)

            def down(g, n, p, c):
                pe.wait_ge(wd_lo_ready, g + STAGES + 1)
                pe.wait_ge(a_lo_ready, g * CK + 2 * CK)
                if c == 0:
                    pe.wait_ge(y_by_act, n + 1)
                    pe.wait_ge(y_by_dve, n + 1)
                for j in range(TP):
                    for m in range(CK):
                        cols = slice(j * P, (j + 1) * P)
                        wrows = slice(WD + m * H, WD + (m + 1) * H)
                        last = mm3(pe, y_bank(p, j)[:, :], a_hi[:, c % 2, m, cols], a_lo[:, c % 2, m, cols],
                                   w_hi[:, c % 2, wrows], w_lo[:, c % 2, wrows], c == 0 and m == 0,
                                   c == C - 1 and m == CK - 1)
                last.then_inc(down_done, 1)

            def turn(it, last):
                for g, n, p, c in slots(it, last):
                    if c < C - 1:
                        up(g + 1, n, p, c + 1)
                    elif not last:
                        up(g + 1, n + 1, 1 - p, 0)
                    down(g, n, p, c)
                    if c == 1 and not last:
                        turn_x(n + 1, 1 - p, it + p, False)

            turn_x(0, 0, 0, True)
            up(0, 0, 0, 0)
            with pe.Fori(0, TURNS) as it:
                turn(it, False)
            turn(TURNS, True)


def combine_phase(nc, routing, d):
    slots, _, weights = routing
    tokens = "(j p) h -> p j h"
    with ExitStack() as ctx:
        def sb(nm, shape, dt=F32):
            return ctx.enter_context(nc.sbuf_tensor("co_" + nm, shape, dt))

        def sem(nm):
            return ctx.enter_context(nc.semaphore("co_" + nm))

        pre = sb("pre", [P, T_ALL, H])
        y = sb("y", [P, T_ALL, 2, H])
        pre_in = [sem(f"pre_in{b}") for b in range(B)]
        y_in = [sem(f"y_in{b}") for b in range(B)]
        added = sem("added")
        out_done = sem("out_done")
        block = ctx.enter_context(nc.Block())

        @block.sync
        def _(sp):
            for b in range(B):
                sp.dma_start(pre[:, b * TT:(b + 1) * TT, :],
                             d["pre2"][b].rearrange(tokens, p=P)).then_inc(pre_in[b], 16)
            for b in range(B):
                sp.wait_ge(added, 2 * TT * (b + 1))
                sp.dma_start(d["out"][b].rearrange(tokens, p=P),
                             pre[:, b * TT:(b + 1) * TT, :]).then_inc(out_done, 16)
            sp.wait_ge(out_done, 16 * B)

        @block.gpsimd
        def _(pool):
            for b in range(B):
                for j in range(TT):
                    for n in range(2):
                        pool.indirect_dma_start(
                            out=y[:, b * TT + j, n, :], out_offset=None, in_=d["tiles_out"],
                            in_offset=bass.IndirectOffsetOnAxis(ap=slots[:, n, b, j:j + 1], axis=0)
                        ).then_inc(y_in[b], 16)

        @block.vector
        def _(dve):
            for b in range(B):
                dve.wait_ge(pre_in[b], 16)
                dve.wait_ge(y_in[b], 16 * 2 * TT)
                for n in range(2):
                    for j in range(TT):
                        t = b * TT + j
                        if n:
                            dve.wait_ge(added, b * 2 * TT + j + 1)
                        dve.scalar_tensor_tensor(pre[:, t, :], y[:, t, n, :], weights[:, n, b, j:j + 1], pre[:, t, :],
                                                 ALU.mult, ALU.add).then_inc(added, 1)


def attention_phase(nc, psum, ident, ident_bf, causal, d):
    N_W = 4
    S_AT = {3: (0, 0), 2: (1, 0), 0: (1, 3 * P), 1: (2, 0)}
    PT_AT = {0: (0, 0), 1: (1, 0), 3: (1, 3 * P), 2: (2, 0)}
    PT_COLS = 512 + 512 + 256

    with ExitStack() as ctx:
        def sb(name, shape, dt=F32):
            return ctx.enter_context(nc.sbuf_tensor("at_" + name, shape, dt))

        def sem(name):
            return ctx.enter_context(nc.semaphore("at_" + name))

        w_stage = sb("w_stage", [P, 2, HC * H])
        w_hi = sb("w_hi", [P, N_W, HC, H], F32R)
        w_lo = sb("w_lo", [P, N_W, HC, H], F32R)
        wr = sb("wr", [P, HC, E])
        vecs = sb("vecs", [P, 8, HC])
        prefer = sb("prefer", [P, E])
        xn = sb("xn", [P, TT, H])
        t = sb("t", [P, TT, H])
        xT = sb("xT", [P, HC, S])
        x_hi = sb("x_hi", [P, HC, S], F32R)
        x_lo = sb("x_lo", [P, HC, S], F32R)
        qT = sb("qT", [P, HC, S])
        kT = sb("kT", [P, HC, S])
        v = sb("v", [P, TT, H])
        probs = sb("probs", [P, 2, TT, S])
        pT = sb("pT", [P, 2, PT_COLS])
        xp = sb("xp", [P, TT, H])
        base = sb("base", [P, TT, H])
        sq = sb("sq", [P, TT])
        mean_sq = sb("mean_sq", [P, TT])
        spare = sb("spare", [P, 8])
        minus_half = sb("minus_half", [P, TT])
        rstd = sb("rstd", [P, TT])
        row_max = sb("row_max", [P, HEADS, TT])
        bias = sb("bias", [P, HEADS, TT])
        row_sum = sb("row_sum", [P, HEADS, TT])
        row_rec = sb("row_rec", [P, HEADS, TT])
        logits = sb("logits", [P, TT, E])
        left = sb("left", [P, TT, E])
        hit = sb("hit", [P, TT, E])
        top = sb("top", [P, 2, TT])
        pick = sb("pick", [P, TT])
        gap = sb("gap", [P, TT])
        odds = sb("odds", [P, TT])
        odds1 = sb("odds1", [P, TT])
        routes = sb("routes", [P, ROUTE])
        first = routes[:, 0:TT * E].rearrange("p (j e) -> p j e", e=E)
        second = routes[:, TT * E:2 * TT * E].rearrange("p (j e) -> p j e", e=E)
        p1 = routes[:, 2 * TT * E:2 * TT * E + TT]
        p2 = routes[:, 2 * TT * E + TT:ROUTE]

        const_in = sem("const_in")
        w_in = [sem(f"w_in{n}") for n in range(N_W)]
        w_hi_ready = sem("w_hi_ready")
        w_lo_ready = sem("w_lo_ready")
        prefer_ready = sem("prefer_ready")
        xn_loaded = sem("xn_loaded")
        res_loaded = sem("res_loaded")
        sq_ready = sem("sq_ready")
        mean_sq_ready = sem("mean_sq_ready")
        half_ready = sem("half_ready")
        rstd_ready = sem("rstd_ready")
        norm_ready = sem("norm_ready")
        turned = sem("turned")
        xT_ready = sem("xT_ready")
        x_hi_ready = sem("x_hi_ready")
        x_lo_ready = sem("x_lo_ready")
        q_done = sem("q_done")
        k_done = sem("k_done")
        v_done = sem("v_done")
        q_ready = sem("q_ready")
        k_ready = sem("k_ready")
        v_ready = sem("v_ready")
        scores_done = sem("scores_done")
        max_step = sem("max_step")
        bias_ready = sem("bias_ready")
        exp_ready = sem("exp_ready")
        probs_turned = sem("probs_turned")
        pT_by_act = sem("pT_by_act")
        pT_by_dve = sem("pT_by_dve")
        heads_done = sem("heads_done")
        rec_ready = sem("rec_ready")
        o_ready = sem("o_ready")
        proj_done = sem("proj_done")
        xp_ready = sem("xp_ready")
        logits_done = sem("logits_done")
        route = sem("route")
        gap_ready = sem("gap_ready")
        odds_ready = sem("odds_ready")
        routes_ready = sem("routes_ready")
        pre_ready = sem("pre_ready")
        x2_out = sem("x2_out")
        route_out = sem("route_out")
        pre_out = sem("pre_out")

        tokens = "(j p) h -> p j h"
        block = ctx.enter_context(nc.Block())

        @block.sync
        def _(sp):
            sp.dma_start(vecs[:, :, :], d["vecs"]).then_inc(const_in, 16)
            sp.dma_start(wr[:, :, :], d["w_r"]).then_inc(const_in, 16)
            for n in range(N_W):
                if n >= 2:
                    sp.wait_ge(w_lo_ready, n - 1)
                sp.dma_start(w_stage[:, n % 2, :], d["w_at"][n]).then_inc(w_in[n], 16)
            with sp.Fori(0, B) as b:
                sp.dma_start(xn[:, :, :], d["xn"][b].rearrange(tokens, p=P)).then_inc(xn_loaded, 16)
                sp.wait_ge(pre_out, b * 16 + 16)
                sp.dma_start(base[:, :, :], d["base"][b].rearrange(tokens, p=P)).then_inc(res_loaded, 16)
                sp.wait_ge(norm_ready, b * 2 * TT + 2 * TT)
                sp.dma_start(d["x2"][b].rearrange(tokens, p=P), t[:, :, :]).then_inc(x2_out, 16)
                sp.wait_ge(pre_ready, b + 1)
                sp.dma_start(d["pre"][b].rearrange(tokens, p=P), base[:, :, :]).then_inc(pre_out, 16)
                sp.wait_ge(routes_ready, b + 1)
                sp.dma_start(d["route"][b], routes[:, :]).then_inc(route_out, 16)
            sp.wait_ge(x2_out, 16 * (B + 1))
            sp.wait_ge(pre_out, 16 * (B + 1))
            sp.wait_ge(route_out, 16 * (B + 1))

        @block.gpsimd
        def _(pool):
            pool.iota(prefer[:, :], [[-1, E]], base=E, channel_multiplier=0,
                      allow_small_or_imprecise_dtypes=True).then_inc(prefer_ready, 1)
            pool.memset(spare[:, 0:1], 0.0).then_inc(x2_out, 16)
            pool.memset(spare[:, 1:2], 0.0).then_inc(pre_out, 16)
            pool.memset(spare[:, 2:3], 0.0).then_inc(route_out, 16)
            for n in range(N_W):
                pool.wait_ge(w_hi_ready, n + 1)
                pool.tensor_tensor(w_lo[:, n, :, :].rearrange("p k n -> p (k n)"), w_stage[:, n % 2, :],
                                   w_hi[:, n, :, :].rearrange("p k n -> p (k n)").bitcast(F32),
                                   ALU.subtract).then_inc(w_lo_ready, 1)

            def low(b, turn):
                for c in range(HC):
                    pool.wait_ge(x_hi_ready, b * 2 * HC + turn * HC + c + 1)
                    pool.tensor_tensor(x_lo[:, c, :], xT[:, c, :], x_hi[:, c, :].bitcast(F32),
                                       ALU.subtract).then_inc(x_lo_ready, 1)

            pool.memset(minus_half[:, :], -0.5).then_inc(half_ready, 1)
            pool.wait_ge(half_ready, 1)

            def inverse_root(turn):
                pool.wait_ge(mean_sq_ready, turn + 1)
                pool.tensor_tensor(rstd[:, :], mean_sq[:, :], minus_half[:, :], ALU.pow).then_inc(rstd_ready, 1)

            with pool.Fori(0, B) as b:
                inverse_root(b * 2)
                low(b, 0)
                low(b, 1)
                inverse_root(b * 2 + 1)
                pool.wait_ge(res_loaded, b * 16 + 16)
                pool.wait_ge(xp_ready, b * TT + TT)
                pool.tensor_tensor(base[:, :, :], base[:, :, :], xp[:, :, :], ALU.add).then_inc(pre_ready, 1)

        @block.scalar
        def _(act):
            for n in range(N_W):
                act.wait_ge(w_in[n], 16)
                act.activation(w_hi[:, n, :, :].rearrange("p k n -> p (k n)"), w_stage[:, n % 2, :],
                               ACT.Copy).then_inc(w_hi_ready, 1)
            act.wait_ge(const_in, 32)

            def squares(src, b, turn):
                for j in range(TT):
                    if turn:
                        act.wait_ge(xp_ready, b * TT + j + 1)
                    act.activation(t[:, j, :], src[:, j, :], ACT.Square,
                                   accum_out=sq[:, j:j + 1]).then_inc(sq_ready, 1)

            def scaled(src, b, turn):
                act.wait_ge(rstd_ready, b * 2 + turn + 1)
                for j in range(TT):
                    act.activation(t[:, j, :], src[:, j, :], ACT.Copy,
                                   scale=rstd[:, j:j + 1]).then_inc(norm_ready, 1)

            def split_turned(b, turn, gain):
                for c in range(HC):
                    act.wait_ge(turned, b * 3 * HC + turn * HC + c + 1)
                    scale = 1.0 if gain is None else vecs[:, gain, c:c + 1]
                    act.activation(xT[:, c, :], psum[c][:, :], ACT.Copy, scale=scale).then_inc(xT_ready, 1)
                    if turn < 2:
                        act.activation(x_hi[:, c, :], psum[c][:, :], ACT.Copy, scale=scale).then_inc(x_hi_ready, 1)

            def exps(b, h):
                act.wait_ge(bias_ready, b * HEADS + h + 1)
                if h >= 2:
                    act.wait_ge(probs_turned, b * HEADS + h - 1)
                for j in range(TT):
                    bank, col = S_AT[j]
                    n = (j + 1) * P
                    act.activation(probs[:, h % 2, j, 0:n], psum[3 * (h % 2) + bank][:, col:col + n], ACT.Exp,
                                   bias=bias[:, h, j:j + 1], scale=QK_SCALE,
                                   accum_out=row_sum[:, h, j:j + 1]).then_inc(exp_ready, 1)

            with act.Fori(0, B) as b:
                act.wait_ge(xn_loaded, b * 16 + 16)
                act.wait_ge(x2_out, b * 16 + 16)
                squares(xn, b, 0)
                scaled(xn, b, 0)
                split_turned(b, 0, V_W1)
                for m in range(HC):
                    act.wait_ge(k_done, b * HC + m + 1)
                    act.activation(kT[:, m, :], psum[m][:, :], ACT.Copy).then_inc(k_ready, 1)
                exps(b, 0)
                for h in range(HEADS):
                    act.wait_ge(probs_turned, b * HEADS + h + 1)
                    if h >= 2:
                        act.wait_ge(heads_done, b * HEADS + h - 1)
                    act.activation(pT[:, h % 2, 0:S], psum[3 * (h % 2)][:, :], ACT.Copy).then_inc(pT_by_act, 1)
                    if h + 1 < HEADS:
                        exps(b, h + 1)
                split_turned(b, 1, None)
                squares(xp, b, 1)
                scaled(xp, b, 1)
                split_turned(b, 2, V_W2)
                act.wait_ge(gap_ready, b + 1)
                act.activation(odds[:, :], gap[:, :], ACT.Exp).then_inc(odds_ready, 1)

        @block.vector
        def _(dve):
            dve.wait_ge(prefer_ready, 1)

            def inverse_rms(b, turn):
                dve.wait_ge(sq_ready, b * 2 * TT + turn * TT + TT)
                dve.tensor_scalar(mean_sq[:, :], sq[:, :], 1.0 / H, RMS_EPS, ALU.mult, ALU.add).then_inc(mean_sq_ready, 1)

            def maxima(b, h):
                dve.wait_ge(scores_done, b * HEADS + h + 1)
                for j in range(TT):
                    bank, col = S_AT[j]
                    dve.tensor_reduce(row_max[:, h, j:j + 1], psum[3 * (h % 2) + bank][:, col:col + (j + 1) * P],
                                      AX.X, ALU.max).then_inc(max_step, 1)
                dve.wait_ge(max_step, b * HEADS * TT + h * TT + TT)
                dve.tensor_scalar(bias[:, h, :], row_max[:, h, :], -QK_SCALE, None, ALU.mult).then_inc(bias_ready, 1)

            def outputs(b, h):
                dve.wait_ge(exp_ready, b * HEADS * TT + h * TT + TT)
                dve.reciprocal(row_rec[:, h, :], row_sum[:, h, :]).then_inc(rec_ready, 1)
                dve.wait_ge(rec_ready, b * HEADS + h + 1)
                dve.wait_ge(heads_done, b * HEADS + h + 1)
                dve.tensor_tensor(t[:, :, h * HD:(h + 1) * HD],
                                  psum[6 + h % 2][:, 0:TT * HD].rearrange("p (j n) -> p j n", j=TT),
                                  row_rec[:, h, :].unsqueeze(2).to_broadcast([P, TT, HD]),
                                  ALU.mult).then_inc(o_ready, 1)

            def per_tile(x):
                return x.unsqueeze(2).to_broadcast([P, TT, E])

            def routing(b):
                steps = [0]

                def step(i):
                    i.then_inc(route, 1)
                    steps[0] += 1
                    dve.wait_ge(route, b * 14 + steps[0])

                def one_hot(dst, src, n):
                    step(dve.tensor_reduce(top[:, n, :], src[:, :, :], AX.X, ALU.max))
                    step(dve.tensor_tensor(hit[:, :, :], src[:, :, :], per_tile(top[:, n, :]), ALU.is_equal))
                    step(dve.tensor_tensor(hit[:, :, :], hit[:, :, :],
                                           prefer[:, :].unsqueeze(1).to_broadcast([P, TT, E]), ALU.mult))
                    step(dve.tensor_reduce(pick[:, :], hit[:, :, :], AX.X, ALU.max))
                    step(dve.tensor_tensor(dst, hit[:, :, :], per_tile(pick[:, :]), ALU.is_equal))

                dve.wait_ge(logits_done, b + 1)
                dve.wait_ge(route_out, b * 16 + 16)
                step(dve.tensor_copy(logits[:, :, :], psum[4][:, 0:TT * E].rearrange("p (j e) -> p j e", e=E)))
                one_hot(first, logits, 0)
                step(dve.scalar_tensor_tensor(left[:, :, :], first, NEG, logits[:, :, :], ALU.mult, ALU.add))
                one_hot(second, left, 1)
                dve.tensor_tensor(gap[:, :], top[:, 1, :], top[:, 0, :], ALU.subtract).then_inc(gap_ready, 1)
                dve.wait_ge(odds_ready, b + 1)
                step(dve.tensor_scalar(odds1[:, :], odds[:, :], 1.0, None, ALU.add))
                step(dve.reciprocal(p1, odds1[:, :]))
                assert steps[0] == 14
                dve.tensor_tensor(p2, odds[:, :], p1, ALU.mult).then_inc(routes_ready, 1)

            with dve.Fori(0, B) as b:
                inverse_rms(b, 0)
                for m in range(HC):
                    dve.wait_ge(q_done, b * HC + m + 1)
                    dve.tensor_copy(qT[:, m, :], psum[4 + m][:, :]).then_inc(q_ready, 1)
                for j in range(TT):
                    dve.wait_ge(v_done, b * TT + j + 1)
                    dve.tensor_copy(v[:, j, :], psum[4 + j][:, :]).then_inc(v_ready, 1)
                maxima(b, 0)
                for h in range(HEADS):
                    if h + 1 < HEADS:
                        maxima(b, h + 1)
                    dve.wait_ge(probs_turned, b * HEADS + h + 1)
                    if h >= 2:
                        dve.wait_ge(heads_done, b * HEADS + h - 1)
                    dve.tensor_copy(pT[:, h % 2, S:2 * S], psum[3 * (h % 2) + 1][:, :]).then_inc(pT_by_dve, 1)
                    dve.tensor_copy(pT[:, h % 2, 2 * S:PT_COLS],
                                    psum[3 * (h % 2) + 2][:, 0:2 * P]).then_inc(pT_by_dve, 1)
                    if h >= 2:
                        outputs(b, h - 2)
                outputs(b, HEADS - 2)
                outputs(b, HEADS - 1)
                for j in range(TT):
                    dve.wait_ge(proj_done, b * TT + j + 1)
                    dve.tensor_tensor(xp[:, j, :], psum[4 + j][:, :], xn[:, j, :], ALU.add).then_inc(xp_ready, 1)
                inverse_rms(b, 1)
                routing(b)
                dve.wait_ge(pre_ready, b + 1)

        @block.tensor
        def _(pe):
            def turn():
                for c in range(HC):
                    for j in range(TT):
                        i = pe.transpose(psum[c][:, j * P:(j + 1) * P], t[:, j, c * P:(c + 1) * P], ident)
                    i.then_inc(turned, 1)

            def by_feature(n, bank, done):
                for m in range(HC):
                    for k in range(HC):
                        cols = slice(m * P, (m + 1) * P)
                        last = mm3(pe, psum[bank + m][:, :], w_hi[:, n, k, cols], w_lo[:, n, k, cols],
                                   x_hi[:, k, :], x_lo[:, k, :], k == 0, k == HC - 1)
                    last.then_inc(done, 1)

            def by_token(n, bank, done):
                for j in range(TT):
                    for k in range(HC):
                        cols = slice(j * P, (j + 1) * P)
                        last = mm3(pe, psum[bank + j][:, :], x_hi[:, k, cols], x_lo[:, k, cols],
                                   w_hi[:, n, k, :], w_lo[:, n, k, :], k == 0, k == HC - 1)
                    last.then_inc(done, 1)

            def scores(h):
                c, rows = h // 4, slice(h % 4 * HD, h % 4 * HD + HD)
                for j in (3, 2, 0, 1):
                    bank, col = S_AT[j]
                    out = psum[3 * (h % 2) + bank]
                    pe.matmul(out[:, col:col + (j + 1) * P], lhsT=qT[rows, c, j * P:(j + 1) * P],
                              rhs=kT[rows, c, 0:(j + 1) * P], start=True, stop=False)
                    i = pe.matmul(out[:, col + j * P:col + (j + 1) * P], lhsT=ident_bf, rhs=causal,
                                  start=False, stop=True)
                i.then_inc(scores_done, 1)

            def turn_probs(h):
                for kt in range(TT):
                    bank, col = PT_AT[kt]
                    for j in range(kt, TT):
                        at = col + (j - kt) * P
                        i = pe.transpose(psum[3 * (h % 2) + bank][:, at:at + P],
                                         probs[:, h % 2, j, kt * P:(kt + 1) * P], ident)
                i.then_inc(probs_turned, 1)

            def head_output(b, h):
                pe.wait_ge(pT_by_act, b * HEADS + h + 1)
                pe.wait_ge(pT_by_dve, b * 2 * HEADS + 2 * h + 2)
                if h >= 2:
                    pe.wait_ge(o_ready, b * HEADS + h - 1)
                for j in range(TT):
                    for kt in range(j + 1):
                        bank, col = PT_AT[kt]
                        at = bank * S + col + (j - kt) * P
                        i = pe.matmul(psum[6 + h % 2][:, j * HD:(j + 1) * HD], lhsT=pT[:, h % 2, at:at + P],
                                      rhs=v[:, kt, h * HD:(h + 1) * HD], start=(kt == 0), stop=(kt == j))
                i.then_inc(heads_done, 1)

            pe.wait_ge(w_lo_ready, N_W)
            pe.wait_ge(const_in, 32)
            with pe.Fori(0, B) as b:
                pe.wait_ge(norm_ready, b * 2 * TT + TT)
                turn()
                pe.wait_ge(x_lo_ready, b * 2 * HC + HC)
                pe.wait_ge(route_out, b * 16 + 16)
                by_feature(0, 4, q_done)
                by_feature(1, 0, k_done)
                pe.wait_ge(q_ready, b * HC + HC)
                by_token(2, 4, v_done)
                pe.wait_ge(k_ready, b * HC + HC)
                scores(0)
                pe.wait_ge(v_ready, b * TT + TT)
                for h in range(HEADS):
                    if h >= 2:
                        head_output(b, h - 2)
                    if h + 1 < HEADS:
                        if h >= 1:
                            pe.wait_ge(pT_by_act, b * HEADS + h)
                            pe.wait_ge(pT_by_dve, b * 2 * HEADS + 2 * h)
                        scores(h + 1)
                    pe.wait_ge(exp_ready, b * HEADS * TT + h * TT + TT)
                    turn_probs(h)
                head_output(b, HEADS - 2)
                head_output(b, HEADS - 1)
                pe.wait_ge(o_ready, b * HEADS + HEADS)
                turn()
                pe.wait_ge(x_lo_ready, b * 2 * HC + 2 * HC)
                by_token(3, 4, proj_done)
                pe.wait_ge(norm_ready, b * 2 * TT + 2 * TT)
                turn()
                pe.wait_ge(xT_ready, b * 3 * HC + 3 * HC)
                for j in range(TT):
                    for k in range(HC):
                        i = pe.matmul(psum[4][:, j * E:(j + 1) * E], lhsT=xT[:, k, j * P:(j + 1) * P],
                                      rhs=wr[:, k, :], start=(k == 0), stop=(k == HC - 1))
                i.then_inc(logits_done, 1)


def constants(nc, ident, ident_bf, causal, d):
    with ExitStack() as ctx:
        filled = ctx.enter_context(nc.semaphore("c_filled"))
        cleared = ctx.enter_context(nc.semaphore("c_cleared"))
        zeros = ctx.enter_context(nc.sbuf_tensor("c_zeros", [P, TILE * H // P], F32))
        block = ctx.enter_context(nc.Block())

        @block.gpsimd
        def _(pool):
            pool.memset(ident[:, :], 0.0).then_inc(filled, 1)
            pool.memset(ident_bf[:, :], 0.0).then_inc(filled, 1)
            pool.memset(causal[:, :], 0.0).then_inc(filled, 1)
            pool.memset(zeros[:, :], 0.0).then_inc(filled, 1)
            pool.wait_ge(filled, 4)
            for m in (ident, ident_bf):
                pool.affine_select(out=m[:, :], in_=m[:, :], compare_op=ALU.not_equal, fill=1.0, base=0,
                                   pattern=[[-1, P]], channel_multiplier=1).then_inc(filled, 1)
            pool.affine_select(out=causal[:, :], in_=causal[:, :], compare_op=ALU.is_ge, fill=NEG, base=0,
                               pattern=[[-1, P]], channel_multiplier=1).then_inc(filled, 1)
            pool.wait_ge(filled, 7)
            for n in range(TILES):
                pool.dma_start(d["tiles_in"][n * TILE:(n + 1) * TILE, :].rearrange("(p j) h -> p (j h)", p=P),
                               zeros[:, :]).then_inc(cleared, 16)
            pool.wait_ge(cleared, 16 * TILES)


def build(nc, d):
    for name, shape in (("xn", [B, S, H]), ("base", [B, S, H]), ("rc", [B, S, H]), ("pre", [B, S, H]),
                        ("pre2", [B, S, H]), ("x2", [B, S, H]), ("route", [B, P, ROUTE]),
                        ("xc_hi", [B, P, HC, S]), ("xc_lo", [B, P, HC, S]),
                        ("tiles_in", [TILES * TILE, H]), ("tiles_out", [TILES * TILE, H])):
        d[name] = nc.dram_tensor("scratch_" + name, shape, F32, kind="Internal").ap()
    with ExitStack() as ctx:
        psum = [ctx.enter_context(nc.psum_tensor(f"bank{n}", [P, 512], F32)) for n in range(8)]
        ident = ctx.enter_context(nc.sbuf_tensor("ident", [P, P], F32))
        ident_bf = ctx.enter_context(nc.sbuf_tensor("ident_bf", [P, P], BF16))
        causal = ctx.enter_context(nc.sbuf_tensor("causal", [P, P], BF16))
        routing = (ctx.enter_context(nc.sbuf_tensor("slots", [P, 2, B, TT], mybir.dt.int32)),
                   ctx.enter_context(nc.sbuf_tensor("experts", [P, TILES], mybir.dt.int32)),
                   ctx.enter_context(nc.sbuf_tensor("weights", [P, 2, B, TT], F32)))
        constants(nc, ident, ident_bf, causal, d)
        time_mix_phase(nc, psum, ident[:, :], d)
        attention_phase(nc, psum, ident[:, :], ident_bf[:, :], causal[:, :], d)
        channel_mix_phase(nc, psum, d, routing)
        experts_phase(nc, psum, ident[:, :], routing, d)
        combine_phase(nc, routing, d)


def kernel(**inputs):
    import numpy as np
    import concourse.bacc as bacc
    from concourse.bass_utils import run_bass_kernel_spmd

    g = {n.replace("L0_", ""): np.asarray(a) for n, a in inputs.items()}

    def in_tiles(w):
        k = w.shape[0] // P
        return w.reshape(k, P, -1).transpose(1, 0, 2).reshape(P, -1)

    def up_chunks(w):
        return w.reshape(HC, P, -1, CH).transpose(2, 1, 0, 3).reshape(-1, P, HC * CH)

    def down_chunks(w):
        return w.reshape(-1, CK, P, H).transpose(0, 2, 1, 3).reshape(-1, P, CK * H)

    def per_feature(v):
        return v.reshape(HC, P).T

    def experts_up(w):
        return np.concatenate([up_chunks(w[e].T) for e in range(E)])

    arrays = {
        "x": g["attn_x"],
        "w_tm": np.stack([in_tiles(g["attn_" + n]) for n in ("Wv", "Wr", "Wcr", "Wo")]),
        "w_at": np.stack([in_tiles(g["ffn_" + n].T) for n in ("Wq", "Wk", "Wv", "Wo")]),
        "w_r": g["ffn_Wr"].T.reshape(HC, P, E).transpose(1, 0, 2),
        "w_cm": np.concatenate([up_chunks(g["attn_Wck"]), down_chunks(g["attn_Wcv"])], axis=2),
        "w_moe": np.concatenate([experts_up(g["ffn_Wg"]), experts_up(g["ffn_Wu"]),
                                 np.concatenate([down_chunks(g["ffn_Wd"][e].T) for e in range(E)])], axis=2),
        "vecs": np.stack([per_feature(g[n]) for n in (
            "attn_tm_g", "attn_tm_b", "attn_time_first", "attn_time_decay", "attn_cm_g", "attn_cm_b",
            "ffn_w_ln1", "ffn_w_ln2")], axis=1),
        "rows": np.stack([g["attn_" + n] for n in ("ln1_g", "ln1_b", "ln2_g", "ln2_b", "bo")]),
    }
    arrays = {"in_" + n: np.ascontiguousarray(a) for n, a in arrays.items()}
    nc = bacc.Bacc("TRN2", target_bir_lowering=False, num_devices=1)
    d = {n[3:]: nc.dram_tensor(n, a.shape, F32, kind="ExternalInput").ap() for n, a in arrays.items()}
    d["out"] = nc.dram_tensor("out", [B, S, H], F32, kind="ExternalOutput").ap()
    build(nc, d)
    r = run_bass_kernel_spmd(nc, [arrays], core_ids=[0])
    return r.results[0]["out"]
```

```python
from contextlib import ExitStack

import concourse.bass as bass
from concourse import mybir

F32 = mybir.dt.float32
F32R = mybir.dt.float32r
BF16 = mybir.dt.bfloat16
ALU = mybir.AluOpType
ACT = mybir.ActivationFunctionType
AX = mybir.AxisListType

P = 128
B, S, H = 4, 512, 512
TT = S // P
HC = H // P
HEADS, HD = 16, 32
E = 8
I_CM = 2048
I_MOE = 1024
CH = 256
CK = CH // P
CHUNKS_CM = I_CM // CH
CHUNKS_E = I_MOE // CH
T_ALL = B * TT
TILE = 256
TP = TILE // P
TILES = (2 * B * S - E) // TILE + E
MAX_TILES = B * S // TILE
ROUTE = 2 * TT * E + 2 * TT
NEG = -1.0e30
LN_EPS = 1e-5
LN12_EPS = 1e-12
RMS_EPS = 1e-5
QK_SCALE = HD ** -0.5

V_TMG, V_TMB, V_TF, V_TD, V_CMG, V_CMB, V_W1, V_W2 = range(8)
R_G1, R_B1, R_G2, R_B2 = range(4)


def mm3(pe, out, w_hi, w_lo, x_hi, x_lo, first, last):
    pe.matmul(out, lhsT=w_hi, rhs=x_hi, start=first, stop=False)
    pe.matmul(out, lhsT=w_hi, rhs=x_lo, start=False, stop=False)
    return pe.matmul(out, lhsT=w_lo, rhs=x_hi, start=False, stop=last)


def time_mix_phase(nc, psum, ident, d):
    ZERO_PARTS = 32
    ZEROS = TILES * TILE * H // (B * ZERO_PARTS * P)
    assert ZEROS * B * ZERO_PARTS * P == TILES * TILE * H
    MOMENTS, AFFINE = 2 * TT + 2, 2 * TT
    STATS_A = 3 * MOMENTS + AFFINE
    STATS_C = 2 * MOMENTS + AFFINE

    with ExitStack() as ctx:
        def sb(name, shape, dt=F32):
            return ctx.enter_context(nc.sbuf_tensor("tm_" + name, shape, dt))

        def sem(name):
            return ctx.enter_context(nc.semaphore("tm_" + name))

        with ExitStack() as shared:
            w_stage = shared.enter_context(nc.sbuf_tensor("tm_w_stage", [P, 3, HC * H], F32))
        xn_res = sb("xn_res", [P, TT, H])
        t2 = sb("t2", [P, TT, H])
        xcT = sb("xcT", [P, HC, S])
        vmix_wide = xcT[:, 0, :].rearrange("p (m n) -> p m n", m=HC)
        w_hi = sb("w_hi", [P, 3, HC, H], F32R)
        w_lo = sb("w_lo", [P, 3, HC, H], F32R)
        wo = sb("wo", [P, HC, H])
        bo_row = sb("bo_row", [1, H])
        ones_row = sb("ones_row", [1, P])
        vecs = sb("vecs", [P, 8, HC])
        rows = sb("rows", [P, 4, H])
        one_minus_tf = sb("one_minus_tf", [P, HC])
        steps_left = sb("steps_left", [P, S])
        decay = sb("decay", [P, HC, S])
        x_in = sb("x_in", [P, TT, H])
        xn = sb("xn", [P, TT, H])
        t1 = sb("t1", [P, TT, H])
        xT = sb("xT", [P, HC, S + 2])
        x_hi = sb("x_hi", [P, HC, S], F32R)
        x_lo = sb("x_lo", [P, HC, S], F32R)
        mix = sb("mix", [P, HC, S])
        m_hi = sb("m_hi", [P, HC, S], F32R)
        m_lo = sb("m_lo", [P, HC, S], F32R)
        x2 = sb("x2", [P, TT, H])
        xc_hi = sb("xc_hi", [P, HC, S], F32R)
        xc_lo = sb("xc_lo", [P, HC, S], F32R)
        vmix = sb("vmix", [P, HC])
        A, C = 0, 1
        stats = sb("stats", [P, 2, TT, 6])
        mv = sb("mv", [P, 2, TT, 2])
        rstd = sb("rstd", [P, 2, TT])
        nmr = sb("nmr", [P, 2, TT])
        var_eps = sb("var_eps", [P, 2, TT])
        spare = sb("spare", [P, 8])
        minus_half = sb("minus_half", [P, TT])
        zeros = sb("zeros", [P, ZEROS])

        const_in = sem("const_in")
        w_in = sem("w_in")
        w_hi_ready = sem("w_hi_ready")
        w_lo_ready = sem("w_lo_ready")
        consts_ready = sem("consts_ready")
        steps_ready = sem("steps_ready")
        x_loaded = sem("x_loaded")
        stat = [sem("stat_a"), sem("stat_c")]
        rstd_ready = [sem("rstd_a_ready"), sem("rstd_c_ready")]
        xn_ready = sem("xn_ready")
        norm_ready = [sem("norm_a_ready"), sem("norm_c_ready")]
        x_turned = sem("x_turned")
        xc_turned = sem("xc_turned")
        x_split = sem("x_split")
        x_lo_ready = sem("x_lo_ready")
        mix_step = sem("mix_step")
        m_hi_ready = sem("m_hi_ready")
        m_lo_ready = sem("m_lo_ready")
        v_done = sem("v_done")
        vmix_step = sem("vmix_step")
        r_done = sem("r_done")
        r_ready = sem("r_ready")
        res_loaded = sem("res_loaded")
        x2_step = sem("x2_step")
        xc_hi_ready = sem("xc_hi_ready")
        xc_lo_ready = sem("xc_lo_ready")
        rc_done = sem("rc_done")
        rc_ready = sem("rc_ready")
        xn_out = sem("xn_out")
        x2_out = sem("x2_out")
        xc_out = sem("xc_out")
        rc_out = sem("rc_out")

        N_CONST = 6
        CONSTS = HC + 3
        R = TT + 1
        tokens = "(j p) h -> p j h"
        block = ctx.enter_context(nc.Block())

        @block.sync
        def _(sp):
            def load_x(b):
                sp.dma_start(x_in[:, :, :], d["x"][b].rearrange(tokens, p=P)).then_inc(x_loaded, 16)

            def xn_rows_out(b):
                sp.wait_ge(xn_ready, b * TT + TT)
                sp.dma_start(d["xn"][b].rearrange(tokens, p=P), xn[:, :, :]).then_inc(xn_out, 16)

            def xc_halves_out(b):
                sp.wait_ge(xc_hi_ready, b * HC + HC)
                sp.dma_start(d["xc_hi"][b], xc_hi[:, :, :].bitcast(F32)).then_inc(xc_out, 16)
                sp.wait_ge(xc_lo_ready, b * HC + HC)
                sp.dma_start(d["xc_lo"][b], xc_lo[:, :, :].bitcast(F32)).then_inc(xc_out, 16)

            def sequence(b, before, more, more2):
                sp.wait_ge(xn_out, b * 16 + 16)
                sp.dma_start(xn_res[:, :, :], d["xn"][b].rearrange(tokens, p=P)).then_inc(res_loaded, 16)
                if more:
                    xn_rows_out(b + 1)
                if more2:
                    load_x(b + 2)
                sp.dma_start(d["tiles_in"].rearrange("r h -> (r h)").rearrange(
                    "(b n p e) -> b p n e", b=B, n=ZERO_PARTS, p=P)[b],
                    zeros[:, :].unsqueeze(1).to_broadcast([P, ZERO_PARTS, ZEROS])).then_inc(w_in, 16)
                sp.wait_ge(x2_step, b * 2 * TT + 2 * TT)
                sp.dma_start(d["x2"][b].rearrange(tokens, p=P), x2[:, :, :]).then_inc(x2_out, 16)
                if before:
                    xc_halves_out(b - 1)

            load_x(0)
            sp.dma_start(vecs[:, :, :], d["vecs"]).then_inc(const_in, 16)
            for n in range(4):
                sp.dma_start(rows[:, n, :], d["rows"][n:n + 1, :].partition_broadcast(P)).then_inc(const_in, 16)
            sp.dma_start(bo_row[:, :], d["rows"][4:5, :]).then_inc(const_in, 16)
            for n in range(3):
                sp.dma_start(w_stage[:, n, :], d["w_tm"][n]).then_inc(w_in, 16)
            sp.dma_start(wo[:, :, :], d["w_tm"][3].rearrange("p (k n) -> p k n", k=HC)).then_inc(res_loaded, 16)
            xn_rows_out(0)
            load_x(1)
            sp.wait_ge(res_loaded, 16)
            sp.wait_ge(consts_ready, CONSTS)
            sp.wait_ge(w_lo_ready, 3)
            sequence(0, False, True, True)
            with sp.Fori(1, B - 2) as b:
                sequence(b, True, True, True)
            sequence(B - 2, True, True, False)
            sequence(B - 1, True, False, False)
            xc_halves_out(B - 1)
            sp.wait_ge(w_in, 16 * (3 + B))
            sp.wait_ge(xn_out, 16 * B)
            sp.wait_ge(x2_out, 16 * B)
            sp.wait_ge(xc_out, 32 * (B + 1))
            sp.wait_ge(rc_out, 16 * (B + TT))

        @block.gpsimd
        def _(pool):
            pool.iota(steps_left[:, :], [[-1, S]], base=S - 1, channel_multiplier=0,
                      allow_small_or_imprecise_dtypes=True).then_inc(steps_ready, 1)
            pool.memset(minus_half[:, :], -0.5).then_inc(steps_ready, 1)
            pool.wait_ge(steps_ready, 2)

            def inverse_root(chain, at):
                pool.wait_ge(stat[chain], at + 2 * TT + 1)
                pool.tensor_tensor(rstd[:, chain, :], var_eps[:, chain, :], minus_half[:, :],
                                   ALU.pow).then_inc(rstd_ready[chain], 1)

            def low(dst, src, hi, hi_ready, first, step, ready):
                for c in range(HC):
                    pool.wait_ge(hi_ready, first + step * (c + 1))
                    pool.tensor_tensor(dst[:, c, :], src(c), hi[:, c, :].bitcast(F32), ALU.subtract).then_inc(ready, 1)

            def low_x(b):
                low(x_lo, lambda c: xT[:, c, 1:S + 1], x_hi, x_split, b * 2 * HC, 2, x_lo_ready)

            def low_mix(b):
                low(m_lo, lambda c: mix[:, c, :], m_hi, m_hi_ready, b * HC, 1, m_lo_ready)

            def low_xc(b, xcT):
                low(xc_lo, lambda c: xcT[:, c, :], xc_hi, xc_hi_ready, b * HC, 1, xc_lo_ready)

            def sequence(b, before, more):
                if before:
                    inverse_root(C, (b - 1) * STATS_C)
                if more:
                    inverse_root(A, (b + 1) * STATS_A)
                if before:
                    inverse_root(C, (b - 1) * STATS_C + MOMENTS + AFFINE)
                if more:
                    inverse_root(A, (b + 1) * STATS_A + MOMENTS)
                    inverse_root(A, (b + 1) * STATS_A + 2 * MOMENTS + AFFINE)
                if before:
                    low_xc(b - 1, xcT)
                if more:
                    low_x(b + 1)
                    low_mix(b + 1)

            inverse_root(A, 0)
            inverse_root(A, MOMENTS)
            inverse_root(A, 2 * MOMENTS + AFFINE)
            low_x(0)
            low_mix(0)
            sequence(0, False, True)
            with pool.Fori(1, B - 1) as b:
                sequence(b, True, True)
            sequence(B - 1, True, False)
            inverse_root(C, (B - 1) * STATS_C)
            inverse_root(C, (B - 1) * STATS_C + MOMENTS + AFFINE)
            low_xc(B - 1, mix)

        @block.scalar
        def _(act):
            def normed(dst, src, chain, at, ready):
                act.wait_ge(stat[chain], at + MOMENTS)
                for j in range(TT):
                    act.activation(dst[:, j, :], src[:, j, :], ACT.Identity, bias=nmr[:, chain, j:j + 1],
                                   scale=rstd[:, chain, j:j + 1]).then_inc(ready, 1)

            def norm_x(b):
                normed(xn, x_in, A, b * STATS_A, xn_ready)

            def norm_x1(b):
                normed(t1, t1, A, b * STATS_A + 2 * MOMENTS + AFFINE, norm_ready[A])

            def norm_x2(b):
                normed(t2, t2, C, b * STATS_C + MOMENTS + AFFINE, norm_ready[C])

            def split_x(b):
                for c in range(HC):
                    act.wait_ge(x_turned, b * HC + c + 1)
                    act.activation(xT[:, c, 1:S + 1], psum[c][:, :], ACT.Identity, bias=vecs[:, V_TMB, c:c + 1],
                                   scale=vecs[:, V_TMG, c:c + 1]).then_inc(x_split, 1)
                    act.activation(x_hi[:, c, :], psum[c][:, :], ACT.Identity, bias=vecs[:, V_TMB, c:c + 1],
                                   scale=vecs[:, V_TMG, c:c + 1]).then_inc(x_split, 1)

            def split_xc(b, xcT):
                act.wait_ge(xc_out, b * 32 + 32)
                for c in range(HC):
                    act.wait_ge(xc_turned, b * HC + c + 1)
                    act.activation(xcT[:, c, :], psum[HC + c][:, :], ACT.Identity, bias=vecs[:, V_CMB, c:c + 1],
                                   scale=vecs[:, V_CMG, c:c + 1])
                    act.activation(xc_hi[:, c, :], psum[HC + c][:, :], ACT.Identity, bias=vecs[:, V_CMB, c:c + 1],
                                   scale=vecs[:, V_CMG, c:c + 1]).then_inc(xc_hi_ready, 1)

            def high_mix(b):
                for c in range(HC):
                    act.wait_ge(mix_step, b * 2 * HC + 2 * c + 2)
                    act.activation(m_hi[:, c, :], mix[:, c, :], ACT.Copy).then_inc(m_hi_ready, 1)

            def gate_r(b, before):
                if before:
                    act.wait_ge(x2_out, b * 16)
                for j in range(TT):
                    act.wait_ge(r_done, b * R + j + 1)
                    act.activation(x2[:, j, :], psum[HC + j][:, :], ACT.Sigmoid).then_inc(r_ready, 1)

            def gate_rc(b, rc, last=False):
                for j in range(TT):
                    act.wait_ge(rc_done, b * TT + j + 1)
                    act.activation(rc[:, j, :], psum[HC + j][:, :], ACT.Sigmoid).then_inc(rc_ready, 1)
                    if last:
                        act.wait_ge(rc_ready, b * TT + TT + j + 1)
                        act.dma_start(d["rc"][b][j * P:(j + 1) * P, :], rc[:, j, :]).then_inc(rc_out, 16)
                if not last:
                    act.wait_ge(rc_ready, b * TT + 2 * TT)
                    act.dma_start(d["rc"][b].rearrange(tokens, p=P), rc[:, :, :]).then_inc(rc_out, 16)

            def sequence(b, before, more):
                if more:
                    norm_x(b + 1)
                if before:
                    norm_x2(b - 1)
                gate_r(b, before)
                if before:
                    split_xc(b - 1, xcT)
                if more:
                    norm_x1(b + 1)
                    split_x(b + 1)
                    high_mix(b + 1)
                if before:
                    gate_rc(b - 1, xcT)

            norm_x(0)
            act.wait_ge(const_in, 16 * N_CONST)
            act.wait_ge(steps_ready, 2)
            for c in range(HC):
                act.activation(decay[:, c, :], steps_left[:, :], ACT.Exp,
                               scale=vecs[:, V_TD, c:c + 1]).then_inc(w_hi_ready, 1)
            act.wait_ge(w_in, 16 * 3)
            for n in range(3):
                act.activation(w_hi[:, n, :, :].rearrange("p k n -> p (k n)"), w_stage[:, n, :],
                               ACT.Copy).then_inc(w_hi_ready, 1)
            norm_x1(0)
            split_x(0)
            high_mix(0)
            sequence(0, False, True)
            with act.Fori(1, B - 1) as b:
                sequence(b, True, True)
            sequence(B - 1, True, False)
            norm_x2(B - 1)
            split_xc(B - 1, mix)
            gate_rc(B - 1, mix, True)

        @block.vector
        def _(dve):
            def moments(chain, src, at, eps):
                for j in range(TT):
                    dve.bn_stats(stats[:, chain, j, :], src[:, j, :]).then_inc(stat[chain], 1)
                dve.wait_ge(stat[chain], at + TT)
                dve.memset(spare[:, 4:5], 0.0)
                for j in range(TT):
                    dve.bn_aggr(mv[:, chain, j, :], stats[:, chain, j, :]).then_inc(stat[chain], 1)
                dve.wait_ge(stat[chain], at + 2 * TT)
                dve.tensor_scalar(var_eps[:, chain, :], mv[:, chain, :, 1], eps, None, ALU.add).then_inc(stat[chain], 1)

            def scales(chain, at, turn):
                dve.wait_ge(rstd_ready[chain], turn + 1)
                dve.scalar_tensor_tensor(nmr[:, chain, :], mv[:, chain, :, 0], -1.0, rstd[:, chain, :], ALU.mult,
                                         ALU.mult).then_inc(stat[chain], 1)
                dve.wait_ge(stat[chain], at + MOMENTS)

            def affine_norm(chain, dst, src, row_g, row_b, at):
                for j in range(TT):
                    dve.scalar_tensor_tensor(dst[:, j, :], src[:, j, :], mv[:, chain, j, 0:1], rows[:, row_g, :],
                                             ALU.subtract, ALU.mult).then_inc(stat[chain], 1)
                for j in range(TT):
                    dve.wait_ge(stat[chain], at + j + 1)
                    dve.scalar_tensor_tensor(dst[:, j, :], dst[:, j, :], rstd[:, chain, j:j + 1], rows[:, row_b, :],
                                             ALU.mult, ALU.add).then_inc(stat[chain], 1)
                dve.wait_ge(stat[chain], at + 2 * TT)

            def first_moments_x(b, before):
                dve.wait_ge(x_loaded, b * 16 + 16)
                if before:
                    dve.wait_ge(xn_out, b * 16)
                moments(A, x_in, b * STATS_A, LN_EPS)

            def norm_xn(b):
                at = b * STATS_A + MOMENTS
                dve.wait_ge(xn_ready, b * TT + TT)
                moments(A, xn, at, LN12_EPS)
                scales(A, at, b * 3 + 1)
                affine_norm(A, t1, xn, R_G1, R_B1, at + MOMENTS)
                moments(A, t1, at + MOMENTS + AFFINE, LN12_EPS)
                scales(A, at + MOMENTS + AFFINE, b * 3 + 2)

            def first_moments_x2(b):
                moments(C, x2, b * STATS_C, LN12_EPS)

            def norm_x2(b):
                at = b * STATS_C
                scales(C, at, b * 2)
                affine_norm(C, t2, x2, R_G2, R_B2, at + MOMENTS)
                moments(C, t2, at + MOMENTS + AFFINE, LN12_EPS)

            def mixed(b):
                for c in range(HC):
                    dve.wait_ge(x_split, b * 2 * HC + 2 * c + 2)
                    dve.tensor_scalar(mix[:, c, :], xT[:, c, 1:S + 1], vecs[:, V_TF, c:c + 1], None,
                                      ALU.mult).then_inc(mix_step, 1)
                    dve.wait_ge(mix_step, b * 2 * HC + 2 * c + 1)
                    dve.scalar_tensor_tensor(mix[:, c, :], xT[:, c, 0:S], one_minus_tf[:, c:c + 1], mix[:, c, :],
                                             ALU.mult, ALU.add).then_inc(mix_step, 1)

            def time_sums(b, before):
                for m in range(HC):
                    dve.wait_ge(v_done, b * HC + m + 1)
                    if m:
                        dve.wait_ge(vmix_step, b * (HC + 1) + m)
                    dve.tensor_tensor_reduce(steps_left[:, :], psum[m][:, :], decay[:, m, :], 1.0, 0.0, ALU.mult,
                                             ALU.add, vmix[:, m:m + 1]).then_inc(vmix_step, 1)
                dve.wait_ge(vmix_step, b * (HC + 1) + HC)
                if before:
                    dve.wait_ge(rc_out, b * 16)
                dve.tensor_copy(vmix_wide,
                                vmix[:, :].unsqueeze(2).to_broadcast([P, HC, P])).then_inc(vmix_step, 1)

            def residual(b):
                dve.wait_ge(r_done, b * R + R)
                for j in range(TT):
                    dve.wait_ge(r_ready, b * TT + j + 1)
                    dve.tensor_tensor(x2[:, j, :], x2[:, j, :], psum[0][:, :], ALU.mult).then_inc(x2_step, 1)
                dve.wait_ge(res_loaded, b * 16 + 32)
                for j in range(TT):
                    dve.wait_ge(x2_step, b * 2 * TT + j + 1)
                    dve.tensor_tensor(x2[:, j, :], x2[:, j, :], xn_res[:, j, :], ALU.add).then_inc(x2_step, 1)
                dve.wait_ge(x2_step, b * 2 * TT + 2 * TT)

            def sequence(b, before, more, more2):
                if more:
                    scales(A, (b + 1) * STATS_A, (b + 1) * 3)
                if before:
                    norm_x2(b - 1)
                time_sums(b, before)
                if before:
                    scales(C, (b - 1) * STATS_C + MOMENTS + AFFINE, (b - 1) * 2 + 1)
                if more:
                    norm_xn(b + 1)
                residual(b)
                first_moments_x2(b)
                if more2:
                    first_moments_x(b + 2, True)
                if more:
                    mixed(b + 1)

            dve.memset(ones_row[:, :], 1.0).then_inc(consts_ready, 1)
            for c in range(HC):
                dve.memset(xT[:, c, 0:1], 0.0).then_inc(consts_ready, 1)
            dve.memset(zeros[:, :], 0.0).then_inc(consts_ready, 1)
            for i, (sm, n) in enumerate(((xc_out, 32), (rc_out, 16), (rc_ready, TT))):
                dve.memset(spare[:, i:i + 1], 0.0).then_inc(sm, n)
            first_moments_x(0, False)
            scales(A, 0, 0)
            dve.wait_ge(const_in, 16 * N_CONST)
            dve.tensor_scalar(one_minus_tf[:, :], vecs[:, V_TF, :], -1.0, 1.0, ALU.mult,
                              ALU.add).then_inc(consts_ready, 1)
            dve.wait_ge(consts_ready, CONSTS)
            norm_xn(0)

            def low_w(n):
                dve.wait_ge(w_hi_ready, HC + n + 1)
                dve.tensor_tensor(w_lo[:, n, :, :].rearrange("p k n -> p (k n)"), w_stage[:, n, :],
                                  w_hi[:, n, :, :].rearrange("p k n -> p (k n)").bitcast(F32),
                                  ALU.subtract).then_inc(w_lo_ready, 1)

            low_w(0)
            low_w(1)
            mixed(0)
            low_w(2)
            first_moments_x(1, True)
            sequence(0, False, True, True)
            with dve.Fori(1, B - 2) as b:
                sequence(b, True, True, True)
            sequence(B - 2, True, True, False)
            sequence(B - 1, True, False, False)
            dve.wait_ge(xc_turned, (B - 1) * HC)
            norm_x2(B - 1)
            scales(C, (B - 1) * STATS_C + MOMENTS + AFFINE, (B - 1) * 2 + 1)

        @block.tensor
        def _(pe):
            def turn(src, bank, done):
                for c in range(HC):
                    for j in range(TT):
                        t = pe.transpose(psum[bank + c][:, j * P:(j + 1) * P], src[:, j, c * P:(c + 1) * P], ident)
                    t.then_inc(done, 1)

            def turn_x(b):
                pe.wait_ge(norm_ready[A], b * TT + TT)
                turn(t1, 0, x_turned)

            def turn_xc(b):
                pe.wait_ge(norm_ready[C], b * TT + TT)
                turn(t2, HC, xc_turned)

            def by_token(n, hi, lo, done):
                for j in range(TT):
                    for k in range(HC):
                        cols = slice(j * P, (j + 1) * P)
                        last = mm3(pe, psum[HC + j][:, :], hi[:, k, cols], lo[:, k, cols],
                                   w_hi[:, n, k, :], w_lo[:, n, k, :], k == 0, k == HC - 1)
                    last.then_inc(done, 1)

            def v(b):
                for m in range(HC):
                    for k in range(HC):
                        if m == 0:
                            pe.wait_ge(x_lo_ready, b * HC + k + 1)
                        if m == 0 and k == 0:
                            pe.wait_ge(x_split, b * 2 * HC + 2 * HC)
                        cols = slice(m * P, (m + 1) * P)
                        last = mm3(pe, psum[m][:, :], w_hi[:, 0, k, cols], w_lo[:, 0, k, cols],
                                   x_hi[:, k, :], x_lo[:, k, :], k == 0, k == HC - 1)
                    last.then_inc(v_done, 1)

            def r(b):
                pe.wait_ge(m_lo_ready, b * HC + HC)
                by_token(1, m_hi, m_lo, r_done)

            def time_row(b):
                pe.wait_ge(vmix_step, b * (HC + 1) + HC + 1)
                for m in range(HC):
                    pe.matmul(psum[0][:, :], lhsT=vmix_wide[:, m, :], rhs=wo[:, m, :], start=(m == 0), stop=False)
                pe.matmul(psum[0][:, :], lhsT=ones_row[:, :], rhs=bo_row[:, :], start=False,
                          stop=True).then_inc(r_done, 1)

            def rc(b):
                pe.wait_ge(xc_lo_ready, b * HC + HC)
                by_token(2, xc_hi, xc_lo, rc_done)

            def sequence(b, before, more):
                if before:
                    v(b)
                    pe.wait_ge(rc_ready, b * TT)
                r(b)
                time_row(b)
                if before:
                    pe.wait_ge(r_ready, b * TT + TT)
                    turn_xc(b - 1)
                if more:
                    pe.wait_ge(x2_step, b * 2 * TT + TT)
                    turn_x(b + 1)
                if before:
                    rc(b - 1)

            pe.wait_ge(consts_ready, CONSTS)
            turn_x(0)
            pe.wait_ge(w_lo_ready, 1)
            v(0)
            pe.wait_ge(w_lo_ready, 3)
            pe.wait_ge(const_in, 16 * N_CONST)
            pe.wait_ge(res_loaded, 16)
            sequence(0, False, True)
            with pe.Fori(1, B - 1) as b:
                sequence(b, True, True)
            sequence(B - 1, True, False)
            pe.wait_ge(rc_ready, B * TT)
            turn_xc(B - 1)
            rc(B - 1)


def channel_mix_phase(nc, psum, d, routing, acc, stage, first_tile):
    WD = HC * CH
    WW = WD + CK * H
    STEPS = 2 * B
    TURNS = CHUNKS_CM // 2
    tokens = "(j p) h -> p j h"

    with ExitStack() as ctx:
        def sb(nm, shape, dt=F32):
            return ctx.enter_context(nc.sbuf_tensor("cm_" + nm, shape, dt))

        def sem(nm):
            return ctx.enter_context(nc.semaphore("cm_" + nm))

        x_hi = sb("x_hi", [P, HC, B, S + 2], F32R)
        x_lo = sb("x_lo", [P, HC, B, S + 2], F32R)
        w_hi = sb("w_hi", [P, 2, WW], F32R)
        w_lo = sb("w_lo", [P, 2, WW], F32R)
        relu = sb("relu", [P, CK, S])
        a = sb("a", [P, CK, S])
        a_hi = sb("a_hi", [P, 2, CK, S], F32R)
        a_lo = sb("a_lo", [P, 2, CK, S], F32R)
        gates = [sb(f"gate{n}", [P, TT, H]) for n in range(3)]
        rows = gates[2]
        spare = sb("spare", [P, 8])

        x_loaded = [sem(f"x_loaded{b}") for b in range(B)]
        stage_in = [sem(f"stage_in{u}") for u in range(2)]
        w_hi_ready = [sem(f"w_hi_ready{u}") for u in range(2)]
        w_lo_ready = [sem(f"w_lo_ready{u}") for u in range(2)]
        zeroed = sem("zeroed")
        up_done = sem("up_done")
        relu_ready = sem("relu_ready")
        a_full = sem("a_full")
        a_hi_ready = sem("a_hi_ready")
        a_lo_ready = sem("a_lo_ready")
        y_done = sem("y_done")
        y_free = sem("y_free")
        gate_in = [sem(f"gate_in{n}") for n in range(3)]
        gated = sem("gated")
        pre_added = sem("pre_added")
        first_in = sem("first_in")
        rows_loaded = sem("rows_loaded")
        sent = sem("sent")
        up_bank = psum[0:CK]
        y_bank = psum[2 * CK:2 * CK + TT]
        route = Router(nc, ctx, psum[2], psum[3], routing)

        block = ctx.enter_context(nc.Block())

        @block.sync
        def _(sp):
            def load(u, n):
                sp.dma_start(stage[:, u, :], d["w_cm"][n]).then_inc(stage_in[u], 16)

            sp.dma_start(route.rows_in, d["route"].rearrange("b p t -> p b t")).then_inc(route.loaded, 16)
            load(0, 0)
            for b in range(B):
                sp.dma_start(x_hi[:, :, b, 2:S + 2].bitcast(F32), d["xc_hi"][b]).then_inc(x_loaded[b], 16)
                sp.dma_start(x_lo[:, :, b, 2:S + 2].bitcast(F32), d["xc_lo"][b]).then_inc(x_loaded[b], 16)
                if b == 0:
                    load(1, 1)
            with sp.Fori(0, TURNS - 1) as it:
                for u in range(2):
                    sp.wait_ge(w_lo_ready[u], it + 1)
                    load(u, it * 2 + u + 2)

            first_x, first_w, gain = first_tile
            sp.wait_ge(sent, B * 32 * TT)
            sp.wait_ge(route.step, route.DONE)
            sp.dma_start(gain[:, :, :], d["vecs"]).then_inc(first_in, 16)
            e = sp.value_load(routing[1][0:1, 0:1], min_val=0, max_val=E - 1)
            for n in range(2 * B):
                if n >= 3:
                    sp.wait_ge((gated, pre_added)[(n - 3) % 2], (n - 3) // 2 * TT + TT)
                sp.dma_start(gates[n % 3][:, :, :],
                             d[("rc", "pre")[n % 2]][n // 2].rearrange(tokens, p=P)).then_inc(gate_in[n % 3], 16)
                if n == 2:
                    for u in range(2):
                        sp.wait_ge(w_lo_ready[u], TURNS)
                    sp.dma_start(first_x[:, :, :],
                                 d["tiles_in"][0:TILE, :].rearrange("(j p) h -> p j h", p=P)).then_inc(first_in, 16)
                    sp.dma_start(first_w[:, :], d["w_moe"][e * CHUNKS_E]).then_inc(first_in, 16)
            sp.wait_ge(first_in, 16 * 3)

        @block.gpsimd
        def _(pool):
            pool.memset(spare[:, 5:6], 0.0)
            route.masks_on_pool(pool)
            pool.memset(acc[:, :, :], 0.0).then_inc(route.consts, 1)
            pool.wait_ge(route.step, route.SLOTS)
            with pool.Fori(0, B) as b:
                pool.dma_start(rows[:, :, :], d["rows_in"][b].rearrange(tokens, p=P)).then_inc(rows_loaded, 16)
                for n in range(2):
                    pool.tensor_copy(route.now[:, n, :], route.slots[:, n, b, :]).then_inc(route.now_ready, 1)
                pool.wait_ge(route.now_ready, b * 2 + 2)
                pool.wait_ge(rows_loaded, b * 16 + 16)
                pool.tensor_tensor(spare[:, 6:7], spare[:, 5:6], spare[:, 5:6], ALU.add)
                for j in range(TT):
                    for n in range(2):
                        pool.indirect_dma_start(
                            out=d["tiles_in"], out_offset=bass.IndirectOffsetOnAxis(ap=route.now[:, n, j:j + 1], axis=0),
                            in_=rows[:, j, :], in_offset=None).then_inc(sent, 16)
                pool.wait_ge(sent, b * 32 * TT + 32 * TT)
            for b in range(B):
                pool.wait_ge(gate_in[(2 * b + 1) % 3], (2 * b + 1) // 3 * 16 + 16)
                for j in range(TT if b < B - 1 else TT // 2):
                    t = b * TT + j
                    pool.wait_ge(gated, t + 1)
                    pool.tensor_tensor(acc[:, t, :], acc[:, t, :], gates[(2 * b + 1) % 3][:, j, :],
                                       ALU.add).then_inc(pre_added, 1)

        @block.scalar
        def _(act):
            def split(u, n, g):
                act.wait_ge(stage_in[u], n * 16 + 16)
                if g is not None:
                    act.wait_ge(y_done, g * TT + 2 * TT)
                act.activation(w_hi[:, u, :], stage[:, u, :], ACT.Copy).then_inc(w_hi_ready[u], 1)

            def up(g, s):
                for m in range(CK):
                    act.wait_ge(up_done, g * CK + m + 1)
                    act.wait_ge(a_full, g * CK + m + 1)
                    act.activation(relu[:, m, :], up_bank[m][:, :], ACT.Relu).then_inc(relu_ready, 1)
                for m in range(CK):
                    act.wait_ge(a_full, g * CK + CK + m + 1)
                    if m == 0:
                        act.wait_ge(y_done, g * TT + TT)
                    act.activation(a_hi[:, s % 2, m, :], a[:, m, :], ACT.Copy).then_inc(a_hi_ready, 1)

            def turn(it, last):
                for s in range(STEPS):
                    if s == 0:
                        split(1, it, it * STEPS)
                    if s == B and not last:
                        split(0, it + 1, it * STEPS + B)
                    if not (last and s == STEPS - 1):
                        up(it * STEPS + s + 1, s + 1)

            split(0, 0, None)
            up(0, 0)
            with act.Fori(0, TURNS - 1) as it:
                turn(it, False)
            turn(TURNS - 1, True)

        @block.vector
        def _(dve):
            dve.memset(x_hi[:, :, :, 0:2].bitcast(F32), 0.0).then_inc(zeroed, 1)
            dve.memset(x_lo[:, :, :, 0:2].bitcast(F32), 0.0).then_inc(zeroed, 1)
            dve.memset(spare[:, 1:2], 0.0).then_inc(a_full, CK)
            dve.memset(spare[:, 2:3], 0.0).then_inc(y_done, 2 * TT)
            dve.memset(spare[:, 3:4], 0.0).then_inc(y_free, 4 * TT)
            dve.memset(spare[:, 4:5], 0.0).then_inc(a_lo_ready, CK)

            def split(u, n):
                dve.wait_ge(w_hi_ready[u], n + 1)
                dve.tensor_tensor(w_lo[:, u, :], stage[:, u, :], w_hi[:, u, :].bitcast(F32),
                                  ALU.subtract).then_inc(w_lo_ready[u], 1)

            def product(g, s):
                for m in range(CK):
                    dve.wait_ge(relu_ready, g * CK + m + 1)
                    dve.wait_ge(a_lo_ready, g * CK + m + 1)
                    dve.scalar_tensor_tensor(a[:, m, :], up_bank[m][:, :], 0.0, relu[:, m, :],
                                             ALU.max, ALU.mult).then_inc(a_full, 1)
                for m in range(CK):
                    dve.wait_ge(a_hi_ready, g * CK + m + 1)
                    dve.tensor_tensor(a_lo[:, s % 2, m, :], a[:, m, :], a_hi[:, s % 2, m, :].bitcast(F32),
                                      ALU.subtract).then_inc(a_lo_ready, 1)

            def accumulate(g, s, gate):
                for j in range(TT):
                    t = (s % B) * TT + j
                    dve.wait_ge(y_done, g * TT + 2 * TT + j + 1)
                    dve.wait_ge(y_free, g * TT + j + 1)
                    dve.tensor_tensor(acc[:, t, :], y_bank[j][:, :], acc[:, t, :], ALU.add).then_inc(y_free, 1)
                    if gate:
                        if j == 0:
                            dve.wait_ge(gate_in[2 * (s % B) % 3], 2 * (s % B) // 3 * 16 + 16)
                        dve.wait_ge(y_free, g * TT + 4 * TT + j + 1)
                        dve.tensor_tensor(acc[:, t, :], acc[:, t, :], gates[2 * (s % B) % 3][:, j, :],
                                          ALU.mult).then_inc(gated, 1)
                if gate and s % B == B - 1:
                    dve.wait_ge(gate_in[(2 * B - 1) % 3], (2 * B - 1) // 3 * 16 + 16)
                    for j in range(TT // 2, TT):
                        t = T_ALL - TT + j
                        dve.wait_ge(gated, t + 1)
                        dve.tensor_tensor(acc[:, t, :], acc[:, t, :], gates[(2 * B - 1) % 3][:, j, :], ALU.add)

            def turn(it, last):
                for s in range(STEPS):
                    if s == 0:
                        split(1, it)
                    if s == B and not last:
                        split(0, it + 1)
                    if not (last and s == STEPS - 1):
                        product(it * STEPS + s + 1, s + 1)
                    accumulate(it * STEPS + s, s, last and s >= B)

            route.on_dve(dve, lambda: split(0, 0))
            product(0, 0)
            dve.wait_ge(route.consts, 6)
            with dve.Fori(0, TURNS - 1) as it:
                turn(it, False)
            turn(TURNS - 1, True)

        @block.tensor
        def _(pe):
            def up(g, s, n):
                u, b = (s // B) % 2, s % B
                if b == 0:
                    pe.wait_ge(w_lo_ready[u], n + 1)
                pe.wait_ge(x_loaded[b], 32)
                for m in range(CK):
                    pe.wait_ge(a_full, g * CK + m + 1)
                    for k in range(HC):
                        cols = slice(k * CH + m * P, k * CH + (m + 1) * P)
                        last = mm3(pe, up_bank[m][:, :], w_hi[:, u, cols], w_lo[:, u, cols],
                                   x_hi[:, k, b, 1:S + 1], x_lo[:, k, b, 1:S + 1], k == 0, k == HC - 1)
                    last.then_inc(up_done, 1)

            def down(g, s):
                u = s // B
                pe.wait_ge(a_lo_ready, g * CK + 2 * CK)
                for j in range(TT):
                    pe.wait_ge(y_free, g * TT + 3 * TT + j + 1)
                    for m in range(CK):
                        cols = slice(j * P, (j + 1) * P)
                        rws = slice(WD + m * H, WD + (m + 1) * H)
                        last = mm3(pe, y_bank[j][:, :], a_hi[:, s % 2, m, cols], a_lo[:, s % 2, m, cols],
                                   w_hi[:, u, rws], w_lo[:, u, rws], m == 0, m == CK - 1)
                    last.then_inc(y_done, 1)

            def turn(it, last):
                for s in range(STEPS):
                    if not (last and s == STEPS - 1):
                        up(it * STEPS + s + 1, s + 1, it + (s + 1) // STEPS)
                    down(it * STEPS + s, s)

            route.on_pe(pe)
            pe.wait_ge(zeroed, 2)
            up(0, 0, 0)
            with pe.Fori(0, TURNS - 1) as it:
                turn(it, False)
            turn(TURNS - 1, True)


class Router:

    MEMBER, SLOTS, DONE = 1, 18 + E, 21 + E

    def __init__(self, nc, ctx, rank_bank, total_bank, routing):
        def sb(nm, shape, dt=F32):
            return ctx.enter_context(nc.sbuf_tensor("rt_" + nm, shape, dt))

        def sem(nm):
            return ctx.enter_context(nc.semaphore("rt_" + nm))

        self.slots, self.experts, self.weights = routing
        self.rank_bank, self.total_bank = rank_bank, total_bank
        self.raw = sb("raw", [P, B, ROUTE])
        self.rows_in = self.raw[:, :, :]
        self.now = sb("now", [P, 2, TT], mybir.dt.int32)
        self.before = sb("before", [P, P], BF16)
        self.ones = sb("ones", [P, P], BF16)
        self.member = sb("member", [P, T_ALL, E], BF16)
        self.total = sb("total", [P, T_ALL, E])
        self.upto = sb("upto", [P, T_ALL, E])
        self.slot = sb("slot", [P, T_ALL, E])
        self.one = sb("one", [P, TILES])
        self.limits = sb("limits", [P, MAX_TILES])
        self.numbers = sb("numbers", [P, TILES])
        self.over = sb("over", [P, E, MAX_TILES])
        self.n_tiles = sb("n_tiles", [P, E])
        self.tile_end = sb("tile_end", [P, E])
        self.first_slot = sb("first_slot", [P, E])
        self.picked = sb("picked", [P, 2, T_ALL, E])
        self.slot_f = sb("slot_f", [P, 2, T_ALL])
        self.past = sb("past", [P, TILES, E])
        self.expert_f = sb("expert_f", [P, TILES])
        self.loaded = sem("loaded")
        self.consts = sem("consts")
        self.step = sem("step")
        self.counted = sem("counted")
        self.now_ready = sem("now_ready")

    def masks_on_pool(self, pool):
        pool.memset(self.ones[:, :], 1.0).then_inc(self.consts, 1)
        pool.memset(self.one[:, :], 1.0).then_inc(self.consts, 1)
        pool.iota(self.limits[:, :], [[TILE, MAX_TILES]], base=0, channel_multiplier=0,
                  allow_small_or_imprecise_dtypes=True).then_inc(self.consts, 1)
        pool.iota(self.numbers[:, :], [[1, TILES]], base=0, channel_multiplier=0,
                  allow_small_or_imprecise_dtypes=True).then_inc(self.consts, 1)
        pool.wait_ge(self.consts, 4)
        pool.affine_select(out=self.before[:, :], in_=self.ones[:, :], compare_op=ALU.is_gt, fill=0.0, base=0,
                           pattern=[[1, P]], channel_multiplier=-1).then_inc(self.consts, 1)

    def on_pe(self, pe):
        pe.wait_ge(self.consts, 5)
        pe.wait_ge(self.step, self.MEMBER)
        member = self.member[:, :, :].rearrange("p t e -> p (t e)")
        pe.matmul(self.rank_bank[:, 0:T_ALL * E], lhsT=self.before[:, :], rhs=member, start=True,
                  stop=True).then_inc(self.counted, 1)
        pe.matmul(self.total_bank[:, 0:T_ALL * E], lhsT=self.ones[:, :], rhs=member, start=True,
                  stop=True).then_inc(self.counted, 1)

    def on_dve(self, dve, meanwhile):
        steps = [0]

        def step(i):
            i.then_inc(self.step, 1)
            steps[0] += 1
            dve.wait_ge(self.step, steps[0])

        dve.wait_ge(self.loaded, 16)
        dve.wait_ge(self.consts, 5)
        onehots = [self.raw[:, :, n * TT * E:(n + 1) * TT * E].rearrange("p b (j e) -> p b j e", e=E) for n in range(2)]

        def by_seq(x):
            return x.rearrange("p (b j) e -> p b j e", b=B)

        step(dve.tensor_tensor(by_seq(self.member[:, :, :]), onehots[0], onehots[1], ALU.add))
        assert steps[0] == self.MEMBER
        for n in range(2):
            step(dve.tensor_copy(self.weights[:, n, :, :], self.raw[:, :, 2 * TT * E + n * TT:2 * TT * E + (n + 1) * TT]))
        dve.wait_ge(self.counted, 2)
        step(dve.tensor_copy(self.total[:, :, :], self.total_bank[:, 0:T_ALL * E].rearrange("p (t e) -> p t e", e=E)))
        for e in range(E):
            step(dve.tensor_tensor_scan(self.upto[:, :, e], self.one[:, 0:T_ALL], self.total[:, :, e], 0.0,
                                        ALU.mult, ALU.add))
        meanwhile()
        count = self.upto[:, T_ALL - 1, :]
        step(dve.tensor_tensor(self.over[:, :, :], count.unsqueeze(2).to_broadcast([P, E, MAX_TILES]),
                               self.limits[:, :].unsqueeze(1).to_broadcast([P, E, MAX_TILES]), ALU.is_gt))
        step(dve.tensor_reduce(self.n_tiles[:, :], self.over[:, :, :], AX.X, ALU.add))
        step(dve.tensor_tensor_scan(self.tile_end[:, :], self.one[:, 0:E], self.n_tiles[:, :], 0.0, ALU.mult, ALU.add))
        step(dve.tensor_tensor(self.first_slot[:, :], self.tile_end[:, :], self.n_tiles[:, :], ALU.subtract))
        step(dve.tensor_scalar(self.first_slot[:, :], self.first_slot[:, :], float(TILE), None, ALU.mult))
        step(dve.tensor_tensor(self.upto[:, :, :], self.upto[:, :, :], self.total[:, :, :], ALU.subtract))
        step(dve.tensor_tensor(self.slot[:, :, :], self.upto[:, :, :],
                               self.first_slot[:, :].unsqueeze(1).to_broadcast([P, T_ALL, E]), ALU.add))
        step(dve.tensor_tensor(self.slot[:, :, :], self.slot[:, :, :],
                               self.rank_bank[:, 0:T_ALL * E].rearrange("p (t e) -> p t e", e=E), ALU.add))
        for n in range(2):
            step(dve.tensor_tensor(by_seq(self.picked[:, n, :, :]), by_seq(self.slot[:, :, :]), onehots[n], ALU.mult))
            step(dve.tensor_reduce(self.slot_f[:, n, :], self.picked[:, n, :, :], AX.X, ALU.add))
        for n in range(2):
            step(dve.tensor_copy(self.slots[:, n, :, :], self.slot_f[:, n, :].rearrange("p (b j) -> p b j", b=B)))
        assert steps[0] == self.SLOTS
        step(dve.tensor_tensor(self.past[:, :, :], self.numbers[:, :].unsqueeze(2).to_broadcast([P, TILES, E]),
                               self.tile_end[:, :].unsqueeze(1).to_broadcast([P, TILES, E]), ALU.is_ge))
        step(dve.tensor_reduce(self.expert_f[:, :], self.past[:, :, :], AX.X, ALU.add))
        step(dve.tensor_scalar(self.experts[:, :], self.expert_f[:, :], float(E - 1), None, ALU.min))
        assert steps[0] == self.DONE


def experts_phase(nc, psum, ident, routing, first_tile, d):
    C = CHUNKS_E
    WU, WD = HC * CH, 2 * HC * CH
    WW = WD + CK * H
    STAGES = C
    G = TILES * C
    TURNS = TILES // 2
    assert TILES % 2 == 1
    experts = routing[1]
    first_x, first_w, gain = first_tile

    with ExitStack() as ctx:
        def sb(nm, shape, dt=F32):
            return ctx.enter_context(nc.sbuf_tensor("ex_" + nm, shape, dt))

        def sem(nm):
            return ctx.enter_context(nc.semaphore("ex_" + nm))

        x_in = [first_x, sb("x_in", [P, TP, H])]
        x_hi = sb("x_hi", [P, 2, HC, TILE], F32R)
        x_lo = sb("x_lo", [P, 2, HC, TILE], F32R)
        stage = [first_w] + [sb(f"stage{c}", [P, WW]) for c in range(1, STAGES)]
        w_hi = sb("w_hi", [P, 2, WW], F32R)
        w_lo = sb("w_lo", [P, 2, WW], F32R)
        gate = sb("gate", [P, CK, TILE])
        a = sb("a", [P, CK, TILE])
        a_hi = sb("a_hi", [P, 2, CK, TILE], F32R)
        a_lo = sb("a_lo", [P, 2, CK, TILE], F32R)
        y = sb("y", [P, 2, TP, H])
        spare = sb("spare", [P, 16])

        stage_in = [sem(f"stage_in{c}") for c in range(STAGES)]
        x_loaded = [sem(f"x_loaded{p}") for p in range(2)]
        wu_hi_ready = sem("wu_hi_ready")
        wu_lo_ready = sem("wu_lo_ready")
        wd_hi_ready = sem("wd_hi_ready")
        wd_lo_ready = sem("wd_lo_ready")
        turned = sem("turned")
        x_hi_ready = sem("x_hi_ready")
        x_lo_ready = sem("x_lo_ready")
        up_done = sem("up_done")
        gate_ready = sem("gate_ready")
        a_full = sem("a_full")
        a_hi_ready = sem("a_hi_ready")
        a_lo_ready = sem("a_lo_ready")
        down_done = sem("down_done")
        y_by_act = sem("y_by_act")
        y_by_dve = sem("y_by_dve")
        y_out = [sem(f"y_out{p}") for p in range(2)]
        up_bank = psum[0:CK]
        turn_bank = psum[2:4]
        UP, DOWN = slice(0, WD), slice(WD, WW)

        def y_bank(p, j):
            return psum[4 + p * TP + j]

        rows = "(j p) h -> p j h"
        block = ctx.enter_context(nc.Block())

        def slots(it, last):
            for s in range(C if last else 2 * C):
                yield it * 2 * C + s, it * 2 + s // C, s // C, s % C

        @block.sync
        def _(sp):
            def weights(n, c, e):
                sp.wait_ge(wd_lo_ready, n * C + c + 1)
                sp.dma_start(stage[c][:, :], d["w_moe"][e * C + c]).then_inc(stage_in[c], 16)

            def expert_of(n):
                return sp.value_load(experts[0:1, bass.ds(n, 1)], min_val=0, max_val=E - 1)

            def tile(n, p):
                sp.wait_ge(turned, n + 1)
                sp.dma_start(x_in[p][:, :, :],
                             d["tiles_in"][bass.ds(n * TILE, TILE), :].rearrange(rows, p=P)).then_inc(x_loaded[p], 16)
                e = expert_of(n)
                for c in range(C):
                    weights(n, c, e)

            e = expert_of(0)
            for c in range(1, C):
                weights(0, c, e)
            with sp.Fori(0, TURNS) as it:
                for p in range(2):
                    tile(it * 2 + 1 + p, 1 - p)

        @block.gpsimd
        def _(pool):
            def low(g, s):
                for m in range(CK):
                    pool.wait_ge(a_hi_ready, g * CK + m + 1)
                    pool.tensor_tensor(a_lo[:, s % 2, m, :], a[:, m, :], a_hi[:, s % 2, m, :].bitcast(F32),
                                       ALU.subtract).then_inc(a_lo_ready, 1)

            def turn(it, last):
                for g, n, p, c in slots(it, last):
                    if not (last and c == C - 1):
                        low(g + 1, c + 1)

            low(0, 0)
            with pool.Fori(0, TURNS) as it:
                turn(it, False)
            turn(TURNS, True)

        @block.scalar
        def _(act):
            def split_up(g, n, c):
                act.wait_ge(stage_in[c], n * 16 + 16)
                act.activation(w_hi[:, c % 2, UP], stage[c][:, UP], ACT.Copy).then_inc(wu_hi_ready, 1)

            def split_down(g, c):
                act.activation(w_hi[:, c % 2, DOWN], stage[c][:, DOWN], ACT.Copy).then_inc(wd_hi_ready, 1)

            def split_x(n, p):
                act.wait_ge(turned, n + 3)
                for k in range(HC):
                    act.activation(x_hi[:, p, k, :], turn_bank[k // 2][:, k % 2 * TILE:(k % 2 + 1) * TILE], ACT.Copy,
                                   scale=gain[:, V_W2, k:k + 1]).then_inc(x_hi_ready, 1)

            def up(g, s, first):
                for m in range(CK):
                    act.wait_ge(up_done, g * CK + m + 1)
                    act.wait_ge(a_full, g * CK + m + 1)
                    act.activation(gate[:, m, :], up_bank[m][:, 0:TILE], ACT.Silu).then_inc(gate_ready, 1)
                for m in range(CK):
                    act.wait_ge(a_full, g * CK + CK + m + 1)
                    if m == 0 and not first:
                        act.wait_ge(down_done, g)
                    act.activation(a_hi[:, s % 2, m, :], a[:, m, :], ACT.Copy).then_inc(a_hi_ready, 1)

            def turn(it, last):
                for g, n, p, c in slots(it, last):
                    if not (last and c >= C - 2):
                        act.wait_ge(up_done, g * CK + CK)
                        split_up(g + 2, n + (c + 2) // C, (c + 2) % C)
                    if not (last and c == C - 1):
                        act.wait_ge(down_done, g + 1)
                        split_down(g + 1, (c + 1) % C)
                    if not (last and c == C - 1):
                        up(g + 1, c + 1, False)
                    if c == 1 and not last:
                        split_x(n + 1, 1 - p)
                    if c == C - 1:
                        act.wait_ge(down_done, g + 2)
                        act.wait_ge(y_out[p], it * 16 + 16)
                        act.activation(y[:, p, 0, :], y_bank(p, 0)[:, :], ACT.Copy).then_inc(y_by_act, 1)
                        act.wait_ge(y_by_act, n + 3)
                        act.wait_ge(y_by_dve, n + 3)
                        act.dma_start(d["tiles_out"][bass.ds(n * TILE, TILE), :].rearrange(rows, p=P),
                                      y[:, p, :, :]).then_inc(y_out[p], 16)

            act.preload_act_table_set("silu_and_others")
            split_up(0, 0, 0)
            split_x(0, 0)
            split_down(0, 0)
            split_up(1, 0, 1)
            up(0, 0, True)
            with act.Fori(0, TURNS) as it:
                turn(it, False)
            turn(TURNS, True)
            act.wait_ge(y_out[0], 16 * (TURNS + 2))
            act.wait_ge(y_out[1], 16 * (TURNS + 1))

        @block.vector
        def _(dve):
            def low(dst, src, hi):
                return dve.tensor_tensor(dst, src, hi.bitcast(F32), ALU.subtract)

            def split_up(g, c):
                dve.wait_ge(wu_hi_ready, g + 1)
                low(w_lo[:, c % 2, UP], stage[c][:, UP], w_hi[:, c % 2, UP]).then_inc(wu_lo_ready, 1)

            def split_down(g, c):
                dve.wait_ge(wd_hi_ready, g + 1)
                low(w_lo[:, c % 2, DOWN], stage[c][:, DOWN], w_hi[:, c % 2, DOWN]).then_inc(wd_lo_ready, 1)

            def split_x(n, p):
                for k in range(HC):
                    dve.wait_ge(x_hi_ready, n * HC + (k // 2) * 2 + 2)
                    dve.scalar_tensor_tensor(x_lo[:, p, k, :], turn_bank[k // 2][:, k % 2 * TILE:(k % 2 + 1) * TILE],
                                             gain[:, V_W2, k:k + 1], x_hi[:, p, k, :].bitcast(F32),
                                             ALU.mult, ALU.subtract).then_inc(x_lo_ready, 1)

            def product(g):
                for m in range(CK):
                    dve.wait_ge(gate_ready, g * CK + m + 1)
                    dve.wait_ge(a_lo_ready, g * CK + m + 1)
                    dve.tensor_tensor(a[:, m, :], gate[:, m, :], up_bank[m][:, TILE:2 * TILE],
                                      ALU.mult).then_inc(a_full, 1)

            def turn(it, last):
                for g, n, p, c in slots(it, last):
                    if not (last and c >= C - 2):
                        split_up(g + 2, (c + 2) % C)
                    if not (last and c == C - 1):
                        split_down(g + 1, (c + 1) % C)
                    if not (last and c == C - 1):
                        product(g + 1)
                    if c == 1 and not last:
                        split_x(n + 1, 1 - p)
                    if c == C - 1:
                        dve.wait_ge(down_done, g + 2)
                        dve.wait_ge(y_out[p], it * 16 + 16)
                        dve.tensor_copy(y[:, p, 1, :], y_bank(p, 1)[:, :]).then_inc(y_by_dve, 1)

            for i, (sm, n) in enumerate(((down_done, 1), (wd_lo_ready, STAGES), (a_full, CK), (a_lo_ready, CK),
                                         (x_loaded[0], 16), (stage_in[0], 16), (turned, 2), (y_by_act, 2), (y_by_dve, 2), (y_out[0], 16),
                                         (y_out[1], 16))):
                dve.memset(spare[:, i:i + 1], 0.0).then_inc(sm, n)
            split_up(0, 0)
            split_x(0, 0)
            split_down(0, 0)
            split_up(1, 1)
            product(0)
            with dve.Fori(0, TURNS) as it:
                turn(it, False)
            turn(TURNS, True)

        @block.tensor
        def _(pe):
            def turn_x(n, p, load, first):
                pe.wait_ge(x_loaded[p], load * 16 + 16)
                if not first:
                    pe.wait_ge(x_lo_ready, n * HC)
                for k in range(HC):
                    for j in range(TP):
                        at = k % 2 * TILE + j * P
                        i = pe.transpose(turn_bank[k // 2][:, at:at + P], x_in[p][:, j, k * P:(k + 1) * P], ident)
                i.then_inc(turned, 1)

            def up(g, n, p, c):
                pe.wait_ge(wu_lo_ready, g + 1)
                if c == 0:
                    pe.wait_ge(x_lo_ready, n * HC + HC)
                for m in range(CK):
                    pe.wait_ge(a_full, g * CK + m + 1)
                    for half, w0 in enumerate((0, WU)):
                        for k in range(HC):
                            cols = slice(w0 + k * CH + m * P, w0 + k * CH + (m + 1) * P)
                            last = mm3(pe, up_bank[m][:, half * TILE:(half + 1) * TILE], w_hi[:, c % 2, cols],
                                       w_lo[:, c % 2, cols], x_hi[:, p, k, :], x_lo[:, p, k, :], k == 0, k == HC - 1)
                    last.then_inc(up_done, 1)

            def down(g, n, p, c):
                pe.wait_ge(wd_lo_ready, g + STAGES + 1)
                pe.wait_ge(a_lo_ready, g * CK + 2 * CK)
                if c == 0:
                    pe.wait_ge(y_by_act, n + 1)
                    pe.wait_ge(y_by_dve, n + 1)
                for j in range(TP):
                    for m in range(CK):
                        cols = slice(j * P, (j + 1) * P)
                        wrows = slice(WD + m * H, WD + (m + 1) * H)
                        last = mm3(pe, y_bank(p, j)[:, :], a_hi[:, c % 2, m, cols], a_lo[:, c % 2, m, cols],
                                   w_hi[:, c % 2, wrows], w_lo[:, c % 2, wrows], c == 0 and m == 0,
                                   c == C - 1 and m == CK - 1)
                last.then_inc(down_done, 1)

            def turn(it, last):
                for g, n, p, c in slots(it, last):
                    if c < C - 1:
                        up(g + 1, n, p, c + 1)
                    elif not last:
                        up(g + 1, n + 1, 1 - p, 0)
                    down(g, n, p, c)
                    if c == 1 and not last:
                        turn_x(n + 1, 1 - p, it + p, False)

            turn_x(0, 0, 0, True)
            up(0, 0, 0, 0)
            with pe.Fori(0, TURNS) as it:
                turn(it, False)
            turn(TURNS, True)


def combine_phase(nc, routing, acc, d):
    slots, _, weights = routing
    tokens = "(j p) h -> p j h"
    with ExitStack() as ctx:
        def sb(nm, shape, dt=F32):
            return ctx.enter_context(nc.sbuf_tensor("co_" + nm, shape, dt))

        def sem(nm):
            return ctx.enter_context(nc.semaphore("co_" + nm))

        y = sb("y", [P, T_ALL, 2, H])
        y_in = [sem(f"y_in{b}") for b in range(B)]
        added = sem("added")
        out_done = sem("out_done")
        block = ctx.enter_context(nc.Block())

        @block.sync
        def _(sp):
            for b in range(B - 1):
                sp.wait_ge(added, 2 * TT * (b + 1))
                sp.dma_start(d["out"][b].rearrange(tokens, p=P),
                             acc[:, b * TT:(b + 1) * TT, :]).then_inc(out_done, 16)
            for j in range(TT):
                sp.wait_ge(added, 2 * TT * (B - 1) + 2 * j + 2)
                sp.dma_start(d["out"][B - 1][j * P:(j + 1) * P, :],
                             acc[:, (B - 1) * TT + j, :]).then_inc(out_done, 16)
            sp.wait_ge(out_done, 16 * (B - 1 + TT))

        @block.gpsimd
        def _(pool):
            for b in range(B):
                for j in range(TT):
                    for n in range(2):
                        pool.indirect_dma_start(
                            out=y[:, b * TT + j, n, :], out_offset=None, in_=d["tiles_out"],
                            in_offset=bass.IndirectOffsetOnAxis(ap=slots[:, n, b, j:j + 1], axis=0)
                        ).then_inc(y_in[b], 16)

        @block.vector
        def _(dve):
            for b in range(B):
                dve.wait_ge(y_in[b], 16 * 2 * TT)
                for j in range(TT):
                    for n in range(2):
                        t = b * TT + j
                        if n:
                            dve.wait_ge(added, b * 2 * TT + 2 * j + 1)
                        dve.scalar_tensor_tensor(acc[:, t, :], y[:, t, n, :], weights[:, n, b, j:j + 1], acc[:, t, :],
                                                 ALU.mult, ALU.add).then_inc(added, 1)


def attention_phase(nc, psum, ident, ident_bf, causal, causal_t, d):
    N_W = 3
    LAG = 8
    WO_AT = LAG + 12
    SETS = ((0, 4, 7), (4, 10, 7), (10, HEADS, 0))
    MOST = max(stop - start for start, stop, _ in SETS)
    GROUP = HEADS // 2
    PARTS = [[(max(start, g), min(stop, g + GROUP)) for g in (0, GROUP) if start < g + GROUP and stop > g]
             for start, stop, _ in SETS]
    MAX_DMAS = [sum(2 * len(p) for p in PARTS[:n + 1]) for n in range(len(SETS))]
    PAIR = 2 * HD
    PAIRS = HEADS // 2

    def high_by_dve(n):
        return n >= HEADS - LAG

    BY_DVE = [high_by_dve(n) for n in range(HEADS)].count(True)

    def rounded(n, by_dve):
        return [high_by_dve(m) for m in range(n + 1)].count(by_dve)

    V_HI_COLS, V_HI_STEP, V_HI_TILE = 7 * HD, 4 * HD, 3 * HD
    V_LO_COLS, V_LO_STEP, V_LO_TILE = 3 * HD, 2 * HD, HD
    S_AT = {3: (0, 0), 2: (1, 0), 0: (1, 3 * P), 1: (2, 0)}
    PT_AT = {0: (0, 0), 1: (1, 0), 3: (1, 3 * P), 2: (2, 0)}
    PT_PARTS = ((0, 512), (512, 512), (1024, 256))
    PT_COLS = 512 + 512 + 256
    STACK = 3 * HD

    def stack(n):
        half, c, place = n // 8, n % 8 // 2, n % 2
        return c, half, place, (half * 2 + place) * HC + c

    with ExitStack() as ctx:
        def sb(name, shape, dt=F32):
            return ctx.enter_context(nc.sbuf_tensor("at_" + name, shape, dt))

        def shared(*tensors):
            with ExitStack() as shared_ctx:
                return [shared_ctx.enter_context(nc.sbuf_tensor("at_" + name, shape, dt)) for name, shape, dt in tensors]

        def sem(name):
            return ctx.enter_context(nc.semaphore("at_" + name))

        w_hi = sb("w_hi", [P, N_W, HC, H], F32R)
        w_lo = sb("w_lo", [P, N_W, HC, H], F32R)
        wr = sb("wr", [P, HC, E])
        vecs = sb("vecs", [P, 8, HC])
        prefer = sb("prefer", [P, E])
        ones = sb("ones", [HEADS * TT, P])
        o, = shared(("o", [P, HC, S], F32))
        x_hi = sb("x_hi", [P, HC, S], F32R)
        xn, = shared(("xn", [P, TT, H], F32))
        x_lo = sb("x_lo", [P, HC, S], F32R)
        q2 = sb("q2", [P, HEADS, S], F32R)
        v_hi = sb("v_hi", [P, TT * PAIRS, V_HI_COLS], F32R)
        v_lo = sb("v_lo", [P, TT * PAIRS, V_LO_COLS], F32R)
        wo, xp, base, xT = (x[:, :, :] for x in shared(
            ("wo", [P, HC, H], F32), ("xp", [P, TT, H], F32), ("base", [P, TT, H], F32), ("xT", [P, HC, S], F32)))
        junk1, rows, x = wo, wo, xT
        k2 = sb("k2", [P, HEADS, S], F32R)
        wo_hi, wo_lo, o_hi, o_lo = (q2[:, n * HC:(n + 1) * HC, :] for n in range(4))
        w_stage, = shared(("w_stage", [P, N_W, HC * H], F32))
        p_full0, p_full1, p_hi0, p_hi1, p_lo0, p_lo1, sums_rec = shared(
            *((name, [P, PT_COLS], F32) for name in ("p_full0", "p_full1")),
            *((name, [P, PT_COLS], F32R) for name in ("p_hi0", "p_hi1", "p_lo0", "p_lo1")), ("sums_rec", [P, S], F32))
        p_full, p_hi, p_lo = (p_full0, p_full1), (p_hi0, p_hi1), (p_lo0, p_lo1)
        q_hi, q_lo, k_hi, k_lo = (sb(n, [P, HC, S], F32R) for n in ("q_hi", "q_lo", "k_hi", "k_lo"))
        sq = sb("sq", [P, 2, TT])
        mean_sq = sb("mean_sq", [P, 2, TT])
        rstd = sb("rstd", [P, 2, TT])
        spare = sb("spare", [P, 8])
        minus_half = sb("minus_half", [P, TT])
        max_rows = sb("max_rows", [MOST, S], F32R)
        row_max = sb("row_max", [P, TT, HEADS])
        logits = sb("logits", [P, TT, E])
        left = sb("left", [P, TT, E])
        hit = sb("hit", [P, TT, E])
        top = sb("top", [P, 2, TT])
        pick = sb("pick", [P, TT])
        gap = sb("gap", [P, TT])
        odds = sb("odds", [P, TT])
        odds1 = sb("odds1", [P, TT])
        routes = sb("routes", [P, ROUTE])
        first = routes[:, 0:TT * E].rearrange("p (j e) -> p j e", e=E)
        second = routes[:, TT * E:2 * TT * E].rearrange("p (j e) -> p j e", e=E)
        p1 = routes[:, 2 * TT * E:2 * TT * E + TT]
        p2 = routes[:, 2 * TT * E + TT:ROUTE]

        const_in = sem("const_in")
        w_in = {n: sem(f"w_in{n}") for n in range(1, N_W)}
        wo_hi_ready = sem("wo_hi_ready")
        wo_lo_ready = sem("wo_lo_ready")
        w_hi_ready = sem("w_hi_ready")
        w_lo_ready = sem("w_lo_ready")
        consts_ready = sem("consts_ready")
        xn_loaded = sem("xn_loaded")
        sq_ready = [sem(f"sq_ready{n}") for n in range(2)]
        mean_ready = [sem(f"mean_ready{n}") for n in range(2)]
        rstd_ready = [sem(f"rstd_ready{n}") for n in range(2)]
        norm_ready = [sem(f"norm_ready{n}") for n in range(2)]
        x_turned = sem("x_turned")
        x_hi_ready = sem("x_hi_ready")
        x_lo_ready = sem("x_lo_ready")
        q_done = sem("q_done")
        k_done = sem("k_done")
        v_done = sem("v_done")
        q_hi_ready = sem("q_hi_ready")
        q_lo_ready = sem("q_lo_ready")
        k_hi_ready = sem("k_hi_ready")
        k_lo_ready = sem("k_lo_ready")
        v_hi_ready = sem("v_hi_ready")
        v_lo_ready = sem("v_lo_ready")
        q2_in = sem("q2_in")
        k2_in = sem("k2_in")
        scores_done = sem("scores_done")
        max_step = sem("max_step")
        max_turned = sem("max_turned")
        max_rows_ready = sem("max_rows_ready")
        max_in = sem("max_in")
        turned_scores_done = sem("turned_scores_done")
        exp_ready = sem("exp_ready")
        p_hi_by_act = sem("p_hi_by_act")
        p_hi_by_dve = sem("p_hi_by_dve")
        p_lo_ready = sem("p_lo_ready")
        heads_done = sem("heads_done")
        rec_ready = sem("rec_ready")
        o_ready = sem("o_ready")
        wo_in = sem("wo_in")
        o_hi_ready = sem("o_hi_ready")
        o_lo_ready = sem("o_lo_ready")
        res_loaded = sem("res_loaded")
        proj_done = sem("proj_done")
        xp_ready = sem("xp_ready")
        pre_ready = sem("pre_ready")
        rows_turned = sem("rows_turned")
        xT_ready = sem("xT_ready")
        logits_done = sem("logits_done")
        route = sem("route")
        odds_ready = sem("odds_ready")
        routes_ready = sem("routes_ready")
        rows_sent = sem("rows_sent")
        route_out = sem("route_out")
        pre_out = sem("pre_out")

        tokens = "(j p) h -> p j h"
        block = ctx.enter_context(nc.Block())

        def value_columns(values, step, j, place):
            return values[:, j * PAIRS:(j + 1) * PAIRS, place * step:place * step + HD]

        def value_products(j, place):
            return psum[j][:, :].rearrange("p (pair place n) -> p pair place n", place=2, n=HD)[:, :, place, :]

        @block.sync
        def _(sp):
            def load_x(b):
                sp.dma_start(xn[:, :, :], d["xn"][b].rearrange(tokens, p=P)).then_inc(xn_loaded, 16)

            def stack_halves(dst, halves, loaded):
                for g, half in enumerate(halves):
                    for n in range(4):
                        sp.dma_start(dst[g * HD:(g + 1) * HD, n * HC:(n + 1) * HC, :].bitcast(F32),
                                     half[n * HD:(n + 1) * HD, :, :].bitcast(F32)).then_inc(loaded, 16)

            def stack_q():
                stack_halves(q2, (q_hi, q_hi, q_lo), q2_in)

            def stack_k():
                stack_halves(k2, (k_hi, k_lo, k_hi), k2_in)
                sp.dma_start(k2[STACK:STACK + 1, :, :].bitcast(F32),
                             ones[:, :]).then_inc(k2_in, 16)

            def maxima(b):
                for n, (start, _, _) in enumerate(SETS):
                    sp.wait_ge(max_rows_ready, b * len(SETS) + n + 1)
                    for first_head, end in PARTS[n]:
                        for place in range(2):
                            at, pairs = stack(first_head + place)[3], (end - first_head) // 2
                            row = first_head - start + place
                            sp.dma_start(q2[STACK:STACK + 1, at:at + pairs, :].bitcast(F32),
                                         max_rows[row:row + 2 * pairs - 1:2, :].bitcast(F32)).then_inc(max_in, 16)

            def residual(b):
                sp.wait_ge(turned_scores_done, b * HEADS + GROUP)
                sp.dma_start(wo, d["w_at"][N_W].rearrange("p (k n) -> p k n", k=HC)).then_inc(wo_in, 16)
                sp.dma_start(xp, d["xn"][b].rearrange(tokens, p=P)).then_inc(res_loaded, 16)
                sp.wait_ge(turned_scores_done, b * HEADS + HEADS)
                sp.dma_start(base, d["x2"][b].rearrange(tokens, p=P)).then_inc(res_loaded, 16)
                sp.dma_start(x, d["x"][b].rearrange(tokens, p=P)).then_inc(res_loaded, 16)

            def rows_out(b):
                sp.wait_ge(norm_ready[1], b * TT + TT)
                sp.dma_start(d["rows_in"][b].rearrange(tokens, p=P), rows).then_inc(rows_sent, 16)
                sp.wait_ge(pre_ready, b * 2 + 2)
                sp.dma_start(d["pre"][b].rearrange(tokens, p=P), base).then_inc(pre_out, 16)

            def route_rows_out(b):
                sp.wait_ge(routes_ready, b + 1)
                sp.dma_start(d["route"][b], routes[:, :]).then_inc(route_out, 16)

            load_x(0)
            sp.dma_start(vecs[:, :, :], d["vecs"]).then_inc(const_in, 16)
            sp.dma_start(wr[:, :, :], d["w_r"]).then_inc(const_in, 16)
            sp.dma_start(w_stage[:, 0, :], d["w_at"][0]).then_inc(const_in, 16)
            for n in range(1, N_W):
                sp.dma_start(w_stage[:, n, :], d["w_at"][n]).then_inc(w_in[n], 16)
            sp.wait_ge(consts_ready, 7)
            sp.wait_ge(q_lo_ready, HC)
            stack_q()
            sp.wait_ge(k_lo_ready, HC)
            stack_k()
            with sp.Fori(0, B - 1) as b:
                sp.wait_ge(v_done, b * TT + TT)
                load_x(b + 1)
                maxima(b)
                residual(b)
                rows_out(b)
                sp.wait_ge(q_lo_ready, b * HC + 2 * HC)
                stack_q()
                sp.wait_ge(logits_done, b + 1)
                stack_k()
                route_rows_out(b)
            maxima(B - 1)
            residual(B - 1)
            rows_out(B - 1)
            route_rows_out(B - 1)
            sp.wait_ge(rows_sent, 16 * B)
            sp.wait_ge(pre_out, 16 * B)
            sp.wait_ge(route_out, 16 * (B + 1))

        @block.gpsimd
        def _(pool):
            def inverse_root(n, b):
                pool.wait_ge(mean_ready[n], b + 1)
                pool.tensor_tensor(rstd[:, n, :], mean_sq[:, n, :], minus_half[:, :], ALU.pow).then_inc(rstd_ready[n], 1)

            pool.memset(minus_half[:, :], -0.5).then_inc(consts_ready, 1)
            pool.iota(prefer[:, :], [[-1, E]], base=E, channel_multiplier=0,
                      allow_small_or_imprecise_dtypes=True).then_inc(consts_ready, 1)
            pool.memset(ones[:, :], 1.0).then_inc(consts_ready, 1)
            pool.wait_ge(consts_ready, 1)
            inverse_root(0, 0)
            for values in (v_hi, v_lo):
                pool.memset(values[:, :, :].bitcast(F32), 0.0).then_inc(consts_ready, 1)
            pool.wait_ge(consts_ready, 5)
            for place in range(2):
                at = 2 * HD + place * V_HI_STEP
                pool.memset(v_hi[:, :, at:at + HD].bitcast(F32), 1.0).then_inc(consts_ready, 1)
            pool.memset(spare[:, 2:3], 0.0).then_inc(route_out, 16)

            def tail(b):
                pool.wait_ge(res_loaded, b * 48 + 48)
                pool.tensor_tensor(base, base, x, ALU.add).then_inc(pre_ready, 1)
                inverse_root(1, b)
                pool.wait_ge(pre_ready, b * 2 + 1)
                pool.wait_ge(xp_ready, b * TT + TT)
                pool.tensor_tensor(base, base, xp, ALU.add).then_inc(pre_ready, 1)

            with pool.Fori(0, B - 1) as b:
                inverse_root(0, b + 1)
                tail(b)
            tail(B - 1)

        @block.scalar
        def _(act):
            def squares(n, src, unused, b):
                for j in range(TT):
                    if n:
                        act.wait_ge(xp_ready, b * TT + j + 1)
                    act.activation(unused[:, j, :], src[:, j, :], ACT.Square,
                                   accum_out=sq[:, n, j:j + 1]).then_inc(sq_ready[n], 1)

            def scaled(n, dst, src, b):
                act.wait_ge(rstd_ready[n], b + 1)
                for j in range(TT):
                    act.activation(dst[:, j, :], src[:, j, :], ACT.Copy,
                                   scale=rstd[:, n, j:j + 1]).then_inc(norm_ready[n], 1)

            def high(dst, bank, done, ready, b, gain=None):
                for c in range(HC):
                    act.wait_ge(done, b * HC + c + 1)
                    act.activation(dst[:, c, :], psum[bank + c][:, :], ACT.Copy,
                                   scale=1.0 if gain is None else vecs[:, gain, c:c + 1]).then_inc(ready, 1)

            def high_v(b):
                for j in range(TT):
                    act.wait_ge(v_done, b * TT + j + 1)
                    for place in range(2):
                        act.activation(value_columns(v_hi, V_HI_STEP, j, place), value_products(j, place),
                                       ACT.Copy).then_inc(v_hi_ready, 1)

            def max_row(b, n):
                start, stop, bank = SETS[n]
                act.wait_ge(max_turned, b * len(SETS) + n + 1)
                if n:
                    act.wait_ge(max_in, (b * MAX_DMAS[-1] + MAX_DMAS[n - 1]) * 16)
                act.activation(max_rows[0:stop - start, :], psum[bank][0:stop - start, :], ACT.Copy,
                               scale=-1.0).then_inc(max_rows_ready, 1)

            def exps(b, i):
                act.wait_ge(turned_scores_done, b * HEADS + i + 1)
                if i >= 2:
                    act.wait_ge(p_lo_ready, b * HEADS + i - 1)
                for n, (at, cols) in enumerate(PT_PARTS):
                    act.activation(p_full[i % 2][:, at:at + cols], psum[3 + n][:, 0:cols], ACT.Exp,
                                   scale=QK_SCALE).then_inc(exp_ready, 1)
                if not high_by_dve(i):
                    act.wait_ge(exp_ready, (b * HEADS + i) * 3 + 3)
                    if i >= 2:
                        act.wait_ge(heads_done, b * HEADS + i - 1)
                    act.activation(p_hi[i % 2][:, :], p_full[i % 2][:, :], ACT.Copy).then_inc(p_hi_by_act, 1)

            def inverse_sums(b, n):
                act.wait_ge(heads_done, b * HEADS + 2 * n + 2)
                if n:
                    act.wait_ge(o_ready, b * HEADS // 2 + n)
                act.activation(sums_rec[0:PAIR, :], psum[6 + n % 2][PAIR:2 * PAIR, :], ACT.Ln).then_inc(rec_ready, 1)
                act.wait_ge(rec_ready, b * HEADS + 2 * n + 1)
                act.activation(sums_rec[0:PAIR, :], sums_rec[0:PAIR, :], ACT.Exp, scale=-1.0).then_inc(rec_ready, 1)

            def heads(b, more):
                for s in range(HEADS + LAG + 2):
                    if s == 3 and more:
                        act.wait_ge(xn_loaded, b * 16 + 32)
                        squares(0, xn, o, b + 1)
                    for n, (_, stop, _) in enumerate(SETS):
                        if s == stop:
                            max_row(b, n)
                    if s == LAG - 1 and more:
                        scaled(0, xn, xn, b + 1)
                    if LAG <= s < HEADS + LAG:
                        exps(b, s - LAG)
                    if s >= LAG + 3 and (s - LAG) % 2:
                        inverse_sums(b, (s - LAG - 3) // 2)
                    if s == WO_AT:
                        high_wo(b)

            def high_wo(b):
                act.wait_ge(wo_in, b * 16 + 16)
                for k in range(HC):
                    act.activation(wo_hi[:, k, :], wo[:, k, :], ACT.Copy).then_inc(wo_hi_ready, 1)

            def high_o(b):
                act.wait_ge(o_ready, b * HEADS // 2 + HEADS // 2)
                for c in range(HC):
                    act.activation(o_hi[:, c, :], o[:, c, :], ACT.Copy).then_inc(o_hi_ready, 1)

            def residual(b):
                squares(1, xp, junk1, b)
                scaled(1, rows, xp, b)

            def turned_rows(b):
                act.wait_ge(pre_ready, b * 2 + 1)
                high(xT, 4, rows_turned, xT_ready, b, V_W2)

            def route_odds(b):
                act.wait_ge(route, b * 15 + 13)
                act.activation(odds[:, :], gap[:, :], ACT.Exp).then_inc(odds_ready, 1)

            act.preload_act_table_set("natural_log_exp_and_others")
            act.wait_ge(xn_loaded, 16)
            squares(0, xn, junk1, 0)
            scaled(0, xn, xn, 0)

            def high_w(n):
                if n:
                    act.wait_ge(w_in[n], 16)
                act.activation(w_hi[:, n, :, :].rearrange("p k n -> p (k n)"), w_stage[:, n, :],
                               ACT.Copy).then_inc(w_hi_ready, 1)

            act.wait_ge(const_in, 48)
            high_w(0)
            high(x_hi, 0, x_turned, x_hi_ready, 0, V_W1)
            for n in range(1, N_W):
                high_w(n)
            act.wait_ge(w_lo_ready, N_W)
            high(q_hi, 0, q_done, q_hi_ready, 0)
            high(k_hi, 0, k_done, k_hi_ready, 0)
            high_v(0)
            with act.Fori(0, B - 1) as b:
                heads(b, True)
                high_o(b)
                act.wait_ge(o_lo_ready, b * HC + HC)
                high(x_hi, 0, x_turned, x_hi_ready, b + 1, V_W1)
                residual(b)
                high(q_hi, 0, q_done, q_hi_ready, b + 1)
                turned_rows(b)
                high(k_hi, 0, k_done, k_hi_ready, b + 1)
                route_odds(b)
                high_v(b + 1)
            heads(B - 1, False)
            high_o(B - 1)
            residual(B - 1)
            turned_rows(B - 1)
            route_odds(B - 1)

        @block.vector
        def _(dve):
            def mean(n, b):
                dve.wait_ge(sq_ready[n], b * TT + TT)
                dve.tensor_scalar(mean_sq[:, n, :], sq[:, n, :], 1.0 / H, RMS_EPS, ALU.mult,
                                  ALU.add).then_inc(mean_ready[n], 1)

            def low(dst, bank, hi, hi_ready, ready, b, gain=None):
                for c in range(HC):
                    dve.wait_ge(hi_ready, b * HC + c + 1)
                    if gain is None:
                        i = dve.tensor_tensor(dst[:, c, :], psum[bank + c][:, :], hi[:, c, :].bitcast(F32), ALU.subtract)
                    else:
                        i = dve.scalar_tensor_tensor(dst[:, c, :], psum[bank + c][:, :], vecs[:, gain, c:c + 1],
                                                     hi[:, c, :].bitcast(F32), ALU.mult, ALU.subtract)
                    i.then_inc(ready, 1)

            def low_wo(b):
                for k in range(HC):
                    dve.wait_ge(wo_hi_ready, b * HC + k + 1)
                    dve.tensor_tensor(wo_lo[:, k, :], wo[:, k, :], wo_hi[:, k, :].bitcast(F32),
                                      ALU.subtract).then_inc(wo_lo_ready, 1)

            def low_o(b):
                for c in range(HC):
                    dve.wait_ge(o_hi_ready, b * HC + c + 1)
                    dve.tensor_tensor(o_lo[:, c, :], o[:, c, :], o_hi[:, c, :].bitcast(F32),
                                      ALU.subtract).then_inc(o_lo_ready, 1)

            def low_v(b):
                for j in range(TT):
                    dve.wait_ge(v_hi_ready, b * 2 * TT + j * 2 + 2)
                    for place in range(2):
                        dve.tensor_tensor(value_columns(v_lo, V_LO_STEP, j, place), value_products(j, place),
                                          value_columns(v_hi, V_HI_STEP, j, place).bitcast(F32),
                                          ALU.subtract).then_inc(v_lo_ready, 1)

            def maxima(b, n, bank0):
                dve.wait_ge(scores_done, b * HEADS + n + 1)
                for j in range(TT):
                    bank, col = S_AT[j]
                    dve.tensor_reduce(row_max[:, j, n:n + 1], psum[bank0 + bank][:, col:col + (j + 1) * P],
                                      AX.X, ALU.max).then_inc(max_step, 1)

            def split_probs(b, i):
                if high_by_dve(i):
                    dve.wait_ge(exp_ready, (b * HEADS + i) * 3 + 3)
                    if i >= 2:
                        dve.wait_ge(heads_done, b * HEADS + i - 1)
                    dve.tensor_copy(p_hi[i % 2][:, :], p_full[i % 2][:, :]).then_inc(p_hi_by_dve, 1)
                    dve.wait_ge(p_hi_by_dve, b * BY_DVE + rounded(i, True))
                else:
                    dve.wait_ge(p_hi_by_act, b * (HEADS - BY_DVE) + rounded(i, False))
                dve.tensor_tensor(p_lo[i % 2][:, :], p_full[i % 2][:, :], p_hi[i % 2][:, :].bitcast(F32),
                                  ALU.subtract).then_inc(p_lo_ready, 1)

            def output(b, n):
                c, half, _, _ = stack(2 * n)
                own = slice(half * PAIR, (half + 1) * PAIR)
                dve.wait_ge(rec_ready, b * HEADS + 2 * n + 2)
                dve.tensor_tensor(o[own, c, :], psum[6 + n % 2][0:PAIR, :], sums_rec[0:PAIR, :],
                                  ALU.mult).then_inc(o_ready, 1)

            def heads(b, more):
                for s in range(HEADS + LAG + 3):
                    if s < HEADS:
                        maxima(b, s, 3 * (s % 2) if s < LAG else 0)
                    if s == LAG - 2 and more:
                        mean(0, b + 1)
                    if s >= LAG + 4 and (s - LAG) % 2 == 0:
                        output(b, (s - LAG - 4) // 2)
                    if LAG <= s < HEADS + LAG:
                        split_probs(b, s - LAG)
                    if s == WO_AT:
                        low_wo(b)

            def residual(b):
                dve.wait_ge(res_loaded, b * 48 + 48)
                for j in range(TT):
                    dve.wait_ge(proj_done, b * TT + j + 1)
                    dve.tensor_tensor(xp[:, j, :], psum[4 + j][:, :], xp[:, j, :], ALU.add).then_inc(xp_ready, 1)
                mean(1, b)

            def per_tile(x):
                return x.unsqueeze(2).to_broadcast([P, TT, E])

            def routing(b):
                steps = [0]

                def step(i):
                    i.then_inc(route, 1)
                    steps[0] += 1
                    dve.wait_ge(route, b * 15 + steps[0])

                def one_hot(dst, src, n):
                    step(dve.tensor_reduce(top[:, n, :], src[:, :, :], AX.X, ALU.max))
                    step(dve.tensor_tensor(hit[:, :, :], src[:, :, :], per_tile(top[:, n, :]), ALU.is_equal))
                    step(dve.tensor_tensor(hit[:, :, :], hit[:, :, :],
                                           prefer[:, :].unsqueeze(1).to_broadcast([P, TT, E]), ALU.mult))
                    step(dve.tensor_reduce(pick[:, :], hit[:, :, :], AX.X, ALU.max))
                    step(dve.tensor_tensor(dst, hit[:, :, :], per_tile(pick[:, :]), ALU.is_equal))

                dve.wait_ge(logits_done, b + 1)
                dve.wait_ge(route_out, b * 16 + 16)
                step(dve.tensor_copy(logits[:, :, :], psum[4][:, 0:TT * E].rearrange("p (j e) -> p j e", e=E)))
                one_hot(first, logits, 0)
                step(dve.scalar_tensor_tensor(left[:, :, :], first, NEG, logits[:, :, :], ALU.mult, ALU.add))
                one_hot(second, left, 1)
                step(dve.tensor_tensor(gap[:, :], top[:, 1, :], top[:, 0, :], ALU.subtract))
                assert steps[0] == 13
                dve.wait_ge(odds_ready, b + 1)
                step(dve.tensor_scalar(odds1[:, :], odds[:, :], 1.0, None, ALU.add))
                step(dve.reciprocal(p1, odds1[:, :]))
                assert steps[0] == 15
                dve.tensor_tensor(p2, odds[:, :], p1, ALU.mult).then_inc(routes_ready, 1)

            def low_w(n):
                dve.wait_ge(w_hi_ready, n + 1)
                dve.tensor_tensor(w_lo[:, n, :, :].rearrange("p k n -> p (k n)"), w_stage[:, n, :],
                                  w_hi[:, n, :, :].rearrange("p k n -> p (k n)").bitcast(F32),
                                  ALU.subtract).then_inc(w_lo_ready, 1)

            mean(0, 0)
            low_w(0)
            dve.wait_ge(const_in, 48)
            dve.wait_ge(x_turned, HC)
            low(x_lo, 0, x_hi, x_hi_ready, x_lo_ready, 0, V_W1)
            for n in range(1, N_W):
                low_w(n)
            dve.wait_ge(w_lo_ready, N_W)
            dve.wait_ge(consts_ready, 7)
            low(q_lo, 0, q_hi, q_hi_ready, q_lo_ready, 0)
            low(k_lo, 0, k_hi, k_hi_ready, k_lo_ready, 0)
            low_v(0)
            with dve.Fori(0, B - 1) as b:
                heads(b, True)
                low_o(b)
                dve.wait_ge(x_turned, b * HC + 2 * HC)
                low(x_lo, 0, x_hi, x_hi_ready, x_lo_ready, b + 1, V_W1)
                residual(b)
                low(q_lo, 0, q_hi, q_hi_ready, q_lo_ready, b + 1)
                low(k_lo, 0, k_hi, k_hi_ready, k_lo_ready, b + 1)
                routing(b)
                low_v(b + 1)
            heads(B - 1, False)
            low_o(B - 1)
            residual(B - 1)
            routing(B - 1)

        @block.tensor
        def _(pe):
            def turn(src, bank, done):
                for c in range(HC):
                    for j in range(TT):
                        i = pe.transpose(psum[bank + c][:, j * P:(j + 1) * P], src[:, j, c * P:(c + 1) * P], ident)
                    i.then_inc(done, 1)

            def by_feature(n, bank, done):
                for m in range(HC):
                    for k in range(HC):
                        cols = slice(m * P, (m + 1) * P)
                        last = mm3(pe, psum[bank + m][:, :], w_hi[:, n, k, cols], w_lo[:, n, k, cols],
                                   x_hi[:, k, :], x_lo[:, k, :], k == 0, k == HC - 1)
                    last.then_inc(done, 1)

            def by_token(hi, lo, wh, wl, bank, done):
                for j in range(TT):
                    for k in range(HC):
                        cols = slice(j * P, (j + 1) * P)
                        last = mm3(pe, psum[bank + j][:, :], hi[:, k, cols], lo[:, k, cols],
                                   wh[:, k, :], wl[:, k, :], k == 0, k == HC - 1)
                    last.then_inc(done, 1)

            def scores(n, bank0):
                i = stack(n)[3]
                for j in (3, 2, 0, 1):
                    bank, col = S_AT[j]
                    out = psum[bank0 + bank]
                    pe.matmul(out[:, col:col + (j + 1) * P], lhsT=q2[0:STACK, i, j * P:(j + 1) * P],
                              rhs=k2[0:STACK, i, 0:(j + 1) * P], start=True, stop=False)
                    last = pe.matmul(out[:, col + j * P:col + (j + 1) * P], lhsT=ident_bf, rhs=causal,
                                     start=False, stop=True)
                last.then_inc(scores_done, 1)

            def turned_scores(n):
                i = stack(n)[3]
                for kt in range(TT):
                    bank, col = PT_AT[kt]
                    out = psum[3 + bank]
                    pe.matmul(out[:, col:col + (TT - kt) * P], lhsT=k2[0:STACK + 1, i, kt * P:(kt + 1) * P],
                              rhs=q2[0:STACK + 1, i, kt * P:S], start=True, stop=False)
                    last = pe.matmul(out[:, col:col + P], lhsT=ident_bf, rhs=causal_t, start=False, stop=True)
                last.then_inc(turned_scores_done, 1)

            def turn_maxima(start, stop, bank):
                for j in range(TT):
                    i = pe.transpose(psum[bank][0:stop - start, j * P:(j + 1) * P], row_max[:, j, start:stop], ident)
                i.then_inc(max_turned, 1)

            def head_output(b, n):
                c, half, place, _ = stack(n)
                pe.wait_ge(p_lo_ready, b * HEADS + n + 1)
                if n >= 4 and place == 0:
                    pe.wait_ge(o_ready, b * HEADS // 2 + n // 2 - 1)
                out = psum[6 + n // 2 % 2]
                for kt in range(TT):
                    bank, col = PT_AT[kt]
                    at = slice(bank * S + col, bank * S + col + (TT - kt) * P)
                    queries = slice(kt * P, S)
                    pair = kt * PAIRS + c * 2 + half
                    high = v_hi[:, pair, place * V_HI_TILE:place * V_HI_TILE + 2 * PAIR]
                    low = v_lo[:, pair, place * V_LO_TILE:place * V_LO_TILE + PAIR]
                    pe.matmul(out[:, queries], lhsT=high, rhs=p_hi[n % 2][:, at], start=(place == 0 and kt == 0), stop=False)
                    pe.matmul(out[0:PAIR, queries], lhsT=low, rhs=p_hi[n % 2][:, at], start=False, stop=False)
                    last = pe.matmul(out[:, queries], lhsT=high, rhs=p_lo[n % 2][:, at], start=False,
                                     stop=(place == 1 and kt == TT - 1))
                last.then_inc(heads_done, 1)

            def heads(b, more):
                pe.wait_ge(v_lo_ready, b * 2 * TT + 2 * TT)
                pe.wait_ge(q2_in, (b + 1) * 16 * 12)
                pe.wait_ge(k2_in, (b + 1) * 16 * 13)
                for s in range(HEADS + LAG + 2):
                    if s < HEADS:
                        before = s - 2 if s <= LAG else s - 1
                        if before >= 0:
                            pe.wait_ge(max_step, (b * HEADS + before + 1) * TT)
                        scores(s, 3 * (s % 2) if s < LAG else 0)
                    for start, stop, bank in SETS:
                        if s == stop:
                            pe.wait_ge(max_step, (b * HEADS + stop) * TT)
                            turn_maxima(start, stop, bank)
                    i = s - LAG
                    if 0 <= i < HEADS:
                        for n, (start, _, _) in enumerate(SETS):
                            if i == start:
                                pe.wait_ge(max_in, (b * MAX_DMAS[-1] + MAX_DMAS[n]) * 16)
                        if i == 0:
                            pe.wait_ge(max_step, (b * HEADS + LAG) * TT)
                        else:
                            pe.wait_ge(exp_ready, (b * HEADS + i) * 3)
                        turned_scores(i)
                    if i >= 2:
                        head_output(b, i - 2)
                if more:
                    pe.wait_ge(exp_ready, (b * HEADS + HEADS) * 3)
                    prepare(b + 1)

            def prepare(b):
                pe.wait_ge(norm_ready[0], b * TT + TT)
                turn(xn, 0, x_turned)

            def q(b):
                pe.wait_ge(x_lo_ready, b * HC + HC)
                by_feature(0, 0, q_done)

            def k(b):
                pe.wait_ge(q_lo_ready, b * HC + HC)
                by_feature(1, 0, k_done)

            def v(b):
                pe.wait_ge(k_lo_ready, b * HC + HC)
                by_token(x_hi, x_lo, w_hi[:, 2, :, :], w_lo[:, 2, :, :], 0, v_done)

            def project(b):
                pe.wait_ge(wo_lo_ready, b * HC + HC)
                pe.wait_ge(o_lo_ready, b * HC + HC)
                by_token(o_hi, o_lo, wo_hi, wo_lo, 4, proj_done)

            def turn_rows(b):
                pe.wait_ge(norm_ready[1], b * TT + TT)
                turn(rows, 4, rows_turned)

            def experts_logits(b, more):
                pe.wait_ge(xT_ready, b * HC + HC)
                for j in range(TT):
                    if j == TT - 1 and more:
                        pe.wait_ge(k_lo_ready, b * HC + 2 * HC)
                        pe.wait_ge(pre_out, b * 16 + 16)
                        pe.wait_ge(rows_sent, b * 16 + 16)
                    for c in range(HC):
                        i = pe.matmul(psum[4][:, j * E:(j + 1) * E], lhsT=xT[:, c, j * P:(j + 1) * P],
                                      rhs=wr[:, c, :], start=(c == 0), stop=(c == HC - 1))
                i.then_inc(logits_done, 1)

            prepare(0)
            pe.wait_ge(const_in, 48)
            pe.wait_ge(w_lo_ready, 1)
            q(0)
            pe.wait_ge(w_lo_ready, N_W)
            k(0)
            v(0)
            with pe.Fori(0, B - 1) as b:
                heads(b, True)
                project(b)
                q(b + 1)
                turn_rows(b)
                k(b + 1)
                experts_logits(b, True)
                v(b + 1)
            heads(B - 1, False)
            project(B - 1)
            turn_rows(B - 1)
            experts_logits(B - 1, False)


def constants(nc, ident, ident_bf, causal, causal_t, d):
    with ExitStack() as ctx:
        filled = ctx.enter_context(nc.semaphore("c_filled"))
        block = ctx.enter_context(nc.Block())

        @block.gpsimd
        def _(pool):
            pool.memset(ident[:, :], 0.0).then_inc(filled, 1)
            pool.memset(ident_bf[:, :], 0.0).then_inc(filled, 1)
            pool.memset(causal[:, :], 0.0).then_inc(filled, 1)
            pool.memset(causal_t[:, :], 0.0).then_inc(filled, 1)
            pool.wait_ge(filled, 4)
            for m in (ident, ident_bf):
                pool.affine_select(out=m[:, :], in_=m[:, :], compare_op=ALU.not_equal, fill=1.0, base=0,
                                   pattern=[[-1, P]], channel_multiplier=1).then_inc(filled, 1)
            pool.affine_select(out=causal[:, :], in_=causal[:, :], compare_op=ALU.is_ge, fill=NEG, base=0,
                               pattern=[[-1, P]], channel_multiplier=1).then_inc(filled, 1)
            pool.affine_select(out=causal_t[:, :], in_=causal_t[:, :], compare_op=ALU.is_ge, fill=NEG, base=0,
                               pattern=[[1, P]], channel_multiplier=-1).then_inc(filled, 1)
            pool.wait_ge(filled, 8)


def build(nc, d):
    for name, shape in (("xn", [B, S, H]), ("x2", [B, S, H]), ("rc", [B, S, H]), ("pre", [B, S, H]),
                        ("rows_in", [B, S, H]), ("route", [B, P, ROUTE]),
                        ("xc_hi", [B, P, HC, S]), ("xc_lo", [B, P, HC, S]),
                        ("tiles_in", [TILES * TILE, H]), ("tiles_out", [TILES * TILE, H])):
        d[name] = nc.dram_tensor("scratch_" + name, shape, F32, kind="Internal").ap()
    with ExitStack() as ctx:
        psum = [ctx.enter_context(nc.psum_tensor(f"bank{n}", [P, 512], F32)) for n in range(8)]
        ident = ctx.enter_context(nc.sbuf_tensor("ident", [P, P], F32))
        ident_bf = ctx.enter_context(nc.sbuf_tensor("ident_bf", [P, P], BF16))
        causal = ctx.enter_context(nc.sbuf_tensor("causal", [P, P], BF16))
        causal_t = ctx.enter_context(nc.sbuf_tensor("causal_t", [P, P], BF16))
        routing = (ctx.enter_context(nc.sbuf_tensor("slots", [P, 2, B, TT], mybir.dt.int32)),
                   ctx.enter_context(nc.sbuf_tensor("experts", [P, TILES], mybir.dt.int32)),
                   ctx.enter_context(nc.sbuf_tensor("weights", [P, 2, B, TT], F32)))
        constants(nc, ident, ident_bf, causal, causal_t, d)
        time_mix_phase(nc, psum, ident[:, :], d)
        attention_phase(nc, psum, ident[:, :], ident_bf[:, :], causal[:, :], causal_t[:, :], d)
        acc = ctx.enter_context(nc.sbuf_tensor("acc", [P, T_ALL, H], F32))
        with ExitStack() as shared:
            stage = shared.enter_context(nc.sbuf_tensor("cm_stage", [P, 2, (HC + 2 * CK) * CH], F32))
        first_tile = (ctx.enter_context(nc.sbuf_tensor("first_x", [P, TP, H], F32)),
                      ctx.enter_context(nc.sbuf_tensor("first_w", [P, 2 * HC * CH + CK * H], F32)),
                      ctx.enter_context(nc.sbuf_tensor("moe_gain", [P, 8, HC], F32)))
        channel_mix_phase(nc, psum, d, routing, acc, stage, first_tile)
        experts_phase(nc, psum, ident[:, :], routing, first_tile, d)
        combine_phase(nc, routing, acc, d)


def kernel(**inputs):
    import numpy as np
    import concourse.bacc as bacc
    from concourse.bass_utils import run_bass_kernel_spmd

    g = {n.replace("L0_", ""): np.asarray(a) for n, a in inputs.items()}

    def in_tiles(w):
        k = w.shape[0] // P
        return w.reshape(k, P, -1).transpose(1, 0, 2).reshape(P, -1)

    def up_chunks(w):
        return w.reshape(HC, P, -1, CH).transpose(2, 1, 0, 3).reshape(-1, P, HC * CH)

    def down_chunks(w):
        return w.reshape(-1, CK, P, H).transpose(0, 2, 1, 3).reshape(-1, P, CK * H)

    def per_feature(v):
        return v.reshape(HC, P).T

    def experts_up(w):
        return np.concatenate([up_chunks(w[e].T) for e in range(E)])

    arrays = {
        "x": g["attn_x"],
        "w_tm": np.stack([in_tiles(g["attn_" + n]) for n in ("Wv", "Wr", "Wcr", "Wo")]),
        "w_at": np.stack([in_tiles(g["ffn_" + n].T) for n in ("Wq", "Wk", "Wv", "Wo")]),
        "w_r": g["ffn_Wr"].T.reshape(HC, P, E).transpose(1, 0, 2),
        "w_cm": np.concatenate([up_chunks(g["attn_Wck"]), down_chunks(g["attn_Wcv"])], axis=2),
        "w_moe": np.concatenate([experts_up(g["ffn_Wg"]), experts_up(g["ffn_Wu"]),
                                 np.concatenate([down_chunks(g["ffn_Wd"][e].T) for e in range(E)])], axis=2),
        "vecs": np.stack([per_feature(g[n]) for n in (
            "attn_tm_g", "attn_tm_b", "attn_time_first", "attn_time_decay", "attn_cm_g", "attn_cm_b",
            "ffn_w_ln1", "ffn_w_ln2")], axis=1),
        "rows": np.stack([g["attn_" + n] for n in ("ln1_g", "ln1_b", "ln2_g", "ln2_b", "bo")]),
    }
    arrays = {"in_" + n: np.ascontiguousarray(a) for n, a in arrays.items()}
    nc = bacc.Bacc("TRN2", target_bir_lowering=False, num_devices=1)
    d = {n[3:]: nc.dram_tensor(n, a.shape, F32, kind="ExternalInput").ap() for n, a in arrays.items()}
    d["out"] = nc.dram_tensor("out", [B, S, H], F32, kind="ExternalOutput").ap()
    build(nc, d)
    r = run_bass_kernel_spmd(nc, [arrays], core_ids=[0])
    return r.results[0]["out"]
```
